# Optimizing a Trainium2 kernel written in Bass

```python
import numpy as np
import jax
import jax.numpy as jnp

def _softmax(x, axis=-1):
    return jax.nn.softmax(x, axis=axis)

def _gelu(x):
    return jax.nn.gelu(x, approximate=True)

def _silu(x):
    return jax.nn.silu(x)

def _sigmoid(x):
    return jax.nn.sigmoid(x)

def _layernorm(x, axis=-1, eps=1e-05):
    m = jnp.mean(x, axis=axis, keepdims=True)
    v = jnp.var(x, axis=axis, keepdims=True)
    return (x - m) / jnp.sqrt(v + eps)

def _scatter_add(tgt, idx, src, axis=0):
    return tgt.at[idx].add(src)

def _segment_sum(src, seg, n):
    return jax.ops.segment_sum(src, seg, n)
kernel_name = 'mk_hybrid_d1_jaxref_r8_d1f7bb'

def setup_inputs(seed: int=0):
    np.random.seed(seed)
    _w = jnp.asarray

    def _L0_attn_a_setup():
        import jax, jax.numpy as jnp
        import numpy as np
        DIM = 128
        H = 16
        HD = DIM // H
        R = 8
        QK = 32
        B = 4
        S = 128
        EPS = 1e-05

        def _lin(x, W, b):
            return x @ W.T + b

        def _ln(x, g, b):
            m = x.mean(-1, keepdims=True)
            v = ((x - m) ** 2).mean(-1, keepdims=True)
            return (x - m) / jnp.sqrt(v + EPS) * g + b
        key = jax.random.key(seed)
        ks = iter(jax.random.split(key, 32))

        def w(shape, fan):
            s = 1.0 / np.sqrt(fan)
            return jax.random.uniform(next(ks), shape, jnp.float32, -s, s)
        d = {}
        d['x'] = jax.random.normal(next(ks), (B, S, DIM), jnp.float32)
        d['Wq'] = w((DIM, DIM), DIM)
        d['bq'] = w((DIM,), DIM)
        d['Wk'] = w((DIM, DIM), DIM)
        d['bk'] = w((DIM,), DIM)
        d['Wv'] = w((HD * R, DIM), DIM)
        d['bv'] = w((HD * R,), DIM)
        d['Wqv'] = w((QK * H, DIM), DIM)
        d['bqv'] = w((QK * H,), DIM)
        d['Ws'] = w((1, HD + QK), HD + QK)
        d['bs'] = w((1,), HD + QK)
        d['Wf'] = w((DIM, DIM), DIM)
        d['bf'] = w((DIM,), DIM)
        d['Wr1'] = w((2 * DIM, DIM), DIM)
        d['br1'] = w((2 * DIM,), DIM)
        d['Wr2'] = w((DIM, 2 * DIM), 2 * DIM)
        d['br2'] = w((DIM,), 2 * DIM)
        d['g1'] = jnp.ones((DIM,), jnp.float32)
        d['b1'] = jnp.zeros((DIM,), jnp.float32)
        d['g2'] = jnp.ones((DIM,), jnp.float32)
        d['b2'] = jnp.zeros((DIM,), jnp.float32)
        return d
    _L0_attn_a_in = _L0_attn_a_setup()

    def _L0_attn_b_setup():
        import jax, jax.numpy as jnp
        import numpy as np
        N_HEADS = 16
        SEG = 64
        EPS = 1e-06

        def _sigma(x):
            return jax.nn.elu(x) + 1.0

        def _infini_attention(x, W_q, W_k, W_v, W_o, beta_param):
            B, T, D = x.shape
            H = N_HEADS
            dk = D // H
            assert T % SEG == 0
            S = T // SEG

            def proj(W):
                y = (x @ W.T).reshape(B, T, H, dk).transpose(0, 2, 1, 3)
                return y.reshape(B, H, S, SEG, dk).transpose(2, 0, 1, 3, 4)
            Qs, Ks, Vs = (proj(W_q), proj(W_k), proj(W_v))
            beta = jax.nn.sigmoid(beta_param).reshape(1, H, 1, 1)
            causal = jnp.triu(jnp.ones((SEG, SEG), dtype=bool), k=1)
            inv_sqrt_dk = 1.0 / jnp.sqrt(jnp.asarray(dk, x.dtype))
            M0 = jnp.zeros((B, H, dk, dk), dtype=x.dtype)
            z0 = jnp.zeros((B, H, dk), dtype=x.dtype)

            def step(carry, qkv):
                M, z = carry
                q, k, v = qkv
                sq = _sigma(q)
                denom_q = jnp.sum(sq * z[:, :, None, :], axis=-1, keepdims=True) + EPS
                A_mem = jnp.matmul(sq, M) / denom_q
                scores = jnp.matmul(q, jnp.swapaxes(k, -2, -1)) * inv_sqrt_dk
                scores = jnp.where(causal, -jnp.inf, scores)
                A_dot = jnp.matmul(jax.nn.softmax(scores, axis=-1), v)
                A_s = beta * A_mem + (1.0 - beta) * A_dot
                sk = _sigma(k)
                denom_k = jnp.sum(sk * z[:, :, None, :], axis=-1, keepdims=True) + EPS
                V_prev = jnp.matmul(sk, M) / denom_k
                M_new = M + jnp.einsum('bhtk,bhtv->bhkv', sk, v - V_prev)
                z_new = z + jnp.sum(sk, axis=-2)
                return ((M_new, z_new), A_s)
            (M, z), outs = jax.lax.scan(step, (M0, z0), (Qs, Ks, Vs))
            out = outs.transpose(1, 3, 0, 2, 4).reshape(B, S * SEG, H, dk)
            out = outs.transpose(1, 2, 0, 3, 4).reshape(B, H, T, dk)
            out = out.transpose(0, 2, 1, 3).reshape(B, T, D)
            out = out @ W_o.T
            return (out, M.mean(0), z.mean(0))

        def _reference_tuple_inner(x, W_q, W_k, W_v, W_o, beta_param):
            return _infini_attention(x, W_q, W_k, W_v, W_o, beta_param)
        key = jax.random.key(seed)
        kx, kq, kk, kv, ko = jax.random.split(key, 5)
        B, T, D = (4, 512, 128)
        scale = D ** (-0.5)
        return {'x': jax.random.normal(kx, (B, T, D), dtype=jnp.float32), 'W_q': jax.random.normal(kq, (D, D), dtype=jnp.float32) * scale, 'W_k': jax.random.normal(kk, (D, D), dtype=jnp.float32) * scale, 'W_v': jax.random.normal(kv, (D, D), dtype=jnp.float32) * scale, 'W_o': jax.random.normal(ko, (D, D), dtype=jnp.float32) * scale, 'beta_param': jnp.zeros((N_HEADS,), dtype=jnp.float32)}
    _L0_attn_b_in = _L0_attn_b_setup()

    def _L0_ffn_setup():
        import jax, jax.numpy as jnp
        import numpy as np
        NUM_GEMMS = 8
        HIDDEN = 128
        INTER = 512
        key = jax.random.key(seed)
        k_x, k_w1, k_b1, k_w2, k_b2 = jax.random.split(key, 5)
        x = jax.random.normal(k_x, (8, 256, HIDDEN), dtype=jnp.float32)
        s1 = 1.0 / np.sqrt(HIDDEN)
        s2 = 1.0 / np.sqrt(INTER)
        W1 = jax.random.uniform(k_w1, (NUM_GEMMS, INTER, HIDDEN), jnp.float32, -s1, s1)
        b1 = jax.random.uniform(k_b1, (NUM_GEMMS, INTER), jnp.float32, -s1, s1)
        W2 = jax.random.uniform(k_w2, (NUM_GEMMS, HIDDEN, INTER), jnp.float32, -s2, s2)
        b2 = jax.random.uniform(k_b2, (NUM_GEMMS, HIDDEN), jnp.float32, -s2, s2)
        return {'x': x, 'W1': W1, 'b1': b1, 'W2': W2, 'b2': b2}
    _L0_ffn_in = _L0_ffn_setup()
    _d = {'L0_attn_a_x': _L0_attn_a_in['x'], 'L0_attn_a_Wq': _L0_attn_a_in['Wq'], 'L0_attn_a_bq': _L0_attn_a_in['bq'], 'L0_attn_a_Wk': _L0_attn_a_in['Wk'], 'L0_attn_a_bk': _L0_attn_a_in['bk'], 'L0_attn_a_Wv': _L0_attn_a_in['Wv'], 'L0_attn_a_bv': _L0_attn_a_in['bv'], 'L0_attn_a_Wqv': _L0_attn_a_in['Wqv'], 'L0_attn_a_bqv': _L0_attn_a_in['bqv'], 'L0_attn_a_Ws': _L0_attn_a_in['Ws'], 'L0_attn_a_bs': _L0_attn_a_in['bs'], 'L0_attn_a_Wf': _L0_attn_a_in['Wf'], 'L0_attn_a_bf': _L0_attn_a_in['bf'], 'L0_attn_a_Wr1': _L0_attn_a_in['Wr1'], 'L0_attn_a_br1': _L0_attn_a_in['br1'], 'L0_attn_a_Wr2': _L0_attn_a_in['Wr2'], 'L0_attn_a_br2': _L0_attn_a_in['br2'], 'L0_attn_a_g1': _L0_attn_a_in['g1'], 'L0_attn_a_b1': _L0_attn_a_in['b1'], 'L0_attn_a_g2': _L0_attn_a_in['g2'], 'L0_attn_a_b2': _L0_attn_a_in['b2'], 'L0_attn_b_W_q': _L0_attn_b_in['W_q'], 'L0_attn_b_W_k': _L0_attn_b_in['W_k'], 'L0_attn_b_W_v': _L0_attn_b_in['W_v'], 'L0_attn_b_W_o': _L0_attn_b_in['W_o'], 'L0_attn_b_beta_param': _L0_attn_b_in['beta_param'], 'L0_ffn_W1': _L0_ffn_in['W1'], 'L0_ffn_b1': _L0_ffn_in['b1'], 'L0_ffn_W2': _L0_ffn_in['W2'], 'L0_ffn_b2': _L0_ffn_in['b2']}
    _x0 = _d['L0_attn_a_x']
    _d['L0_attn_a_x'] = jax.random.normal(jax.random.fold_in(jax.random.key(seed), 1), (32, 256, 128), dtype=_x0.dtype)
    del _x0
    return _d

def reference(L0_attn_a_x, L0_attn_a_Wq, L0_attn_a_bq, L0_attn_a_Wk, L0_attn_a_bk, L0_attn_a_Wv, L0_attn_a_bv, L0_attn_a_Wqv, L0_attn_a_bqv, L0_attn_a_Ws, L0_attn_a_bs, L0_attn_a_Wf, L0_attn_a_bf, L0_attn_a_Wr1, L0_attn_a_br1, L0_attn_a_Wr2, L0_attn_a_br2, L0_attn_a_g1, L0_attn_a_b1, L0_attn_a_g2, L0_attn_a_b2, L0_attn_b_W_q, L0_attn_b_W_k, L0_attn_b_W_v, L0_attn_b_W_o, L0_attn_b_beta_param, L0_ffn_W1, L0_ffn_b1, L0_ffn_W2, L0_ffn_b2):

    def _L0_attn_a_ref(x, Wq, bq, Wk, bk, Wv, bv, Wqv, bqv, Ws, bs, Wf, bf, Wr1, br1, Wr2, br2, g1, b1, g2, b2):
        import jax, jax.numpy as jnp
        import numpy as np
        DIM = 128
        H = 16
        HD = DIM // H
        R = 8
        QK = 32
        B = 4
        S = 128
        EPS = 1e-05

        def _lin(x, W, b):
            return x @ W.T + b

        def _ln(x, g, b):
            m = x.mean(-1, keepdims=True)
            v = ((x - m) ** 2).mean(-1, keepdims=True)
            return (x - m) / jnp.sqrt(v + EPS) * g + b
        b, n, _ = x.shape
        res = x
        xn = _ln(x, g1, b1)
        q = _lin(xn, Wq, bq).reshape(b, n, H, HD) / np.sqrt(HD).astype(np.float32)
        k = _lin(xn, Wk, bk).reshape(b, n, H, HD)
        score = jax.nn.softmax(jnp.einsum('bihd,bjhd->bhij', q, k), axis=-1)
        v = _lin(xn, Wv, bv).reshape(b, n, R, HD)
        out = jnp.einsum('bhij,bjrd->bihrd', score, v)
        qv = _lin(xn, Wqv, bqv).reshape(b, n, H, 1, QK) / np.sqrt(QK).astype(np.float32)
        qv = jnp.broadcast_to(qv, (b, n, H, R, QK))
        comp = jnp.concatenate([qv, out], axis=-1) @ Ws.T + bs
        comp = jax.nn.softmax(comp, axis=3)
        out = (comp * out).sum(axis=3).reshape(b, n, DIM)
        out = res + _lin(out, Wf, bf)
        res2 = out
        on = _ln(out, g2, b2)
        ffn = _lin(jax.nn.relu(_lin(on, Wr1, br1)), Wr2, br2)
        return res2 + ffn

    def _L0_attn_b_ref(x, W_q, W_k, W_v, W_o, beta_param):
        import jax, jax.numpy as jnp
        import numpy as np
        N_HEADS = 16
        SEG = 64
        EPS = 1e-06

        def _sigma(x):
            return jax.nn.elu(x) + 1.0

        def _infini_attention(x, W_q, W_k, W_v, W_o, beta_param):
            B, T, D = x.shape
            H = N_HEADS
            dk = D // H
            assert T % SEG == 0
            S = T // SEG

            def proj(W):
                y = (x @ W.T).reshape(B, T, H, dk).transpose(0, 2, 1, 3)
                return y.reshape(B, H, S, SEG, dk).transpose(2, 0, 1, 3, 4)
            Qs, Ks, Vs = (proj(W_q), proj(W_k), proj(W_v))
            beta = jax.nn.sigmoid(beta_param).reshape(1, H, 1, 1)
            causal = jnp.triu(jnp.ones((SEG, SEG), dtype=bool), k=1)
            inv_sqrt_dk = 1.0 / jnp.sqrt(jnp.asarray(dk, x.dtype))
            M0 = jnp.zeros((B, H, dk, dk), dtype=x.dtype)
            z0 = jnp.zeros((B, H, dk), dtype=x.dtype)

            def step(carry, qkv):
                M, z = carry
                q, k, v = qkv
                sq = _sigma(q)
                denom_q = jnp.sum(sq * z[:, :, None, :], axis=-1, keepdims=True) + EPS
                A_mem = jnp.matmul(sq, M) / denom_q
                scores = jnp.matmul(q, jnp.swapaxes(k, -2, -1)) * inv_sqrt_dk
                scores = jnp.where(causal, -jnp.inf, scores)
                A_dot = jnp.matmul(jax.nn.softmax(scores, axis=-1), v)
                A_s = beta * A_mem + (1.0 - beta) * A_dot
                sk = _sigma(k)
                denom_k = jnp.sum(sk * z[:, :, None, :], axis=-1, keepdims=True) + EPS
                V_prev = jnp.matmul(sk, M) / denom_k
                M_new = M + jnp.einsum('bhtk,bhtv->bhkv', sk, v - V_prev)
                z_new = z + jnp.sum(sk, axis=-2)
                return ((M_new, z_new), A_s)
            (M, z), outs = jax.lax.scan(step, (M0, z0), (Qs, Ks, Vs))
            out = outs.transpose(1, 3, 0, 2, 4).reshape(B, S * SEG, H, dk)
            out = outs.transpose(1, 2, 0, 3, 4).reshape(B, H, T, dk)
            out = out.transpose(0, 2, 1, 3).reshape(B, T, D)
            out = out @ W_o.T
            return (out, M.mean(0), z.mean(0))

        def _reference_tuple_inner(x, W_q, W_k, W_v, W_o, beta_param):
            return _infini_attention(x, W_q, W_k, W_v, W_o, beta_param)
        return _reference_tuple_inner(x, W_q, W_k, W_v, W_o, beta_param)[0]

    def _L0_ffn_ref(x, W1, b1, W2, b2):
        import jax, jax.numpy as jnp
        import numpy as np
        NUM_GEMMS = 8
        HIDDEN = 128
        INTER = 512
        orig_shape = x.shape
        token_num = int(np.prod(orig_shape[:-1]))
        m = token_num // NUM_GEMMS
        xg = x.reshape(NUM_GEMMS, m, HIDDEN)
        h1 = jnp.einsum('gmh,goh->gmo', xg, W1) + b1[:, None, :]
        h2 = jnp.einsum('gmo,gho->gmh', h1, W2) + b2[:, None, :]
        return h2.reshape(orig_shape)
    x = L0_attn_a_x
    x = x + _L0_attn_a_ref(_layernorm(x, axis=-1), L0_attn_a_Wq, L0_attn_a_bq, L0_attn_a_Wk, L0_attn_a_bk, L0_attn_a_Wv, L0_attn_a_bv, L0_attn_a_Wqv, L0_attn_a_bqv, L0_attn_a_Ws, L0_attn_a_bs, L0_attn_a_Wf, L0_attn_a_bf, L0_attn_a_Wr1, L0_attn_a_br1, L0_attn_a_Wr2, L0_attn_a_br2, L0_attn_a_g1, L0_attn_a_b1, L0_attn_a_g2, L0_attn_a_b2)
    x = x + _L0_ffn_ref(_layernorm(x, axis=-1), L0_ffn_W1, L0_ffn_b1, L0_ffn_W2, L0_ffn_b2)
    x = x + _L0_attn_b_ref(_layernorm(x, axis=-1), L0_attn_b_W_q, L0_attn_b_W_k, L0_attn_b_W_v, L0_attn_b_W_o, L0_attn_b_beta_param)
    x = x + _L0_ffn_ref(_layernorm(x, axis=-1), L0_ffn_W1, L0_ffn_b1, L0_ffn_W2, L0_ffn_b2)
    return x

_drawn_inputs = setup_inputs


def setup_inputs(seed=0):
    import zlib

    import numpy as np

    out = dict(_drawn_inputs(seed))
    spreads = {'L0_attn_a_g1': (1.0, 0.6),
     'L0_attn_a_b1': (0.0, 0.8),
     'L0_attn_a_g2': (1.0, 0.6),
     'L0_attn_a_b2': (0.0, 2.0),
     'L0_attn_b_beta_param': (0.0, 2.0)}
    factors = {'L0_attn_a_Wq': 8.0,
     'L0_attn_a_bq': 8.0,
     'L0_attn_a_Wk': 8.0,
     'L0_attn_a_bk': 200.0,
     'L0_attn_a_Wv': 7.537,
     'L0_attn_a_bv': 8.0,
     'L0_attn_a_Wqv': 200.0,
     'L0_attn_a_bqv': 200.0,
     'L0_attn_a_Ws': 8.0,
     'L0_attn_a_Wf': 8.0,
     'L0_attn_a_br1': 43.752,
     'L0_attn_a_br2': 23.48,
     'L0_attn_a_bf': 22.709,
     'L0_attn_a_Wr1': 4.844,
     'L0_attn_a_Wr2': 3.938,
     'L0_attn_b_W_q': 8.0,
     'L0_attn_b_W_k': 8.0,
     'L0_attn_b_W_v': 3.774,
     'L0_attn_b_W_o': 3.749,
     'L0_ffn_b1': 27.296,
     'L0_ffn_b2': 31.334}
    for name, (base, spread) in spreads.items():
        noise = np.random.default_rng([zlib.crc32(name.encode()), seed]).standard_normal(out[name].shape)
        drawn = base * np.exp(spread * noise) if base else spread * noise
        out[name] = jnp.asarray(drawn.astype(out[name].dtype))
    for name, factor in factors.items():
        out[name] = (out[name] * factor).astype(out[name].dtype)
    return out
```

```python
import concourse.bass as bass
import concourse.mybir as mybir
from contextlib import ExitStack

F32 = mybir.dt.float32
BF16 = mybir.dt.bfloat16
ALU = mybir.AluOpType
ACT = mybir.ActivationFunctionType
AX = mybir.AxisListType

P = 128
NB, T = 32, 256
NT = T // P
H, HD, R, QK = 16, 8, 8, 32
RD = R * HD
NPART = 3
SROWS = NPART * NPART * HD
MROW = 96
KROWS = MROW + NPART
VC = 96
CV, CC, CS, CQ = 0, RD, RD + R, RD + R + 1
EPS = 1e-5
NG, NI = 8, 4
LAGS = 4
PEELED = 6


def active(j, u, lag, total=NB):
    return not isinstance(j, int) or 0 <= 2 * j + u - lag < total


def pair(j, u, lag):
    return j + (u - lag) // 2, (u - lag) % 2


def pipeline(eng, body, total=NB, stages=LAGS):
    for n in range(PEELED):
        body(n // 2, n % 2)
    with eng.Fori(PEELED // 2, total // 2) as j:
        body(j, 0)
        body(j, 1)
    for n in range(total, total + stages - 1):
        body(n // 2, n % 2)


def apart(eng, spare):
    eng.sem_inc(spare, 1)


def memory(nc, ctx, prefix):
    def sb(name, shape, dt=F32):
        return ctx.enter_context(nc.sbuf_tensor(f"{prefix}_{name}", shape, dt))

    def sem(name):
        return ctx.enter_context(nc.semaphore(f"{prefix}_{name}"))

    return sb, sem


def attention_a(nc, d):
    ctx = ExitStack()
    with ctx:
        def sb(name, shape, dt=F32):
            return ctx.enter_context(nc.sbuf_tensor(name, shape, dt))

        def sem(name):
            return ctx.enter_context(nc.semaphore(name))

        w_q = sb("a_w_q", [P, P])
        w_k = sb("a_w_k", [P, P])
        w_v = sb("a_w_v", [P, VC])
        b_v = sb("a_b_v", [P, VC])
        w_qv = sb("a_w_qv", [P, 4, P])
        w_vn = sb("a_w_vn", [RD, P])
        s_qv = sb("a_s_qv", [P, 4, H])
        s_v = sb("a_s_v", [RD, R])
        b_qv = sb("a_b_qv", [P, 4, P])
        b_vr = sb("a_b_vr", [RD, P])
        cols = sb("a_cols", [P, 5])
        b_qs = sb("a_b_qs", [P, 1])
        ident = sb("a_ident", [P, P])
        ident16 = sb("a_ident16", [P, P], BF16)
        half = sb("a_half", [P, NT])
        x = [sb(f"a_x{i}", [P, NT, P]) for i in range(2)]
        y = [sb(f"a_y{i}", [P, NT, P]) for i in range(2)]
        z = [sb(f"a_z{i}", [P, NT, P]) for i in range(2)]
        stats = sb("a_stats", [P, NT, 6])
        mv = sb("a_mv", [P, NT, 2])
        r1 = sb("a_r1", [P, NT])
        r2 = sb("a_r2", [P, NT])
        rt = sb("a_rt", [P, 4, NT])
        xn = [sb(f"a_xn{i}", [P, T]) for i in range(2)]
        qk = [sb(f"a_qk{i}", [P, 2, T]) for i in range(2)]
        rest = sb("a_rest", [P, 2, T])
        parts = [sb(f"a_parts{i}", [P, 2, NPART, T], BF16) for i in range(2)]
        q_st = [sb(f"a_q_st{i}", [P, H, T], BF16) for i in range(2)]
        k_st = [sb(f"a_k_st{i}", [P, H, T], BF16) for i in range(2)]
        vp = [sb(f"a_vp{i}", [P, NT, VC]) for i in range(2)]
        nmax = sb("a_nmax", [P, NT, H])
        nrest = sb("a_nrest", [P, NT, H])
        mpart = sb("a_mpart", [P, NT, 2, NPART, H // 2], BF16)
        mt = [sb(f"a_mt{i}", [NPART * H // 2, T], BF16) for i in range(2)]
        prob = [sb(f"a_prob{i}", [P, NT, T]) for i in range(4)]
        ov = [sb(f"a_ov{i}", [P, H * NT, RD + R + 1]) for i in range(2)]
        inv = sb("a_inv", [P, H * NT])
        comp = sb("a_comp", [P, H * NT, R])
        comp2 = sb("a_comp2", [P, H * NT, R])
        cmax = sb("a_cmax", [P, H * NT])
        comp3 = sb("a_comp3", [P, H * NT, R])
        cexp = sb("a_cexp", [P, H * NT, R])
        csum = sb("a_csum", [P, H * NT])
        cinv = sb("a_cinv", [P, H * NT])
        cw = sb("a_cw", [P, H * NT])
        wgt = sb("a_wgt", [P, H * NT, R])
        prod = sb("a_prod", [P, H * NT, RD])
        ao = [sb(f"a_ao{i}", [P, NT, P]) for i in range(2)]
        bank = [ctx.enter_context(nc.psum_tensor(f"a_bank{i}", [P, 512], F32)) for i in range(8)]
        zv_ps, qk_ps, s_ps, t_ps, o_ps = bank[0], bank[1], bank[2:4], bank[4:6], bank[6:8]
        mt_ps = qk_ps[0:NPART * H // 2, 0:T // 2].bitcast(BF16)

        spare = sem("a_spare")
        loaded = sem("a_loaded")
        consts = sem("a_consts")
        blank = sem("a_blank")
        fold_p = sem("a_fold_p")
        folded = sem("a_folded")
        x_in = sem("a_x_in")
        stats_d = sem("a_stats_d")
        mv_d = sem("a_mv_d")
        norm_d = sem("a_norm_d")
        y_d = sem("a_y_d")
        z_d = sem("a_z_d")
        z_t = sem("a_z_t")
        xn_d = sem("a_xn_d")
        qk_p = sem("a_qk_p")
        qk_d = sem("a_qk_d")
        split_d = sem("a_split_d")
        parts_out = sem("a_parts_out")
        stack_in = sem("a_stack_in")
        v_p = sem("a_v_p")
        v_d = sem("a_v_d")
        score = sem("a_score")
        maxed = sem("a_maxed")
        mp_d = sem("a_mp_d")
        mt_p = sem("a_mt_p")
        mt_d = sem("a_mt_d")
        mt_out = sem("a_mt_out")
        m_in = [sem(f"a_m_in{i}") for i in range(2)]
        shifted = sem("a_shifted")
        exped = sem("a_exped")
        pv = sem("a_pv")
        ov_d = sem("a_ov_d")
        post = sem("a_post")
        cexp_d = sem("a_cexp_d")
        prod_d = sem("a_prod_d")
        ao_d = sem("a_ao_d")
        y_out = sem("a_y_out")
        ao_out = sem("a_ao_out")

        parts_dram = d["a_parts_dram"]
        m_dram = d["a_m_dram"]
        pairs = lambda a: a.rearrange("(j u) (i p) f -> j u p i f", u=2, p=P)
        x_dram, y_dram, ao_dram = pairs(d["x"]), pairs(d["y"]), pairs(d["ao"])
        SPLIT, NORM, MP, POST = 4, 7, 8, 9
        OFF = 10
        N_LOAD = 12

        block = ctx.enter_context(nc.Block())

        @block.sync
        def _(sp):
            for dst, src in ((w_q[:, :], d["a_Wq"]), (w_k[:, :], d["a_Wk"]), (w_v[:, 0:RD], d["a_Wv_t"]),
                             (b_v[:, 0:RD], d["a_bv_b"]),
                             (w_qv[:, :, :], d["a_Wqv"].rearrange("(c p) f -> p c f", p=P)),
                             (w_vn[:, :], d["a_Wv"]),
                             (s_qv[:, :, :], d["a_sel_qv"].rearrange("(c p) f -> p c f", p=P)),
                             (s_v[:, :], d["a_sel_v"]),
                             (b_qv[:, :, :], d["a_bqv_b"].rearrange("(c p) f -> p c f", p=P)),
                             (b_vr[:, :], d["a_bv_r"]), (cols[:, :], d["a_cols"]),
                             (ident[:, :], d["ident"])):
                sp.dma_start(dst, src).then_inc(loaded, 16)
            sp.wait_ge(consts, 7)

            def body(j, u):
                n = 2 * j + u
                i = u
                if active(j, u, 0):
                    if not isinstance(j, int) or n >= 2:
                        sp.wait_ge(z_d, (n - 1) * NT)
                        apart(sp, spare)
                    sp.wait_ge(x_in, n * 16)
                    apart(sp, spare)
                    at = pair(j, u, 0)
                    sp.dma_start(x[i][:, :, :], x_dram[at[0], at[1]]).then_inc(x_in, 16)

                def shift_rows(half_):
                    b, o = n - 1, 1 - i
                    sp.wait_ge(mt_d, 2 * b + half_ + 1)
                    apart(sp, spare)
                    sp.dma_start(m_dram[o, half_], mt[half_][:, :]).then_inc(mt_out, 16)
                    sp.wait_ge(mt_out, (2 * b + half_ + 1) * 16)
                    apart(sp, spare)
                    hs = slice(half_ * H // 2, (half_ + 1) * H // 2)
                    sp.dma_start(q_st[o][MROW:KROWS, hs, :],
                                 m_dram[o, half_].rearrange("(a h) t -> a h t", a=NPART)).then_inc(m_in[half_], 16)

                if active(j, u, 1):
                    shift_rows(0)
                if active(j, u, 0):
                    sp.wait_ge(y_d, (n + 1) * NT)
                    apart(sp, spare)
                    sp.wait_ge(y_out, n * 16)
                    apart(sp, spare)
                    at = pair(j, u, 0)
                    sp.dma_start(y_dram[at[0], at[1]], y[i][:, :, :]).then_inc(y_out, 16)
                    sp.wait_ge(split_d, (n + 1) * SPLIT)
                    apart(sp, spare)
                    sp.dma_start(parts_dram[i].rearrange("c p t -> p c t"),
                                 parts[i][:, :, :, :].rearrange("p q c t -> p (q c) t")).then_inc(parts_out, 16)
                if active(j, u, 3):
                    at = pair(j, u, 3)
                    sp.wait_ge(ao_d, (n - 2) * NT)
                    apart(sp, spare)
                    sp.wait_ge(ao_out, (n - 3) * 16)
                    apart(sp, spare)
                    sp.dma_start(ao_dram[at[0], at[1]], ao[1 - i][:, :, :]).then_inc(ao_out, 16)
                if active(j, u, 1):
                    shift_rows(1)
                if active(j, u, 0):
                    sp.wait_ge(parts_out, (n + 1) * 16)
                    apart(sp, spare)
                    if not isinstance(j, int) or n >= 2:
                        sp.wait_ge(shifted, (n - 1) * H)
                        apart(sp, spare)
                    for a in range(NPART):
                        sp.dma_start(q_st[i][a * NPART * HD:(a + 1) * NPART * HD, :, :],
                                     parts_dram[i, a].rearrange("(d h) t -> d h t", d=HD).unsqueeze(0)
                                     .broadcast_to([NPART, HD, H, T])).then_inc(stack_in, 16)
                    sp.dma_start(k_st[i][0:SROWS, :, :],
                                 parts_dram[i, NPART:2 * NPART].rearrange("c (d h) t -> (c d) h t", d=HD)
                                 .unsqueeze(0).broadcast_to([NPART, NPART * HD, H, T])).then_inc(stack_in, 16)

            pipeline(sp, body)
            sp.wait_ge(y_out, NB * 16)
            sp.wait_ge(ao_out, NB * 16)

        @block.gpsimd
        def _(pool):
            def const(k, ins):
                ins.then_inc(consts, 1)
                pool.wait_ge(consts, k)

            const(1, pool.memset(half[:, :], -0.5))
            for i in range(2):
                const(2 + 3 * i, pool.memset(k_st[i][64:P, :, :], 0.0))
                const(3 + 3 * i, pool.memset(k_st[i][MROW:P, :, :], 1.0))
                const(4 + 3 * i, pool.memset(q_st[i][64:MROW, :, :], 0.0))

            def body(j, u):
                n = 2 * j + u
                i = u
                if active(j, u, 0):
                    pool.wait_ge(mv_d, (n + 1) * NT)
                    if not isinstance(j, int) or n >= 1:
                        pool.wait_ge(z_d, n * NT)

                    def norm(k, ins):
                        ins.then_inc(norm_d, 1)
                        pool.wait_ge(norm_d, n * NORM + k)
                        apart(pool, spare)

                    apart(pool, spare)
                    norm(1, pool.tensor_scalar(rt[:, 0, :], mv[:, :, 1], EPS, None, ALU.add))
                    norm(2, pool.tensor_tensor(r1[:, :], rt[:, 0, :], half[:, :], ALU.pow))
                    norm(3, pool.tensor_tensor(rt[:, 1, :], r1[:, :], r1[:, :], ALU.mult))
                    norm(4, pool.tensor_tensor(rt[:, 2, :], rt[:, 1, :], mv[:, :, 1], ALU.mult))
                    norm(5, pool.tensor_scalar(rt[:, 3, :], rt[:, 2, :], EPS, None, ALU.add))
                    norm(6, pool.tensor_tensor(rt[:, 1, :], rt[:, 3, :], half[:, :], ALU.pow))
                    norm(7, pool.tensor_tensor(r2[:, :], rt[:, 1, :], r1[:, :], ALU.mult))

                    pool.wait_ge(qk_d, (n + 1) * 2)
                    if not isinstance(j, int) or n >= 2:
                        pool.wait_ge(parts_out, (n - 1) * 16)

                    def split(k, ins):
                        ins.then_inc(split_d, 1)
                        pool.wait_ge(split_d, n * SPLIT + k)
                        apart(pool, spare)

                    apart(pool, spare)
                    split(1, pool.tensor_copy(parts[i][:, :, 0, :], qk[i][:, :, :]))
                    split(2, pool.tensor_tensor(rest[:, :, :], qk[i][:, :, :], parts[i][:, :, 0, :], ALU.subtract))
                    split(3, pool.tensor_copy(parts[i][:, :, 1, :], rest[:, :, :]))
                    split(4, pool.tensor_tensor(parts[i][:, :, 2, :], rest[:, :, :], parts[i][:, :, 1, :],
                                                ALU.subtract))
                if active(j, u, 2):
                    b, o = n - 2, i
                    pool.wait_ge(post, (b + 1) * POST)
                    if not isinstance(j, int) or n >= 3:
                        pool.wait_ge(ao_d, b * NT)
                    pool.tensor_tensor(
                        prod[:, :, :].rearrange("p g (r e) -> p g r e", r=R),
                        ov[o][:, :, 0:RD].rearrange("p g (r e) -> p g r e", r=R),
                        wgt[:, :, :].unsqueeze(3).broadcast_to([P, H * NT, R, HD]), ALU.mult).then_inc(prod_d, 1)

            pipeline(pool, body)

        @block.scalar
        def _(act):
            act.wait_ge(loaded, N_LOAD * 16)
            act.mul(b_qs[:, :], cols[:, 0:1], HD ** -0.5).then_inc(folded, 1)
            act.copy(ident16[:, :], ident[:, :]).then_inc(folded, 1)
            act.wait_ge(fold_p, 1)
            act.wait_ge(blank, 3)
            act.copy(w_v[:, CC:CS], bank[0][:, 0:R]).then_inc(folded, 1)
            act.mul(w_v[:, CQ:CQ + H], bank[0][:, 16:16 + H], QK ** -0.5).then_inc(folded, 1)
            act.copy(b_v[:, CC:CS], bank[0][:, 32:32 + R]).then_inc(folded, 1)
            act.activation(b_v[:, CQ:CQ + H], bank[0][:, 48:48 + H], ACT.Identity, scale=QK ** -0.5,
                           bias=cols[:, 4:5]).then_inc(folded, 1)

            def body(j, u):
                n = 2 * j + u
                i = u
                for s in range(H):
                    if s == 2 and active(j, u, 0):
                        act.wait_ge(z_t, n + 1)
                        act.activation(xn[i][:, :], zv_ps[:, 0:T], ACT.Identity, scale=cols[:, 2:3],
                                       bias=cols[:, 3:4]).then_inc(xn_d, 1)
                    if s == 4 and active(j, u, 0):
                        act.wait_ge(qk_p, n + 1)
                        act.activation(qk[i][:, 0, :], qk_ps[:, 0:T], ACT.Identity, scale=HD ** -0.5,
                                       bias=b_qs[:, 0:1]).then_inc(qk_d, 1)
                        act.activation(qk[i][:, 1, :], qk_ps[:, T:2 * T], ACT.Identity,
                                       bias=cols[:, 1:2]).then_inc(qk_d, 1)
                    for half_ in range(2):
                        if s == (6, 9)[half_] and active(j, u, 1):
                            b = n - 1
                            act.wait_ge(mt_p, 2 * b + half_ + 1)
                            if not isinstance(j, int) or b >= 1:
                                act.wait_ge(mt_out, (2 * b + half_ - 1) * 16)
                            act.copy(mt[half_][:, :], mt_ps).then_inc(mt_d, 1)
                    lag, h = (1, s - OFF) if s >= OFF else (2, s + H - OFF)
                    b = n - lag
                    if active(j, u, lag):
                        act.wait_ge(shifted, b * H + h + 1)
                        if h >= 4 or not isinstance(j, int) or b >= 1:
                            act.wait_ge(pv, b * H + h - 3)
                        act.activation(prob[h % 4][:, :, :].rearrange("p a b -> p (a b)"), t_ps[h % 2][:, :],
                                       ACT.Exp).then_inc(exped, 1)
                    lag, g = (lag, h // 2 - 1) if h >= 2 else (lag + 1, H // 2 - 1)
                    b = n - lag
                    if h % 2 == 0 and active(j, u, lag):
                        act.wait_ge(pv, b * H + 2 * g + 2)
                        if g == 0 and (not isinstance(j, int) or b >= 2):
                            act.wait_ge(prod_d, b - 1)
                        act.copy(ov[(i + lag) % 2][:, 4 * g:4 * g + 4, :],
                                 o_ps[g % 2][:, 0:4 * VC].rearrange("p (g c) -> p g c", g=4)[:, :, 0:CQ]
                                 ).then_inc(ov_d, 1)
                    if s == 13 and active(j, u, 2):
                        act.wait_ge(post, (n - 2) * POST + 5)
                        if not isinstance(j, int) or n >= 3:
                            act.wait_ge(post, (n - 2) * POST)
                        act.activation(cexp[:, :, :], comp3[:, :, :], ACT.Exp).then_inc(cexp_d, 1)

            pipeline(act, body)

        @block.tensor
        def _(pe):
            pe.wait_ge(loaded, N_LOAD * 16)
            pe.matmul(bank[0][:, 0:R], w_vn[:, :], s_v[:, :], start=True, stop=True)
            for c in range(4):
                pe.matmul(bank[0][:, 16:16 + H], w_qv[:, c, :], s_qv[:, c, :], start=c == 0, stop=c == 3)
            pe.matmul(bank[0][:, 32:32 + R], b_vr[:, :], s_v[:, :], start=True, stop=True)
            for c in range(4):
                mm = pe.matmul(bank[0][:, 48:48 + H], b_qv[:, c, :], s_qv[:, c, :], start=c == 0, stop=c == 3)
            mm.then_inc(fold_p, 1)
            pe.wait_ge(folded, 6)
            pe.wait_ge(consts, 7)

            def body(j, u):
                n = 2 * j + u
                i = u
                for s in range(H):
                    if s == 1 and active(j, u, 0):
                        pe.wait_ge(z_d, (n + 1) * NT)
                        if not isinstance(j, int) or n >= 1:
                            pe.wait_ge(v_d, n)
                        for t in range(NT):
                            mm = pe.transpose(zv_ps[:, t * P:(t + 1) * P], z[i][:, t, :], ident[:, :])
                        mm.then_inc(z_t, 1)
                    if s == 3 and active(j, u, 0):
                        pe.wait_ge(xn_d, n + 1)
                        if not isinstance(j, int) or n >= 2:
                            pe.wait_ge(mt_d, 2 * (n - 1))
                        pe.matmul(qk_ps[:, 0:T], w_q[:, :], xn[i][:, :], start=True, stop=True)
                        pe.matmul(qk_ps[:, T:2 * T], w_k[:, :], xn[i][:, :], start=True, stop=True).then_inc(qk_p, 1)
                    if s == 11 and active(j, u, 0):
                        for t in range(NT):
                            mm = pe.matmul(zv_ps[:, t * VC:(t + 1) * VC], xn[i][:, t * P:(t + 1) * P], w_v[:, :],
                                           start=True, stop=True)
                        mm.then_inc(v_p, 1)
                    if s < H // 2 and active(j, u, 1):
                        b, o = n - 1, 1 - i
                        if s == 0:
                            pe.wait_ge(stack_in, (b + 1) * 4 * 16)
                        for t in range(NT):
                            w = 2 * s + t
                            if w >= 2 or not isinstance(j, int) or b >= 1:
                                pe.wait_ge(maxed, b * H + w - 1)
                            for hh in range(2):
                                mm = pe.matmul(s_ps[t][:, hh * T:(hh + 1) * T],
                                               q_st[o][0:MROW, 2 * s + hh, t * P:(t + 1) * P],
                                               k_st[o][0:MROW, 2 * s + hh, :], start=True, stop=True)
                            mm.then_inc(score, 1)
                    for half_ in range(2):
                        if s == (5, 8)[half_] and active(j, u, 1):
                            b = n - 1
                            pe.wait_ge(mp_d, b * MP + 4 * (half_ + 1))
                            pe.wait_ge(qk_d, min(n + 1, NB) * 2 if isinstance(j, int) else (n + 1) * 2)
                            if half_ or not isinstance(j, int) or b >= 1:
                                pe.wait_ge(mt_d, 2 * b + half_)
                            for t in range(NT):
                                mm = pe.transpose(mt_ps[:, t * P:(t + 1) * P],
                                                  mpart[:, t, half_, :, :].rearrange("p a h -> p (a h)"),
                                                  ident16[:, :])
                            mm.then_inc(mt_p, 1)
                    lag, h = (1, s - OFF) if s >= OFF else (2, s + H - OFF)
                    if active(j, u, lag):
                        b, o = n - lag, (i + lag) % 2
                        if h % (H // 2) == 0:
                            pe.wait_ge(m_in[h // (H // 2)], (b + 1) * 16)
                        if h >= 2 or not isinstance(j, int) or b >= 1:
                            pe.wait_ge(exped, b * H + h - 1)
                        for c in range(NT):
                            mm = pe.matmul(t_ps[h % 2][:, c * T:(c + 1) * T],
                                           k_st[o][0:KROWS, h, c * P:(c + 1) * P], q_st[o][0:KROWS, h, :],
                                           start=True, stop=True)
                        mm.then_inc(shifted, 1)
                    lag, h = (lag, h - 1) if h else (lag + 1, H - 1)
                    if active(j, u, lag):
                        b, o = n - lag, (i + lag) % 2
                        g = h // 2
                        pe.wait_ge(exped, b * H + h + 1)
                        if h == 0:
                            pe.wait_ge(v_d, b + 1)
                        if h % 2 == 0 and (g >= 2 or not isinstance(j, int) or b >= 1):
                            pe.wait_ge(ov_d, b * (H // 2) + g - 1)
                        for t in range(NT):
                            for c in range(NT):
                                at = (2 * (h % 2) + t) * VC
                                mm = pe.matmul(o_ps[g % 2][:, at:at + VC], prob[h % 4][:, c, t * P:(t + 1) * P],
                                               vp[o][:, c, :], start=c == 0, stop=c == NT - 1)
                        mm.then_inc(pv, 1)

            pipeline(pe, body)

        @block.vector
        def _(dve):
            dve.memset(w_v[:, RD:VC], 0.0).then_inc(blank, 1)
            dve.memset(b_v[:, RD:VC], 0.0).then_inc(blank, 1)
            dve.wait_ge(blank, 2)
            dve.memset(b_v[:, CS:CS + 1], 1.0).then_inc(blank, 1)
            dve.wait_ge(folded, 6)

            def body(j, u):
                n = 2 * j + u
                i = u
                first = isinstance(j, int)
                if active(j, u, 0):
                    dve.wait_ge(x_in, (n + 1) * 16)
                    if not first or n >= 1:
                        dve.wait_ge(norm_d, n * NORM)
                    for t in range(NT):
                        dve.bn_stats(stats[:, t, :], x[i][:, t, :]).then_inc(stats_d, 1)
                    for t in range(NT):
                        dve.wait_ge(stats_d, n * NT + t + 1)
                        apart(dve, spare)
                        dve.bn_aggr(mv[:, t, :], stats[:, t, :]).then_inc(mv_d, 1)

                def reduce_unit(w):
                    b = n - 1
                    dve.wait_ge(score, b * H + w + 1)
                    g, t = w // 2, w % 2
                    if w == 0 and (not first or b >= 1):
                        dve.wait_ge(mp_d, b * MP)
                    dve.tensor_reduce(nmax[:, t, 2 * g:2 * g + 2],
                                      s_ps[t][:, :].rearrange("p (h k) -> p h k", h=2), AX.X, ALU.max,
                                      negate=True).then_inc(maxed, 1)

                def split_max(half_):
                    b = n - 1
                    hs = slice(half_ * H // 2, (half_ + 1) * H // 2)
                    dve.wait_ge(maxed, b * H + 8 * (half_ + 1))
                    if not first or b >= 1:
                        dve.wait_ge(mt_p, 2 * (b - 1) + half_ + 1)

                    def link(k, ins):
                        ins.then_inc(mp_d, 1)
                        dve.wait_ge(mp_d, b * MP + 4 * half_ + k)

                    link(1, dve.tensor_copy(mpart[:, :, half_, 0, :], nmax[:, :, hs]))
                    link(2, dve.tensor_tensor(nrest[:, :, hs], nmax[:, :, hs], mpart[:, :, half_, 0, :],
                                              ALU.subtract))
                    link(3, dve.tensor_copy(mpart[:, :, half_, 1, :], nrest[:, :, hs]))
                    link(4, dve.tensor_tensor(mpart[:, :, half_, 2, :], nrest[:, :, hs],
                                              mpart[:, :, half_, 1, :], ALU.subtract))

                for w in range(H):
                    if active(j, u, 1):
                        reduce_unit(w)
                        if w in (7, 15):
                            split_max(w // 8)
                    if w == 1 and active(j, u, 0):
                        dve.wait_ge(norm_d, (n + 1) * NORM)
                        if not first or n >= 2:
                            dve.wait_ge(y_out, (n - 1) * 16)
                            dve.wait_ge(z_t, n - 1)
                        for t in range(NT):
                            dve.tensor_scalar(y[i][:, t, :], x[i][:, t, :], mv[:, t, 0:1], r1[:, t:t + 1],
                                              ALU.subtract, ALU.mult).then_inc(y_d, 1)
                        for t in range(NT):
                            dve.tensor_scalar(z[i][:, t, :], x[i][:, t, :], mv[:, t, 0:1], r2[:, t:t + 1],
                                              ALU.subtract, ALU.mult).then_inc(z_d, 1)
                    if w == 5 and active(j, u, 3):
                        b, o = n - 3, 1 - i
                        dve.wait_ge(prod_d, b + 1)
                        if not first or b >= 2:
                            dve.wait_ge(ao_out, (b - 1) * 16)
                        for t in range(NT):
                            dve.tensor_reduce(
                                ao[o][:, t, :].rearrange("p (h e) -> p h e", h=H),
                                prod[:, :, :].rearrange("p (h i) (r e) -> p i h e r", i=NT, r=R)[:, t],
                                AX.X, ALU.add).then_inc(ao_d, 1)
                if active(j, u, 2):
                    b, o = n - 2, i
                    dve.wait_ge(ov_d, (b + 1) * H // 2)
                    if not first or b >= 1:
                        dve.wait_ge(prod_d, b)

                    def link(k, ins):
                        ins.then_inc(post, 1)
                        dve.wait_ge(post, b * POST + k)

                    def wide(a):
                        return a[:, :].unsqueeze(2).broadcast_to([P, H * NT, R])

                    link(1, dve.reciprocal(inv[:, :], ov[o][:, :, CS]))
                    link(2, dve.tensor_tensor(comp[:, :, :], ov[o][:, :, CC:CS], wide(inv), ALU.mult))
                    link(3, dve.tensor_tensor(
                        comp2[:, :, :].rearrange("p (h i) r -> p h i r", i=NT),
                        comp[:, :, :].rearrange("p (h i) r -> p h i r", i=NT),
                        vp[o][:, :, CQ:CQ + H].rearrange("p i h -> p h i").unsqueeze(3)
                        .broadcast_to([P, H, NT, R]), ALU.add))
                    link(4, dve.tensor_reduce(cmax[:, :], comp2[:, :, :], AX.X, ALU.max))
                    link(5, dve.tensor_tensor(comp3[:, :, :], comp2[:, :, :], wide(cmax), ALU.subtract))
                    dve.wait_ge(cexp_d, b + 1)
                    link(6, dve.tensor_reduce(csum[:, :], cexp[:, :, :], AX.X, ALU.add))
                    link(7, dve.reciprocal(cinv[:, :], csum[:, :]))
                    link(8, dve.tensor_tensor(cw[:, :], cinv[:, :], inv[:, :], ALU.mult))
                    link(9, dve.tensor_tensor(wgt[:, :, :], cexp[:, :, :], wide(cw), ALU.mult))
                if active(j, u, 0):
                    dve.wait_ge(v_p, n + 1)
                    if not first or n >= 2:
                        dve.wait_ge(pv, (n - 1) * H)
                    dve.tensor_tensor(vp[i][:, :, :], zv_ps[:, 0:NT * VC].rearrange("p (i c) -> p i c", i=NT),
                                      b_v[:, :].unsqueeze(1).broadcast_to([P, NT, VC]), ALU.add).then_inc(v_d, 1)

            pipeline(dve, body)


def fold_ffn(nc, d):
    ctx = ExitStack()
    with ctx:
        sb, sem = memory(nc, ctx, "w")
        w1 = [sb(f"w1_{i}", [P, NI, P]) for i in range(2)]
        w2 = [sb(f"w2_{i}", [P, NI, P]) for i in range(2)]
        bias = [sb(f"bias_{i}", [P, NI + 1]) for i in range(2)]
        ones = sb("ones", [P, P])
        ident = sb("ident", [P, P])
        rows = [sb(f"rows_{i}", [P, P]) for i in range(2)]
        col = [sb(f"col_{i}", [P, 1]) for i in range(2)]
        fold = [sb(f"fold_{i}", [P, 2, P]) for i in range(2)]
        bank = [ctx.enter_context(nc.psum_tensor(f"w_bank{i}", [P, 512], F32)) for i in range(6)]
        w_in = [sem(f"in{i}") for i in range(2)]
        ident_in = sem("ident_in")
        ones_d = sem("ones_d")
        prod_p = sem("prod_p")
        col_d = sem("col_d")
        rows_d = sem("rows_d")
        turned = sem("turned")
        fold_d = sem("fold_d")
        out_d = sem("out_d")
        block = ctx.enter_context(nc.Block())

        def store(sp, g):
            sp.wait_ge(fold_d, 2 * (g + 1))
            sp.wait_ge(out_d, 2 * g * 16)
            for c in range(2):
                sp.dma_start(d["folded"][2 * g + c], fold[g % 2][:, :, :].rearrange("p a o -> p (a o)")
                             ).then_inc(out_d, 16)

        @block.sync
        def _(sp):
            sp.dma_start(ident[:, :], d["ident"]).then_inc(ident_in, 16)
            for g in range(NG):
                i = g % 2
                if g >= 2:
                    sp.wait_ge(prod_p, g - 1)
                    sp.wait_ge(col_d, g - 1)
                sp.dma_start(w1[i][:, :, :], d["W1"][g].rearrange("(c p) h -> p c h", p=P)).then_inc(w_in[i], 16)
                sp.dma_start(w2[i][:, :, :], d["W2_t"][g].rearrange("(c p) o -> p c o", p=P)).then_inc(w_in[i], 16)
                sp.dma_start(bias[i][:, :], d["ffn_b"][g]).then_inc(w_in[i], 16)
                if g >= 1:
                    store(sp, g - 1)
            store(sp, NG - 1)
            sp.wait_ge(out_d, NG * 2 * 16)

        @block.vector
        def _(dve):
            dve.memset(ones[:, :], 1.0).then_inc(ones_d, 1)
            dve.wait_ge(ones_d, 1)
            for g in range(NG):
                i = g % 2
                dve.wait_ge(prod_p, g + 1)
                dve.tensor_tensor(col[i][:, :], bank[2 + i][:, 0:1], bias[i][:, NI:NI + 1], ALU.add).then_inc(col_d, 1)
                dve.wait_ge(col_d, g + 1)
                if g >= 2:
                    dve.wait_ge(turned, g - 1)
                dve.tensor_scalar(rows[i][:, :], ones[:, :], col[i][:, 0:1], None, ALU.mult).then_inc(rows_d, 1)

        @block.scalar
        def _(act):
            for g in range(NG):
                i = g % 2
                act.wait_ge(prod_p, g + 1)
                if g >= 2:
                    act.wait_ge(out_d, (g - 1) * 2 * 16)
                act.copy(fold[i][:, 0, :], bank[i][:, 0:P]).then_inc(fold_d, 1)
                act.wait_ge(turned, g + 1)
                act.copy(fold[i][:, 1, :], bank[4 + i][:, 0:P]).then_inc(fold_d, 1)

        @block.tensor
        def _(pe):
            pe.wait_ge(ident_in, 16)
            for g in range(NG):
                i = g % 2
                pe.wait_ge(w_in[i], (g // 2 + 1) * 48)
                if g >= 2:
                    pe.wait_ge(fold_d, 2 * (g - 1))
                for c in range(NI):
                    pe.matmul(bank[i][:, 0:P], w1[i][:, c, :], w2[i][:, c, :], start=c == 0, stop=c == NI - 1)
                for c in range(NI):
                    mm = pe.matmul(bank[2 + i][:, 0:1], w2[i][:, c, :], bias[i][:, c:c + 1], start=c == 0,
                                   stop=c == NI - 1)
                mm.then_inc(prod_p, 1)
                pe.wait_ge(rows_d, g + 1)
                pe.transpose(bank[4 + i][:, 0:P], rows[i][:, :], ident[:, :]).then_inc(turned, 1)


def dense(nc, d):
    ctx = ExitStack()
    with ctx:
        sb, sem = memory(nc, ctx, "b")
        NU, C = NB // 2, 2 * NT
        w_f = sb("w_f", [P, P])
        w_r1 = sb("w_r1", [P, 2, P])
        w_r2 = sb("w_r2", [P, 2, P])
        b_f = sb("b_f", [P, P])
        b_r2 = sb("b_r2", [P, P])
        cols = sb("cols", [P, 4])
        ident = sb("ident", [P, P])
        half = sb("half", [P, C])
        two = lambda name, shape: [sb(f"{name}{i}", shape) for i in range(2)]
        x, y, ao = two("x", [P, C, P]), two("y", [P, C, P]), two("ao", [P, C, P])
        wc = two("wc", [P, 2, P])
        ao_t, r, xr = two("ao_t", [P, C * P]), two("r", [P, C, P]), two("xr", [P, C, P])
        yb, z, on = two("yb", [P, C, P]), two("z", [P, C, P]), two("on", [P, C * P])
        hid, x1, xb = two("hid", [P, 2, C * P]), two("x1", [P, C, P]), two("xb", [P, C, P])
        z1, z1t, x2 = two("z1_", [P, C, P]), two("z1t", [P, C * P]), two("x2_", [P, C, P])
        stats, mv = two("stats", [P, C, 6]), two("mv", [P, C, 2])
        var, rs = two("var", [P, C]), two("rs", [P, C])
        bank = [ctx.enter_context(nc.psum_tensor(f"b_bank{i}", [P, 512], F32)) for i in range(8)]
        aot_ps, zt_ps, z1t_ps, r_ps, h_ps, f_ps, g_ps = *bank[0:4], bank[4:6], bank[6], bank[7]

        spare = sem("spare")
        loaded = sem("loaded")
        half_d = sem("half_d")
        ay_in = sem("ay_in")
        x_in = sem("x_in")
        wc_in = sem("wc_in")
        aot_p, aot_d = sem("aot_p"), sem("aot_d")
        yb_d = sem("yb_d")
        r_p, r_d = sem("r_p"), sem("r_d")
        xr_d = sem("xr_d")
        stat_d = [sem(f"stat_d{i}") for i in range(2)]
        mv_d = [sem(f"mv_d{i}") for i in range(2)]
        norm_d = [sem(f"norm_d{i}") for i in range(2)]
        z_d = [sem(f"z_d{i}") for i in range(2)]
        zt_p, on_d = sem("zt_p"), sem("on_d")
        h_p, hid_d = sem("h_p"), sem("hid_d")
        f_p, x1_d, xb_d = sem("f_p"), sem("x1_d"), sem("xb_d")
        z1t_p, z1t_d = sem("z1t_p"), sem("z1t_d")
        g_p, x2_d, x2_out = sem("g_p"), sem("x2_d"), sem("x2_out")

        units = lambda a: a.rearrange("b t f -> (b t) f").rearrange("(j u c p) f -> j u p c f", u=2, c=C, p=P)
        x_dram, y_dram, ao_dram, x2_dram = units(d["x"]), units(d["y"]), units(d["ao"]), units(d["x2"])
        wc_dram = d["folded"].rearrange("(j u) p f -> j u p f", u=2)
        has = lambda j, u, lag: active(j, u, lag, NU)
        later = lambda j, n, k: not isinstance(j, int) or n >= k
        flat = lambda a: a[:, :, :].rearrange("p c f -> p (c f)")
        block = ctx.enter_context(nc.Block())

        @block.sync
        def _(sp):
            for dst, src in ((w_f[:, :], d["a_Wf_t"]),
                             (w_r1[:, :, :].rearrange("p a f -> p (a f)"), d["a_Wr1_t"]),
                             (w_r2[:, :, :], d["a_Wr2_t"].rearrange("(a p) f -> p a f", p=P)),
                             (b_f[:, :], d["a_bf_b"]), (b_r2[:, :], d["a_br2_b"]), (cols[:, :], d["b_cols"]),
                             (ident[:, :], d["ident"])):
                sp.dma_start(dst, src).then_inc(loaded, 16)

            def body(j, u):
                n, i = 2 * j + u, u
                if has(j, u, 0):
                    at = pair(j, u, 0)
                    sp.wait_ge(ay_in, n * 32)
                    apart(sp, spare)
                    if later(j, n, 2):
                        sp.wait_ge(aot_p, n - 1)
                        apart(sp, spare)
                        sp.wait_ge(yb_d, n - 1)
                        apart(sp, spare)
                    sp.dma_start(ao[i][:, :, :], ao_dram[at[0], at[1]]).then_inc(ay_in, 16)
                    sp.dma_start(y[i][:, :, :], y_dram[at[0], at[1]]).then_inc(ay_in, 16)
                    if later(j, n, 2):
                        sp.wait_ge(xr_d, (n - 1) * 2)
                        apart(sp, spare)
                    sp.wait_ge(x_in, n * 16)
                    apart(sp, spare)
                    sp.dma_start(x[i][:, :, :], x_dram[at[0], at[1]]).then_inc(x_in, 16)
                if has(j, u, 2):
                    sp.wait_ge(x2_d, n - 1)
                    apart(sp, spare)
                    at = pair(j, u, 2)
                    sp.wait_ge(x2_out, (n - 2) * 16)
                    apart(sp, spare)
                    sp.dma_start(x2_dram[at[0], at[1]], x2[i][:, :, :]).then_inc(x2_out, 16)
                if has(j, u, 1):
                    at = pair(j, u, 1)
                    if later(j, n, 3):
                        sp.wait_ge(g_p, n - 2)
                        apart(sp, spare)
                        sp.wait_ge(xb_d, n - 2)
                        apart(sp, spare)
                    sp.wait_ge(wc_in, (n - 1) * 16)
                    apart(sp, spare)
                    sp.dma_start(wc[1 - i][:, :, :].rearrange("p a f -> p (a f)"), wc_dram[at[0], at[1]]
                                 ).then_inc(wc_in, 16)

            pipeline(sp, body, NU, 3)
            sp.wait_ge(x2_out, NU * 16)

        @block.gpsimd
        def _(pool):
            pool.memset(half[:, :], -0.5).then_inc(half_d, 1)
            pool.wait_ge(half_d, 1)
            pool.wait_ge(loaded, 7 * 16)

            def norm(k, n):
                pool.wait_ge(mv_d[k], (n + 1) * C)
                apart(pool, spare)
                pool.tensor_scalar(var[k][:, :], mv[k][:, :, 1], EPS, 1.0, ALU.add, ALU.mult).then_inc(norm_d[k], 1)
                pool.wait_ge(norm_d[k], 2 * n + 1)
                pool.tensor_tensor(rs[k][:, :], var[k][:, :], half[:, :], ALU.pow).then_inc(norm_d[k], 1)

            rows = lambda a: a[:, :].unsqueeze(1).broadcast_to([P, C, P])

            def body(j, u):
                n, i = 2 * j + u, u
                if has(j, u, 0):
                    pool.wait_ge(ay_in, (n + 1) * 32)
                    if later(j, n, 2):
                        pool.wait_ge(r_d, n - 1)
                    pool.tensor_tensor(yb[i][:, :, :], y[i][:, :, :], rows(b_f), ALU.add).then_inc(yb_d, 1)
                    pool.wait_ge(x_in, (n + 1) * 16)
                    if later(j, n, 2):
                        pool.wait_ge(x1_d, n - 1)
                    pool.tensor_tensor(xr[i][:, :, :], x[i][:, :, :], rows(b_r2), ALU.add).then_inc(xr_d, 1)
                    norm(0, n)
                    pool.wait_ge(r_d, n + 1)
                    pool.wait_ge(xr_d, 2 * n + 1)
                    pool.tensor_tensor(xr[i][:, :, :], xr[i][:, :, :], r[i][:, :, :], ALU.add).then_inc(xr_d, 1)
                if has(j, u, 1):
                    norm(1, n - 1)
                    pool.wait_ge(wc_in, n * 16)
                    pool.wait_ge(x1_d, n)
                    if later(j, n, 3):
                        pool.wait_ge(x2_d, n - 2)
                    pool.tensor_tensor(xb[1 - i][:, :, :], x1[1 - i][:, :, :],
                                       wc[1 - i][:, 1, :].unsqueeze(1).broadcast_to([P, C, P]), ALU.add
                                       ).then_inc(xb_d, 1)

            pipeline(pool, body, NU, 3)

        @block.scalar
        def _(act):
            act.wait_ge(loaded, 7 * 16)

            def body(j, u):
                n, i = 2 * j + u, u
                if has(j, u, 1):
                    act.wait_ge(zt_p, n)
                    act.activation(on[1 - i][:, :], zt_ps[:, :], ACT.Identity, scale=cols[:, 2:3], bias=cols[:, 3:4]
                                   ).then_inc(on_d, 1)
                if has(j, u, 0):
                    act.wait_ge(aot_p, n + 1)
                    act.copy(ao_t[i][:, :], aot_ps[:, :]).then_inc(aot_d, 1)
                if has(j, u, 1):
                    if later(j, n, 3):
                        act.wait_ge(f_p, n - 2)
                    for c in range(2):
                        act.wait_ge(h_p, 2 * (n - 1) + c + 1)
                        act.activation(hid[1 - i][:, c, :], h_ps[c][:, :], ACT.Relu, bias=cols[:, c:c + 1]
                                       ).then_inc(hid_d, 1)
                if has(j, u, 2):
                    act.wait_ge(z1t_p, n - 1)
                    act.copy(z1t[i][:, :], z1t_ps[:, :]).then_inc(z1t_d, 1)

            pipeline(act, body, NU, 3)

        @block.tensor
        def _(pe):
            pe.wait_ge(loaded, 7 * 16)

            def turn(dst, src):
                for c in range(C):
                    mm = pe.transpose(dst[:, c * P:(c + 1) * P], src[:, c, :], ident[:, :])
                return mm

            def body(j, u):
                n, i = 2 * j + u, u
                if has(j, u, 1):
                    pe.wait_ge(z_d[0], n * C)
                    if later(j, n, 2):
                        pe.wait_ge(on_d, n - 1)
                    turn(zt_ps, z[1 - i]).then_inc(zt_p, 1)
                if has(j, u, 0):
                    pe.wait_ge(ay_in, (n + 1) * 32)
                    if later(j, n, 1):
                        pe.wait_ge(aot_d, n)
                    turn(aot_ps, ao[i]).then_inc(aot_p, 1)
                if has(j, u, 1):
                    pe.wait_ge(on_d, n)
                    for c in range(2):
                        if later(j, n, 2):
                            pe.wait_ge(hid_d, 2 * (n - 2) + c + 1)
                        pe.matmul(h_ps[c][:, :], w_r1[:, c, :], on[1 - i][:, :], start=True, stop=True
                                  ).then_inc(h_p, 1)
                if has(j, u, 0):
                    pe.wait_ge(aot_d, n + 1)
                    if later(j, n, 1):
                        pe.wait_ge(r_d, n)
                    for c in range(C):
                        mm = pe.matmul(r_ps[:, c * P:(c + 1) * P], ao_t[i][:, c * P:(c + 1) * P], w_f[:, :],
                                       start=True, stop=True)
                    mm.then_inc(r_p, 1)
                if has(j, u, 1):
                    pe.wait_ge(hid_d, 2 * n)
                    if later(j, n, 2):
                        pe.wait_ge(x1_d, n - 1)
                    for c in range(C):
                        for k in range(2):
                            mm = pe.matmul(f_ps[:, c * P:(c + 1) * P], hid[1 - i][:, k, c * P:(c + 1) * P],
                                           w_r2[:, k, :], start=k == 0, stop=k == 1)
                    mm.then_inc(f_p, 1)
                if has(j, u, 2):
                    pe.wait_ge(z_d[1], (n - 1) * C)
                    if later(j, n, 3):
                        pe.wait_ge(z1t_d, n - 2)
                    turn(z1t_ps, z1[i]).then_inc(z1t_p, 1)
                    pe.wait_ge(z1t_d, n - 1)
                    pe.wait_ge(wc_in, (n - 1) * 16)
                    if later(j, n, 3):
                        pe.wait_ge(x2_d, n - 2)
                    for c in range(C):
                        mm = pe.matmul(g_ps[:, c * P:(c + 1) * P], z1t[i][:, c * P:(c + 1) * P], wc[i][:, 0, :],
                                       start=True, stop=True)
                    mm.then_inc(g_p, 1)

            pipeline(pe, body, NU, 3)

        @block.vector
        def _(dve):
            def moments(k, n, src):
                for c in range(C):
                    dve.bn_stats(stats[k][:, c, :], src[:, c, :]).then_inc(stat_d[k], 1)
                for c in range(C):
                    dve.wait_ge(stat_d[k], n * C + c + 1)
                    apart(dve, spare)
                    dve.bn_aggr(mv[k][:, c, :], stats[k][:, c, :]).then_inc(mv_d[k], 1)

            def normed(k, n, src, dst):
                dve.wait_ge(norm_d[k], 2 * (n + 1))
                for c in range(C):
                    dve.tensor_scalar(dst[:, c, :], src[:, c, :], mv[k][:, c, 0:1], rs[k][:, c:c + 1],
                                      ALU.subtract, ALU.mult).then_inc(z_d[k], 1)

            def body(j, u):
                n, i = 2 * j + u, u
                if has(j, u, 0):
                    dve.wait_ge(r_p, n + 1)
                    dve.wait_ge(yb_d, n + 1)
                    if later(j, n, 2):
                        dve.wait_ge(xr_d, 2 * (n - 1))
                    dve.tensor_tensor(flat(r[i]), r_ps[:, :], flat(yb[i]), ALU.add).then_inc(r_d, 1)
                    dve.wait_ge(r_d, n + 1)
                    moments(0, n, r[i])
                if has(j, u, 2):
                    dve.wait_ge(g_p, n - 1)
                    dve.wait_ge(xb_d, n - 1)
                    if later(j, n, 4):
                        dve.wait_ge(x2_out, (n - 3) * 16)
                    dve.tensor_tensor(flat(x2[i]), g_ps[:, :], flat(xb[i]), ALU.add).then_inc(x2_d, 1)
                if has(j, u, 0):
                    if later(j, n, 2):
                        dve.wait_ge(zt_p, n - 1)
                    normed(0, n, r[i], z[i])
                if has(j, u, 1):
                    dve.wait_ge(f_p, n)
                    dve.wait_ge(xr_d, 2 * n)
                    if later(j, n, 3):
                        dve.wait_ge(xb_d, n - 2)
                    dve.tensor_tensor(flat(x1[1 - i]), f_ps[:, :], flat(xr[1 - i]), ALU.add).then_inc(x1_d, 1)
                    dve.wait_ge(x1_d, n)
                    moments(1, n - 1, x1[1 - i])
                    if later(j, n, 3):
                        dve.wait_ge(z1t_p, n - 2)
                    normed(1, n - 1, x1[1 - i], z1[1 - i])

            pipeline(dve, body, NU, 3)


def attention_b(nc, d):
    ctx = ExitStack()
    with ctx:
        sb, sem = memory(nc, ctx, "c")
        SEG = 64
        NS = T // SEG
        HV = H * HD
        MW = HV + H
        VW = H * (HD + 1)
        WIN = 96
        ST = 8
        S0, OFF = 1, 6
        two = lambda name, shape, dt=F32: [sb(f"{name}{i}", shape, dt) for i in range(2)]
        w_kq = sb("w_kq", [P, 2, P])
        w_v = sb("w_v", [P, P])
        w_o = sb("w_o", [P, P])
        ident, ident16 = sb("ident", [P, P]), sb("ident16", [P, P], BF16)
        causal, causal_t = sb("causal", [P, 512], BF16), sb("causal_t", [P, 512], BF16)
        causal32 = sb("causal32", [P, 2 * P])
        diag = sb("diag", [P, MW])
        beta = sb("beta", [P, 4])
        bexp = sb("bexp", [P, 1])
        half = sb("half", [P, NT])
        wc = two("wc", [P, 2, P])
        x = two("x", [P, NT, P])
        z, zt = two("z", [P, NT, P]), two("zt", [P, T])
        stats, mv = two("stats", [P, NT, 6]), two("mv", [P, NT, 2])
        var, rs = two("var", [P, NT]), two("rs", [P, NT])
        kq = two("kq", [P, 2, T])
        rest = sb("rest", [P, 2, T])
        parts = two("parts", [P, 2, NPART, T], BF16)
        q_st, k_st = two("q_st", [P, H, T], BF16), two("k_st", [P, H, T], BF16)
        pos, neg, nexp = (sb(a, [P, 2, T]) for a in ("pos", "neg", "nexp"))
        sg = two("sg", [P, NS, 2, SEG])
        skn = sb("skn", [P, NS - 1, P])
        uv = two("uv", [P, NS - 1, MW])
        mz, mzt = sb("mz", [P, MW]), sb("mzt", [P, MW])
        dn, dr = sb("dn", [P, NS - 1, H]), sb("dr", [P, NS - 1, H])
        am = two("am", [P, NS - 1, P])
        vb = two("vb", [P, NT, VW + WIN])
        nmax, nrest = sb("nmax", [P, NT, H]), sb("nrest", [P, NT, H])
        mpart = sb("mpart", [P, NT, 2, NPART, H // 2], BF16)
        mt = [sb(f"mt{i}", [NPART * H // 2, T], BF16) for i in range(2)]
        prob = [sb(f"prob{i}", [P, 2, T]) for i in range(4)]
        dinv, ad = sb("dinv", [P, NT, H]), sb("ad", [P, NT, P])
        at_b = sb("at", [P, T])
        xt, x3, xb, x4 = (two(a, [P, NT, P]) for a in ("xt", "x3_", "xb", "x4_"))
        z4, z4t = sb("z4", [P, NT, P]), sb("z4t", [P, T])
        bank = [ctx.enter_context(nc.psum_tensor(f"c_bank{i}", [P, 512], F32)) for i in range(8)]
        ps_a, ps_b, ps_c, s_ps, t_ps, o_ps = *bank[0:3], bank[3:5], bank[5:7], bank[7]
        mt_ps = ps_a[0:NPART * H // 2, 0:T // 2].bitcast(BF16)

        spare, loaded, const_d, beta_d = sem("spare"), sem("loaded"), sem("const_d"), sem("beta_d")
        mask_d = sem("mask_d")
        x_in, xt_in, wc_in = sem("x_in"), sem("xt_in"), sem("wc_in")
        stat_d = [sem(f"stat_d{i}") for i in range(2)]
        mv_d = [sem(f"mv_d{i}") for i in range(2)]
        norm_d = [sem(f"norm_d{i}") for i in range(2)]
        z_d, zt_p, zt_d = sem("z_d"), sem("zt_p"), sem("zt_d")
        kq_p, kq_d = sem("kq_p"), sem("kq_d")
        pn_d, nexp_d, sg_d = sem("pn_d"), sem("nexp_d"), sem("sg_d")
        split_d, parts_out, stack_in = sem("split_d"), sem("parts_out"), sem("stack_in")
        vs_p, vs_d, v_p, v_d = sem("vs_p"), sem("vs_d"), sem("v_p"), sem("v_d")
        sk_p, sk_d = sem("sk_p"), sem("sk_d")
        mem_p = sem("mem_p")
        mz_d = sem("mz_d")
        read_p = sem("read_p")
        read_d = sem("read_d")
        u_d = sem("u_d")
        score, maxed, mp_d = sem("score"), sem("maxed"), sem("mp_d")
        mt_p, mt_d, mt_out = sem("mt_p"), sem("mt_d"), sem("mt_out")
        m_in = [sem(f"m_in{i}") for i in range(2)]
        shifted, exped, pv = sem("shifted"), sem("exped"), sem("pv")
        ad_d = sem("ad_d")
        at_p, at_d = sem("at_p"), sem("at_d")
        wo_p, x3_d, xb_d = sem("wo_p"), sem("x3_d"), sem("xb_d")
        z4_d, z4_p, z4t_d, g_p, x4_d, x4_out = (sem(a) for a in ("z4_d", "z4_p", "z4t_d", "g_p", "x4_d", "x4_out"))

        USES_A = [(kq_d, 2, 0), (mt_d, 2, 1), (at_d, 2, 2)]
        USES_B = [(x3_d, 1, 3), (zt_d, 1, 0), (vs_d, 1, 0), (z4t_d, 1, 3), (x4_d, 1, 3), (v_d, 1, 0)]

        def free(eng, uses, k, j, u):
            n = 2 * j + u
            if not isinstance(j, int):
                s, per, lag = uses[k - 1]
                eng.wait_ge(s, (n - lag - (k == 0) + 1) * per)
                return
            for m, (s, per, lag) in enumerate(uses):
                done = min(n - lag - (m >= k) + 1, NB)
                if done > 0:
                    eng.wait_ge(s, done * per)

        later = lambda j, b, k: not isinstance(j, int) or b >= k
        pairs = lambda a: a.rearrange("(j u) (i p) f -> j u p i f", u=2, p=P)
        x_dram, out_dram, wc_dram = pairs(d["x2"]), pairs(d["out"]), d["folded"]
        parts_dram, m_dram = d["c_parts_dram"], d["c_m_dram"]
        flat = lambda a: a[:, :, :].rearrange("p c f -> p (c f)")
        N_LOAD, SPLIT, MP = 7, 4, 8

        def turn(s):
            return (1, s - OFF) if s >= OFF else (2, s + ST - OFF)

        def before(lag, g):
            return (lag, g - 1) if g else (lag + 1, ST - 1)

        block = ctx.enter_context(nc.Block())

        @block.sync
        def _(sp):
            for dst, src in ((w_kq[:, :, :].rearrange("p a f -> p (a f)"), d["b_Wkq_t"]), (w_v[:, :], d["b_Wv_t"]),
                             (w_o[:, :], d["b_Wo_t"]), (ident[:, :], d["ident"]), (causal32[:, :], d["causal"]),
                             (diag[:, :], d["diag"]), (beta[:, 0:1], d["b_beta"])):
                sp.dma_start(dst, src).then_inc(loaded, 16)
            sp.wait_ge(const_d, 16)

            def body(j, u):
                n, i = 2 * j + u, u

                def shift_rows(h2):
                    b, o = n - 1, 1 - i
                    sp.wait_ge(mt_d, 2 * b + h2 + 1)
                    apart(sp, spare)
                    sp.dma_start(m_dram[o, h2], mt[h2][:, :]).then_inc(mt_out, 16)
                    sp.wait_ge(mt_out, (2 * b + h2 + 1) * 16)
                    apart(sp, spare)
                    sp.dma_start(q_st[o][MROW:KROWS, h2 * H // 2:(h2 + 1) * H // 2, :],
                                 m_dram[o, h2].rearrange("(a h) t -> a h t", a=NPART)).then_inc(m_in[h2], 16)

                if active(j, u, 0):
                    at = pair(j, u, 0)
                    sp.wait_ge(x_in, n * 16)
                    apart(sp, spare)
                    if later(j, n, 2):
                        sp.wait_ge(z_d, (n - 1) * NT)
                        apart(sp, spare)
                    sp.dma_start(x[i][:, :, :], x_dram[at[0], at[1]]).then_inc(x_in, 16)
                if active(j, u, 2):
                    at = pair(j, u, 2)
                    sp.wait_ge(xt_in, (n - 2) * 16)
                    apart(sp, spare)
                    sp.wait_ge(wc_in, (n - 2) * 16)
                    apart(sp, spare)
                    if later(j, n, 4):
                        sp.wait_ge(x3_d, n - 3)
                        apart(sp, spare)
                        sp.wait_ge(g_p, n - 3)
                        apart(sp, spare)
                        sp.wait_ge(xb_d, n - 3)
                        apart(sp, spare)
                    sp.dma_start(xt[i][:, :, :], x_dram[at[0], at[1]]).then_inc(xt_in, 16)
                    sp.dma_start(wc[i][:, :, :].rearrange("p a f -> p (a f)"), wc_dram[at[0]]).then_inc(wc_in, 16)
                if active(j, u, 1):
                    shift_rows(0)
                if active(j, u, 0):
                    sp.wait_ge(split_d, (n + 1) * SPLIT)
                    apart(sp, spare)
                    sp.dma_start(parts_dram[i].rearrange("c p t -> p c t"),
                                 parts[i][:, :, :, :].rearrange("p q c t -> p (q c) t")).then_inc(parts_out, 16)
                if active(j, u, 3):
                    at = pair(j, u, 3)
                    sp.wait_ge(x4_d, n - 2)
                    apart(sp, spare)
                    sp.wait_ge(x4_out, (n - 3) * 16)
                    apart(sp, spare)
                    sp.dma_start(out_dram[at[0], at[1]], x4[1 - i][:, :, :]).then_inc(x4_out, 16)
                if active(j, u, 0):
                    sp.wait_ge(parts_out, (n + 1) * 16)
                    apart(sp, spare)
                    if later(j, n, 2):
                        sp.wait_ge(shifted, (n - 1) * ST)
                        apart(sp, spare)
                    for a in range(NPART):
                        sp.dma_start(q_st[i][a * NPART * HD:(a + 1) * NPART * HD, :, :],
                                     parts_dram[i, NPART + a].rearrange("(d h) t -> d h t", d=HD).unsqueeze(0)
                                     .broadcast_to([NPART, HD, H, T])).then_inc(stack_in, 16)
                    sp.dma_start(k_st[i][0:SROWS, :, :],
                                 parts_dram[i, 0:NPART].rearrange("c (d h) t -> (c d) h t", d=HD)
                                 .unsqueeze(0).broadcast_to([NPART, NPART * HD, H, T])).then_inc(stack_in, 16)
                if active(j, u, 1):
                    shift_rows(1)

            pipeline(sp, body)
            sp.wait_ge(x4_out, NB * 16)

        @block.gpsimd
        def _(pool):
            def const(k, ins):
                ins.then_inc(const_d, 1)
                pool.wait_ge(const_d, k)

            const(1, pool.memset(half[:, :], -0.5))
            for i in range(2):
                const(2 + 6 * i, pool.memset(k_st[i][64:P, :, :], 0.0))
                const(3 + 6 * i, pool.memset(k_st[i][MROW:P, :, :], 1.0))
                const(4 + 6 * i, pool.memset(vb[i][:, :, :], 0.0))
                const(5 + 6 * i, pool.memset(vb[i][:, :, 0:VW].rearrange("p i (h e) -> p i h e", h=H)[:, :, :, HD:],
                                             1.0))
                const(6 + 6 * i, pool.memset(uv[i][:, :, :], 0.0))
                const(7 + 6 * i, pool.memset(uv[i][0:SEG, :, HV:MW], 1.0))
            const(14, pool.memset(skn[:, :, :], 0.0))
            for i in range(2):
                const(15 + i, pool.memset(q_st[i][64:MROW, :, :], 0.0))

            def norm(k, b):
                pool.wait_ge(mv_d[k], (b + 1) * NT)
                apart(pool, spare)
                pool.tensor_scalar(var[k][:, :], mv[k][:, :, 1], EPS, 1.0, ALU.add, ALU.mult).then_inc(norm_d[k], 1)
                pool.wait_ge(norm_d[k], 2 * b + 1)
                pool.tensor_tensor(rs[k][:, :], var[k][:, :], half[:, :], ALU.pow).then_inc(norm_d[k], 1)

            def body(j, u):
                n, i = 2 * j + u, u
                if active(j, u, 0):
                    if later(j, n, 1):
                        pool.wait_ge(z_d, n * NT)
                    norm(0, n)
                if active(j, u, 3):
                    b = n - 3
                    if later(j, b, 1):
                        pool.wait_ge(z4_d, b * NT)
                    norm(1, b)
                    pool.wait_ge(wc_in, (b + 1) * 16)
                    pool.wait_ge(x3_d, b + 1)
                    if later(j, b, 2):
                        pool.wait_ge(x4_d, b - 1)
                    pool.tensor_tensor(xb[1 - i][:, :, :], x3[1 - i][:, :, :],
                                       wc[1 - i][:, 1, :].unsqueeze(1).broadcast_to([P, NT, P]), ALU.add
                                       ).then_inc(xb_d, 1)
                if active(j, u, 0):
                    pool.wait_ge(kq_d, (n + 1) * 2)
                    if later(j, n, 2):
                        pool.wait_ge(parts_out, (n - 1) * 16)

                    def split(k, ins):
                        ins.then_inc(split_d, 1)
                        pool.wait_ge(split_d, n * SPLIT + k)
                        apart(pool, spare)

                    apart(pool, spare)
                    split(1, pool.tensor_copy(parts[i][:, :, 0, :], kq[i][:, :, :]))
                    split(2, pool.tensor_tensor(rest[:, :, :], kq[i][:, :, :], parts[i][:, :, 0, :], ALU.subtract))
                    split(3, pool.tensor_copy(parts[i][:, :, 1, :], rest[:, :, :]))
                    split(4, pool.tensor_tensor(parts[i][:, :, 2, :], rest[:, :, :], parts[i][:, :, 1, :],
                                                ALU.subtract))
                    pool.wait_ge(nexp_d, n + 1)
                    if later(j, n, 2):
                        pool.wait_ge(read_p, (n - 1) * 3)
                    pool.tensor_tensor(sg[i][:, :, :, :].rearrange("p s a t -> p a s t"),
                                       pos[:, :, :].rearrange("p a (s t) -> p a s t", s=NS),
                                       nexp[:, :, :].rearrange("p a (s t) -> p a s t", s=NS), ALU.add
                                       ).then_inc(sg_d, 1)

            pipeline(pool, body)

        @block.scalar
        def _(act):
            act.wait_ge(loaded, N_LOAD * 16)
            act.activation(bexp[:, :], beta[:, 0:1], ACT.Exp, scale=-1.0).then_inc(beta_d, 1)
            act.copy(ident16[:, :], ident[:, :]).then_inc(mask_d, 1)
            for m, dst in enumerate((causal, causal_t)):
                act.copy(dst[:, :].rearrange("p (c f) -> p c f", c=4),
                         causal32[:, m * P:(m + 1) * P].unsqueeze(1).broadcast_to([P, 4, P])).then_inc(mask_d, 1)
            act.wait_ge(beta_d, 4)
            act.wait_ge(const_d, 16)

            def body(j, u):
                n, i = 2 * j + u, u
                for s in range(ST):
                    lag, g = turn(s)
                    if active(j, u, lag):
                        b = n - lag
                        act.wait_ge(shifted, b * ST + g + 1)
                        if g >= 4 or later(j, b, 1):
                            act.wait_ge(pv, b * ST + g - 3)
                        act.activation(flat(prob[g % 4]), t_ps[g % 2][:, :],
                                       ACT.Exp).then_inc(exped, 1)
                    if s == 1 and active(j, u, 0):
                        act.wait_ge(zt_p, n + 1)
                        act.copy(zt[i][:, :], ps_b[:, 0:T]).then_inc(zt_d, 1)
                    if s == 1 and active(j, u, 1):
                        b = n - 1
                        act.wait_ge(sk_p, b + 1)
                        if later(j, b, 1):
                            act.wait_ge(mem_p, b * 3)
                        act.copy(skn[0:SEG, :, :].rearrange("p s f -> p (s f)"),
                                 ps_c[0:SEG, 0:(NS - 1) * P]).then_inc(sk_d, 1)
                    if s == 2 and active(j, u, 0):
                        act.wait_ge(kq_p, n + 1)
                        act.copy(kq[i][:, 0, :], ps_a[:, 0:T]).then_inc(kq_d, 1)
                        act.mul(kq[i][:, 1, :], ps_a[:, T:2 * T], HD ** -0.5).then_inc(kq_d, 1)
                    if s == 3 and active(j, u, 0):
                        act.wait_ge(vs_p, n + 1)
                        if later(j, n, 2):
                            act.wait_ge(mem_p, (n - 1) * 3)
                        act.copy(uv[i][0:SEG, :, 0:HV], ps_b[0:SEG, 0:(NS - 1) * P].rearrange("p (s f) -> p s f", f=P)
                                 ).then_inc(vs_d, 1)
                        act.wait_ge(pn_d, (n + 1) * 2)
                        if later(j, n, 1):
                            act.wait_ge(sg_d, n)
                        act.activation(nexp[:, :, :], neg[:, :, :], ACT.Exp).then_inc(nexp_d, 1)
                    for h2 in range(2):
                        if s == (4, 6)[h2] and active(j, u, 1):
                            b = n - 1
                            act.wait_ge(mt_p, 2 * b + h2 + 1)
                            if later(j, b, 1):
                                act.wait_ge(mt_out, (2 * b + h2 - 1) * 16)
                            act.copy(mt[h2][:, :], mt_ps).then_inc(mt_d, 1)
                    if s == 4 and active(j, u, 3):
                        b = n - 3
                        act.wait_ge(z4_p, b + 1)
                        act.copy(z4t[:, :], ps_b[:, 0:T]).then_inc(z4t_d, 1)
                    if s == 7 and active(j, u, 0):
                        act.wait_ge(v_p, n + 1)
                        if later(j, n, 2):
                            act.wait_ge(pv, (n - 1) * ST)
                        act.copy(vb[i][:, :, 0:VW].rearrange("p i (h e) -> p i h e", h=H)[:, :, :, 0:HD],
                                 ps_b[:, 0:T].rearrange("p (i h e) -> p i h e", i=NT, h=H)).then_inc(v_d, 1)
                    if s == 7 and active(j, u, 2):
                        b = n - 2
                        act.wait_ge(at_p, b + 1)
                        if later(j, b, 1):
                            act.wait_ge(wo_p, b)
                        act.activation(at_b[:, :], ps_a[:, 0:T], ACT.Copy, scale=beta[:, 3:4]).then_inc(at_d, 1)

            pipeline(act, body)

        @block.tensor
        def _(pe):
            pe.wait_ge(loaded, N_LOAD * 16)
            pe.wait_ge(const_d, 16)
            pe.wait_ge(mask_d, 3)

            def body(j, u):
                n, i = 2 * j + u, u
                o = 1 - i
                for s in range(ST):
                    lag, g = turn(s)
                    if active(j, u, lag):
                        b, st = n - lag, (i + lag) % 2
                        if g % (ST // 2) == 0:
                            pe.wait_ge(m_in[g // (ST // 2)], (b + 1) * 16)
                        if g >= 2 or later(j, b, 1):
                            pe.wait_ge(exped, b * ST + g - 1)
                        pe.matmul(t_ps[g % 2][:, :], ident16[:, :], causal_t[:, :], start=True, stop=True)
                        for hh in range(2):
                            for t in range(NT):
                                at = (hh * NT + t) * P
                                ts = slice(t * P, (t + 1) * P)
                                mm = pe.matmul(t_ps[g % 2][:, at:at + P], k_st[st][0:KROWS, 2 * g + hh, ts],
                                               q_st[st][0:KROWS, 2 * g + hh, ts], start=False,
                                               stop=True, skip_group_check=True)
                        mm.then_inc(shifted, 1)
                    if S0 <= s < S0 + 4 and active(j, u, 1):
                        b = n - 1
                        if s == S0:
                            pe.wait_ge(stack_in, (b + 1) * 64)
                        for t in range(NT):
                            w = 2 * (s - S0) + t
                            ts = slice(t * P, (t + 1) * P)
                            if w >= 2 or later(j, b, 1):
                                pe.wait_ge(maxed, b * ST + w - 1)
                            pe.matmul(s_ps[t][:, :], ident16[:, :], causal[:, :], start=True, stop=True)
                            for c in range(4):
                                h = 4 * (s - S0) + c
                                mm = pe.matmul(s_ps[t][:, c * P:(c + 1) * P], q_st[o][0:MROW, h, ts],
                                               k_st[o][0:MROW, h, ts], start=False, stop=True,
                                               skip_group_check=True)
                            mm.then_inc(score, 1)
                    if s == 0 and active(j, u, 1):
                        b = n - 1
                        pe.wait_ge(sg_d, b + 1)
                        if later(j, b, 1):
                            pe.wait_ge(read_d, b * 9)
                        apart(pe, spare)
                        for c in range(NS - 1):
                            mm = pe.transpose(ps_c[0:SEG, c * P:(c + 1) * P], sg[o][:, c, 0, :], ident[:, :])
                        mm.then_inc(sk_p, 1)
                    if s == 0 and active(j, u, 3):
                        b = n - 3
                        pe.wait_ge(at_d, 2 * (b + 1))
                        free(pe, USES_B, 0, j, u)
                        for t in range(NT):
                            mm = pe.matmul(ps_b[:, t * P:(t + 1) * P], at_b[:, t * P:(t + 1) * P], w_o[:, :],
                                           start=True, stop=True)
                        mm.then_inc(wo_p, 1)
                    if s == 1 and active(j, u, 0):
                        pe.wait_ge(z_d, (n + 1) * NT)
                        free(pe, USES_B, 1, j, u)
                        for t in range(NT):
                            mm = pe.transpose(ps_b[:, t * P:(t + 1) * P], z[i][:, t, :], ident[:, :])
                        mm.then_inc(zt_p, 1)
                    if s in (1, 3, 5) and active(j, u, 1):
                        b, c = n - 1, s // 2
                        if c == 0:
                            pe.wait_ge(sk_d, b + 1)
                            pe.wait_ge(vs_d, b + 1)
                        else:
                            pe.wait_ge(u_d, b * 2 + c)
                        pe.matmul(ps_c[:, 0:MW], skn[:, c, :], uv[o][:, c, :], start=True, stop=True
                                  ).then_inc(mem_p, 1)
                    if s in (2, 4, 6) and active(j, u, 1):
                        b, c = n - 1, s // 2 - 1
                        pe.wait_ge(mz_d, b * 5 + 2 * c + 1)
                        pe.matmul(ps_c[:, 0:MW], sg[o][:, c + 1, :, :].rearrange("p a t -> p (a t)"), mz[:, :],
                                  start=True, stop=True).then_inc(read_p, 1)
                    if s == 2 and active(j, u, 0):
                        pe.wait_ge(zt_d, n + 1)
                        free(pe, USES_A, 0, j, u)
                        if later(j, n, 1):
                            pe.wait_ge(pn_d, n * 2)
                        pe.matmul(ps_a[:, 0:T], w_kq[:, 0, :], zt[i][:, :], start=True, stop=True)
                        pe.matmul(ps_a[:, T:2 * T], w_kq[:, 1, :], zt[i][:, :], start=True, stop=True
                                  ).then_inc(kq_p, 1)
                    if s == 3 and active(j, u, 0):
                        free(pe, USES_B, 2, j, u)
                        for c in range(NS - 1):
                            mm = pe.matmul(ps_b[0:SEG, c * P:(c + 1) * P], zt[i][:, c * SEG:(c + 1) * SEG], w_v[:, :],
                                           start=True, stop=True)
                        mm.then_inc(vs_p, 1)
                    for h2 in range(2):
                        if s == (4, 6)[h2] and active(j, u, 1):
                            b = n - 1
                            pe.wait_ge(mp_d, b * MP + 4 * (h2 + 1))
                            if h2:
                                pe.wait_ge(mt_d, 2 * b + 1)
                            else:
                                free(pe, USES_A, 1, j, u)
                                pe.wait_ge(pn_d, 2 * min(n + 1, NB) if isinstance(j, int) else 2 * (n + 1))
                            for t in range(NT):
                                mm = pe.transpose(mt_ps[:, t * P:(t + 1) * P],
                                                  mpart[:, t, h2, :, :].rearrange("p a h -> p (a h)"), ident16[:, :])
                            mm.then_inc(mt_p, 1)
                    if s == 4 and active(j, u, 3):
                        b = n - 3
                        pe.wait_ge(z4_d, (b + 1) * NT)
                        free(pe, USES_B, 3, j, u)
                        for t in range(NT):
                            mm = pe.transpose(ps_b[:, t * P:(t + 1) * P], z4[:, t, :], ident[:, :])
                        mm.then_inc(z4_p, 1)
                    if s == 5 and active(j, u, 3):
                        b = n - 3
                        pe.wait_ge(wc_in, (b + 1) * 16)
                        pe.wait_ge(z4t_d, b + 1)
                        free(pe, USES_B, 4, j, u)
                        for t in range(NT):
                            mm = pe.matmul(ps_b[:, t * P:(t + 1) * P], z4t[:, t * P:(t + 1) * P], wc[o][:, 0, :],
                                           start=True, stop=True)
                        mm.then_inc(g_p, 1)
                    lag, g = before(lag, g)
                    if active(j, u, lag):
                        b, st = n - lag, (i + lag) % 2
                        pe.wait_ge(exped, b * ST + g + 1)
                        if g == 0:
                            pe.wait_ge(v_d, b + 1)
                            if later(j, b, 1):
                                pe.wait_ge(ad_d, b * 2)
                        for t in range(NT):
                            for hh in range(2):
                                at = (2 * g + hh) * (HD + 1)
                                mm = pe.matmul(o_ps[:, t * 256 + at:t * 256 + at + WIN],
                                               prob[g % 4][:, hh, t * P:(t + 1) * P],
                                               vb[st][:, t, at:at + WIN], start=True, stop=True)
                        mm.then_inc(pv, 1)
                    if s == 7 and active(j, u, 0):
                        free(pe, USES_B, 5, j, u)
                        for t in range(NT):
                            mm = pe.matmul(ps_b[:, t * P:(t + 1) * P], zt[i][:, t * P:(t + 1) * P], w_v[:, :],
                                           start=True, stop=True)
                        mm.then_inc(v_p, 1)
                    if s == 7 and active(j, u, 2):
                        b = n - 2
                        pe.wait_ge(ad_d, (b + 1) * 2)
                        pe.wait_ge(read_d, (b + 1) * 9)
                        free(pe, USES_A, 2, j, u)
                        for t in range(NT):
                            pe.transpose(ps_a[:, t * P:(t + 1) * P], ad[:, t, :], ident[:, :])
                        for c in range(NS - 1):
                            at = T + (c + 1) * SEG
                            mm = pe.transpose(ps_a[:, at:at + SEG], am[i][SEG:P, c, :], ident[SEG:P, SEG:P])
                        mm.then_inc(at_p, 1)

            pipeline(pe, body)

        @block.vector
        def _(dve):
            dve.wait_ge(loaded, N_LOAD * 16)

            def link0(k, ins):
                ins.then_inc(beta_d, 1)
                dve.wait_ge(beta_d, k)

            dve.wait_ge(beta_d, 1)
            link0(2, dve.tensor_scalar(beta[:, 1:2], bexp[:, :], 1.0, None, ALU.add))
            link0(3, dve.reciprocal(beta[:, 2:3], beta[:, 1:2]))
            link0(4, dve.tensor_tensor(beta[:, 3:4], bexp[:, :], beta[:, 2:3], ALU.mult))

            def moments(k, b, src):
                for t in range(NT):
                    dve.bn_stats(stats[k][:, t, :], src[:, t, :]).then_inc(stat_d[k], 1)
                for t in range(NT):
                    dve.wait_ge(stat_d[k], b * NT + t + 1)
                    apart(dve, spare)
                    dve.bn_aggr(mv[k][:, t, :], stats[k][:, t, :]).then_inc(mv_d[k], 1)

            def normed(k, b, src, dst, done):
                dve.wait_ge(norm_d[k], 2 * (b + 1))
                for t in range(NT):
                    dve.tensor_scalar(dst[:, t, :], src[:, t, :], mv[k][:, t, 0:1], rs[k][:, t:t + 1],
                                      ALU.subtract, ALU.mult).then_inc(done, 1)

            def body(j, u):
                n, i = 2 * j + u, u
                o = 1 - i

                def split_max(h2):
                    b = n - 1
                    hs = slice(h2 * H // 2, (h2 + 1) * H // 2)
                    dve.wait_ge(maxed, b * ST + 4 * (h2 + 1))
                    if later(j, b, 1):
                        dve.wait_ge(mt_p, 2 * (b - 1) + h2 + 1)

                    def link(k, ins):
                        ins.then_inc(mp_d, 1)
                        dve.wait_ge(mp_d, b * MP + 4 * h2 + k)

                    link(1, dve.tensor_copy(mpart[:, :, h2, 0, :], nmax[:, :, hs]))
                    link(2, dve.tensor_tensor(nrest[:, :, hs], nmax[:, :, hs], mpart[:, :, h2, 0, :], ALU.subtract))
                    link(3, dve.tensor_copy(mpart[:, :, h2, 1, :], nrest[:, :, hs]))
                    link(4, dve.tensor_tensor(mpart[:, :, h2, 2, :], nrest[:, :, hs], mpart[:, :, h2, 1, :],
                                              ALU.subtract))

                for s in range(ST):
                    if s == 0 and active(j, u, 0):
                        dve.wait_ge(x_in, (n + 1) * 16)
                        if later(j, n, 1):
                            dve.wait_ge(norm_d[0], 2 * n)
                        moments(0, n, x[i])
                    if s == 0 and active(j, u, 3):
                        b = n - 3
                        dve.wait_ge(wo_p, b + 1)
                        dve.wait_ge(xt_in, (b + 1) * 16)
                        if later(j, b, 2):
                            dve.wait_ge(xb_d, b - 1)
                        dve.tensor_tensor(flat(x3[o]), ps_b[:, 0:T], flat(xt[o]), ALU.add).then_inc(x3_d, 1)
                        dve.wait_ge(x3_d, b + 1)
                        if later(j, b, 1):
                            dve.wait_ge(norm_d[1], 2 * b)
                        moments(1, b, x3[o])
                    if s == 1 and active(j, u, 0):
                        if later(j, n, 2):
                            dve.wait_ge(zt_p, n - 1)
                        normed(0, n, x[i], z[i], z_d)
                    if s in (1, 3, 5) and active(j, u, 1):
                        b, c = n - 1, s // 2
                        dve.wait_ge(mem_p, b * 3 + c + 1)
                        if c == 0:
                            if later(j, b, 1):
                                dve.wait_ge(read_p, b * 3)
                            dve.tensor_tensor(mz[:, :], ps_c[:, 0:MW], diag[:, :], ALU.mult).then_inc(mz_d, 1)
                        else:
                            dve.tensor_tensor(mzt[:, :], ps_c[:, 0:MW], diag[:, :], ALU.mult).then_inc(mz_d, 1)
                            dve.wait_ge(mz_d, b * 5 + 2 * c)
                            dve.wait_ge(read_p, b * 3 + c)
                            dve.tensor_tensor(mz[:, :], mz[:, :], mzt[:, :], ALU.add).then_inc(mz_d, 1)
                    if S0 <= s < S0 + 4 and active(j, u, 1):
                        b = n - 1
                        for t in range(NT):
                            w = 2 * (s - S0) + t
                            dve.wait_ge(score, b * ST + w + 1)
                            if w == 0 and later(j, b, 1):
                                dve.wait_ge(mp_d, b * MP)
                            dve.tensor_reduce(nmax[:, t, 4 * (s - S0):4 * (s - S0) + 4],
                                              s_ps[t][:, :].rearrange("p (h k) -> p h k", h=4), AX.X, ALU.max,
                                              negate=True).then_inc(maxed, 1)
                    if s in (2, 4, 6) and active(j, u, 1):
                        b, c = n - 1, s // 2 - 1
                        dve.wait_ge(read_p, b * 3 + c + 1)
                        if c == 0 and later(j, b, 2):
                            dve.wait_ge(at_p, b - 1)

                        def link(k, ins):
                            ins.then_inc(read_d, 1)
                            dve.wait_ge(read_d, b * 9 + 3 * c + k)

                        link(1, dve.tensor_scalar(dn[:, c, :], ps_c[:, HV:MW], 1e-6, None, ALU.add))
                        link(2, dve.reciprocal(dr[:, c, :], dn[:, c, :]))
                        link(3, dve.tensor_tensor(am[o][:, c, :].rearrange("p (h e) -> p h e", h=H),
                                                  ps_c[:, 0:HV].rearrange("p (h e) -> p h e", h=H),
                                                  dr[:, c, :].unsqueeze(2).broadcast_to([P, H, HD]), ALU.mult))
                        if c < 2:
                            dve.tensor_tensor(uv[o][0:SEG, c + 1, 0:HV], uv[o][0:SEG, c + 1, 0:HV],
                                              am[o][0:SEG, c, :], ALU.subtract).then_inc(u_d, 1)
                    if s == 2 and active(j, u, 0):
                        dve.wait_ge(kq_d, (n + 1) * 2)
                        if later(j, n, 1):
                            dve.wait_ge(sg_d, n)
                        dve.tensor_scalar(flat(pos), ps_a[:, :], 0.0, None, ALU.max).then_inc(pn_d, 1)
                        dve.tensor_scalar(flat(neg), ps_a[:, :], 0.0, None, ALU.min).then_inc(pn_d, 1)
                    if s in (3, 5) and active(j, u, 1):
                        split_max(s // 2 - 1)
                    if s == 3 and active(j, u, 3):
                        b = n - 3
                        if later(j, b, 1):
                            dve.wait_ge(z4_p, b)
                        normed(1, b, x3[o], z4, z4_d)
                    if s == 5 and active(j, u, 3):
                        b = n - 3
                        dve.wait_ge(g_p, b + 1)
                        dve.wait_ge(xb_d, b + 1)
                        if later(j, b, 2):
                            dve.wait_ge(x4_out, (b - 1) * 16)
                        dve.tensor_tensor(flat(x4[o]), ps_b[:, 0:T], flat(xb[o]), ALU.add).then_inc(x4_d, 1)
                    if s == 6 and active(j, u, 2):
                        b = n - 2
                        dve.wait_ge(pv, (b + 1) * ST)
                        if later(j, b, 1):
                            dve.wait_ge(at_p, b)
                        out = o_ps[:, :].rearrange("p (i c) -> p i c", i=NT)[:, :, 0:VW].rearrange(
                            "p i (h e) -> p i h e", h=H)
                        dve.reciprocal(dinv[:, :, :], out[:, :, :, HD]).then_inc(ad_d, 1)
                        dve.wait_ge(ad_d, 2 * b + 1)
                        dve.tensor_tensor(ad[:, :, :].rearrange("p i (h e) -> p i h e", h=H), out[:, :, :, 0:HD],
                                          dinv[:, :, :].unsqueeze(3).broadcast_to([P, NT, H, HD]), ALU.mult
                                          ).then_inc(ad_d, 1)
                    if s == 7 and active(j, u, 2):
                        b = n - 2
                        dve.wait_ge(at_d, 2 * b + 1)
                        dve.scalar_tensor_tensor(at_b[:, SEG:T], ps_a[:, T + SEG:2 * T], beta[:, 2:3],
                                                 at_b[:, SEG:T], ALU.mult, ALU.add).then_inc(at_d, 1)

            pipeline(dve, body)


def program(nc, d):
    attention_a(nc, d)
    fold_ffn(nc, d)
    dense(nc, d)
    attention_b(nc, d)


def laid_out(I):
    import numpy as np

    a = lambda k: np.asarray(I[f"L0_attn_a_{k}"])
    b = lambda k: np.asarray(I[f"L0_attn_b_{k}"])
    f = lambda k: np.asarray(I[f"L0_ffn_{k}"])
    on_rows = lambda v: np.broadcast_to(v, (P, v.shape[0]))
    dh = np.arange(P).reshape(H, HD).T.ravel()
    ws = a("Ws")[0]
    sel_qv = np.zeros((H, QK, H), np.float32)
    sel_v = np.zeros((R, HD, R), np.float32)
    for h in range(H):
        sel_qv[h, :, h] = ws[:QK]
    for r in range(R):
        sel_v[r, :, r] = ws[QK:]
    t = np.arange(P)
    seen = (t[:, None] // 64 == t[None] // 64) & (t[None] <= t[:, None])
    causal = np.where(seen, 0.0, -2.0 ** 100).astype(np.float32)
    diag = np.concatenate([(t % H)[:, None] == (t // HD)[None], (t % H)[:, None] == np.arange(H)[None]], 1)
    out = {
        "x": a("x"),
        "a_Wq": a("Wq")[dh].T, "a_Wk": a("Wk")[dh].T, "a_Wv_t": a("Wv").T, "a_Wv": a("Wv"), "a_Wqv": a("Wqv"),
        "a_bv_b": on_rows(a("bv")), "a_bv_r": np.broadcast_to(a("bv")[:, None], (RD, P)),
        "a_bqv_b": np.broadcast_to(a("bqv")[:, None], (QK * H, P)),
        "a_sel_qv": sel_qv.reshape(QK * H, H), "a_sel_v": sel_v.reshape(RD, R),
        "a_cols": np.stack([a("bq")[dh], a("bk")[dh], a("g1"), a("b1"), np.broadcast_to(a("bs"), P)], 1),
        "a_Wf_t": a("Wf").T, "a_Wr1_t": a("Wr1").T, "a_Wr2_t": a("Wr2").T,
        "a_bf_b": on_rows(a("bf")), "a_br2_b": on_rows(a("br2")),
        "b_cols": np.stack([a("br1")[:P], a("br1")[P:], a("g2"), a("b2")], 1),
        "W1": f("W1"), "W2_t": f("W2").transpose(0, 2, 1),
        "ffn_b": np.concatenate([f("b1").reshape(NG, NI, P).transpose(0, 2, 1), f("b2")[:, :, None]], 2),
        "b_Wkq_t": np.concatenate([b("W_k")[dh].T, b("W_q")[dh].T], 1),
        "b_Wv_t": b("W_v").T, "b_Wo_t": b("W_o").T, "b_beta": np.repeat(b("beta_param"), HD)[:, None],
        "ident": np.eye(P, dtype=np.float32),
        "causal": np.concatenate([causal, causal.T], 1),
        "diag": diag.astype(np.float32),
    }
    return {k: np.ascontiguousarray(v) for k, v in out.items()}


SCRATCH = {
    "a_parts_dram": ((2, 2 * NPART, P, T), BF16), "a_m_dram": ((2, 2, NPART * H // 2, T), BF16),
    "c_parts_dram": ((2, 2 * NPART, P, T), BF16), "c_m_dram": ((2, 2, NPART * H // 2, T), BF16),
    "y": ((NB, T, P), F32), "ao": ((NB, T, P), F32), "x2": ((NB, T, P), F32),
    "folded": ((NB // 2, P, 2 * P), F32),
}


def kernel(**inputs):
    import numpy as np
    import concourse.bacc as bacc
    from concourse.bass_utils import run_bass_kernel_spmd

    nc = bacc.Bacc("TRN2", target_bir_lowering=False, num_devices=1)
    arrays, d = {}, {}
    for name, a in laid_out(inputs).items():
        arrays[f"in_{name}"] = a
        d[name] = nc.dram_tensor(f"in_{name}", a.shape, mybir.dt.from_np(a.dtype), kind="ExternalInput").ap()
    for name, (shape, dt) in SCRATCH.items():
        d[name] = nc.dram_tensor(f"scratch_{name}", shape, dt, kind="Internal").ap()
    d["out"] = nc.dram_tensor("out", (NB, T, P), F32, kind="ExternalOutput").ap()
    program(nc, d)
    return run_bass_kernel_spmd(nc, [arrays], core_ids=[0]).results[0]["out"]
```

```python
import concourse.bass as bass
import concourse.mybir as mybir
from contextlib import ExitStack

F32 = mybir.dt.float32
BF16 = mybir.dt.bfloat16
ALU = mybir.AluOpType
ACT = mybir.ActivationFunctionType
AX = mybir.AxisListType

P = 128
NB, T = 32, 256
NT = T // P
H, HD, R, QK = 16, 8, 8, 32
RD = R * HD
NPART = 3
SROWS = NPART * NPART * HD
MROW = 96
KROWS = MROW + NPART
VC = 96
CV, CC, CS, CQ = 0, RD, RD + R, RD + R + 1
EPS = 1e-5
NG, NI = 8, 4
LAGS = 4
PEELED = 6


def active(j, u, lag, total=NB):
    return not isinstance(j, int) or 0 <= 2 * j + u - lag < total


def pair(j, u, lag):
    return j + (u - lag) // 2, (u - lag) % 2


def pipeline(eng, body, total=NB, stages=LAGS, ahead=0):
    for n in range(-ahead, PEELED):
        body(n // 2, n % 2)
    end = total // 2 - ahead
    with eng.Fori(PEELED // 2, end) as j:
        body(j, 0)
        body(j, 1)
    for n in range(2 * end, total + stages - 1):
        body(n // 2, n % 2)


def apart(eng, spare):
    eng.sem_inc(spare, 1)


def memory(nc, ctx, prefix):
    def sb(name, shape, dt=F32):
        return ctx.enter_context(nc.sbuf_tensor(f"{prefix}_{name}", shape, dt))

    def sem(name):
        return ctx.enter_context(nc.semaphore(f"{prefix}_{name}"))

    return sb, sem


def attention_a(nc, d):
    ctx = ExitStack()
    with ctx:
        def sb(name, shape, dt=F32):
            return ctx.enter_context(nc.sbuf_tensor(name, shape, dt))

        def sem(name):
            return ctx.enter_context(nc.semaphore(name))

        w_q = sb("a_w_q", [P, P])
        w_k = sb("a_w_k", [P, P])
        w_v = sb("a_w_v", [P, VC])
        b_v = sb("a_b_v", [P, VC])
        w_qv = sb("a_w_qv", [P, 4, P])
        w_vn = sb("a_w_vn", [RD, P])
        s_qv = sb("a_s_qv", [P, 4, H])
        s_v = sb("a_s_v", [RD, R])
        b_qv = sb("a_b_qv", [P, 4, P])
        b_vr = sb("a_b_vr", [RD, P])
        cols = sb("a_cols", [P, 5])
        b_qs = sb("a_b_qs", [P, 1])
        ident = sb("a_ident", [P, P])
        ident16 = sb("a_ident16", [P, P], BF16)
        half = sb("a_half", [P, NT])
        x = [sb(f"a_x{i}", [P, NT, P]) for i in range(2)]
        y = [sb(f"a_y{i}", [P, NT, P]) for i in range(2)]
        z = [sb(f"a_z{i}", [P, NT, P]) for i in range(2)]
        stats = sb("a_stats", [P, NT, 6])
        mv = sb("a_mv", [P, NT, 2])
        r1 = sb("a_r1", [P, NT])
        r2 = sb("a_r2", [P, NT])
        rt = sb("a_rt", [P, 4, NT])
        xn = [sb(f"a_xn{i}", [P, T]) for i in range(2)]
        qk = [sb(f"a_qk{i}", [P, 2, T]) for i in range(2)]
        rest = sb("a_rest", [P, 2, T])
        parts = [sb(f"a_parts{i}", [P, 2, NPART, T], BF16) for i in range(2)]
        q_st = [sb(f"a_q_st{i}", [P, H, T], BF16) for i in range(2)]
        k_st = [sb(f"a_k_st{i}", [P, H, T], BF16) for i in range(2)]
        vp = [sb(f"a_vp{i}", [P, NT, VC]) for i in range(2)]
        nmax = sb("a_nmax", [P, NT, H])
        nrest = sb("a_nrest", [P, NT, H])
        mpart = sb("a_mpart", [P, NT, 2, NPART, H // 2], BF16)
        mt = [sb(f"a_mt{i}", [NPART * H // 2, T], BF16) for i in range(2)]
        prob = [sb(f"a_prob{i}", [P, NT, T]) for i in range(4)]
        ov = [sb(f"a_ov{i}", [P, H * NT, RD + R + 1]) for i in range(2)]
        inv = sb("a_inv", [P, H * NT])
        comp = sb("a_comp", [P, H * NT, R])
        comp2 = sb("a_comp2", [P, H * NT, R])
        cmax = sb("a_cmax", [P, H * NT])
        comp3 = sb("a_comp3", [P, H * NT, R])
        cexp = sb("a_cexp", [P, H * NT, R])
        csum = sb("a_csum", [P, H * NT])
        cinv = sb("a_cinv", [P, H * NT])
        cw = sb("a_cw", [P, H * NT])
        wgt = sb("a_wgt", [P, H * NT, R])
        prod = sb("a_prod", [P, H * NT, RD])
        ao = [sb(f"a_ao{i}", [P, NT, P]) for i in range(2)]
        bank = [ctx.enter_context(nc.psum_tensor(f"a_bank{i}", [P, 512], F32)) for i in range(8)]
        zv_ps, qk_ps, s_ps, t_ps, o_ps = bank[0], bank[1], bank[2:4], bank[4:6], bank[6:8]
        mt_ps = qk_ps[0:NPART * H // 2, 0:T // 2].bitcast(BF16)

        spare = sem("a_spare")
        loaded = sem("a_loaded")
        consts = sem("a_consts")
        blank = sem("a_blank")
        fold_p = sem("a_fold_p")
        folded = sem("a_folded")
        x_in = sem("a_x_in")
        stats_d = sem("a_stats_d")
        mv_d = sem("a_mv_d")
        norm_d = sem("a_norm_d")
        y_d = sem("a_y_d")
        z_d = sem("a_z_d")
        z_t = sem("a_z_t")
        xn_d = sem("a_xn_d")
        qk_p = sem("a_qk_p")
        qk_d = sem("a_qk_d")
        split_d = sem("a_split_d")
        parts_out = sem("a_parts_out")
        stack_in = [sem(f"a_stack_in{i}") for i in range(2)]
        v_p = sem("a_v_p")
        v_d = sem("a_v_d")
        score = sem("a_score")
        maxed = sem("a_maxed")
        mp_d = sem("a_mp_d")
        mt_p = sem("a_mt_p")
        mt_d = sem("a_mt_d")
        mt_out = sem("a_mt_out")
        m_in = [sem(f"a_m_in{i}") for i in range(2)]
        shifted = sem("a_shifted")
        exped = sem("a_exped")
        pv = sem("a_pv")
        ov_d = sem("a_ov_d")
        post = sem("a_post")
        cexp_d = sem("a_cexp_d")
        prod_d = sem("a_prod_d")
        ao_d = sem("a_ao_d")
        y_out = sem("a_y_out")
        ao_out = sem("a_ao_out")

        parts_dram = d["a_parts_dram"]
        m_dram = d["a_m_dram"]
        pairs = lambda a: a.rearrange("(j u) (i p) f -> j u p i f", u=2, p=P)
        x_dram, y_dram, ao_dram = pairs(d["x"]), pairs(d["y"]), pairs(d["ao"])
        SPLIT, NORM, MP, POST = 4, 7, 8, 9
        OFF = 11
        S_AT = (1, 2, 3, 4, 6, 7, 8, 9)
        MT_AT = (6, 11)
        N_LOAD = 12

        block = ctx.enter_context(nc.Block())

        @block.sync
        def _(sp):
            for dst, src in ((w_q[:, :], d["a_Wq"]), (w_k[:, :], d["a_Wk"]), (w_v[:, 0:RD], d["a_Wv_t"]),
                             (b_v[:, 0:RD], d["a_bv_b"]),
                             (w_qv[:, :, :], d["a_Wqv"].rearrange("(c p) f -> p c f", p=P)),
                             (w_vn[:, :], d["a_Wv"]),
                             (s_qv[:, :, :], d["a_sel_qv"].rearrange("(c p) f -> p c f", p=P)),
                             (s_v[:, :], d["a_sel_v"]),
                             (b_qv[:, :, :], d["a_bqv_b"].rearrange("(c p) f -> p c f", p=P)),
                             (b_vr[:, :], d["a_bv_r"]), (cols[:, :], d["a_cols"]),
                             (ident[:, :], d["ident"])):
                sp.dma_start(dst, src).then_inc(loaded, 16)
            sp.wait_ge(consts, 7)

            def body(j, u):
                n = 2 * j + u
                i = u
                if active(j, u, -1):
                    if not isinstance(j, int) or n >= 1:
                        sp.wait_ge(z_d, n * NT)
                        apart(sp, spare)
                    if not isinstance(j, int) or n >= 0:
                        sp.wait_ge(x_in, (n + 1) * 16)
                        apart(sp, spare)
                    at = pair(j, u, -1)
                    sp.dma_start(x[1 - i][:, :, :], x_dram[at[0], at[1]]).then_inc(x_in, 16)

                def shift_rows(half_):
                    b, o = n - 1, 1 - i
                    sp.wait_ge(mt_d, 2 * b + half_ + 1)
                    apart(sp, spare)
                    sp.dma_start(m_dram[o, half_], mt[half_][:, :]).then_inc(mt_out, 16)
                    sp.wait_ge(mt_out, (2 * b + half_ + 1) * 16)
                    apart(sp, spare)
                    hs = slice(half_ * H // 2, (half_ + 1) * H // 2)
                    sp.dma_start(q_st[o][MROW:KROWS, hs, :],
                                 m_dram[o, half_].rearrange("(a h) t -> a h t", a=NPART)).then_inc(m_in[half_], 16)

                if active(j, u, 0):
                    sp.wait_ge(y_d, (n + 1) * NT)
                    apart(sp, spare)
                    sp.wait_ge(y_out, n * 16)
                    apart(sp, spare)
                    at = pair(j, u, 0)
                    sp.dma_start(y_dram[at[0], at[1]], y[i][:, :, :]).then_inc(y_out, 16)
                if active(j, u, 1):
                    shift_rows(0)
                if active(j, u, 0):
                    sp.wait_ge(split_d, (n + 1) * SPLIT)
                    apart(sp, spare)
                    sp.dma_start(parts_dram[i].rearrange("c p t -> p c t"),
                                 parts[i][:, :, :, :].rearrange("p q c t -> p (q c) t")).then_inc(parts_out, 16)
                if active(j, u, 0):
                    sp.wait_ge(parts_out, (n + 1) * 16)
                    apart(sp, spare)
                    for half_ in range(2):
                        hs = slice(half_ * H // 2, (half_ + 1) * H // 2)
                        if not isinstance(j, int) or n >= 2:
                            sp.wait_ge(shifted, (n - 2) * H + (half_ + 1) * H // 2)
                            apart(sp, spare)
                        for a in range(NPART):
                            sp.dma_start(q_st[i][a * NPART * HD:(a + 1) * NPART * HD, hs, :],
                                         parts_dram[i, a].rearrange("(d h) t -> d h t", d=HD)[:, hs].unsqueeze(0)
                                         .broadcast_to([NPART, HD, H // 2, T])).then_inc(stack_in[half_], 16)
                        sp.dma_start(k_st[i][0:SROWS, hs, :],
                                     parts_dram[i, NPART:2 * NPART].rearrange("c (d h) t -> (c d) h t", d=HD)[:, hs]
                                     .unsqueeze(0).broadcast_to([NPART, NPART * HD, H // 2, T])
                                     ).then_inc(stack_in[half_], 16)
                if active(j, u, 1):
                    shift_rows(1)
                if active(j, u, 3):
                    at = pair(j, u, 3)
                    sp.wait_ge(ao_d, (n - 2) * NT)
                    apart(sp, spare)
                    sp.wait_ge(ao_out, (n - 3) * 16)
                    apart(sp, spare)
                    sp.dma_start(ao_dram[at[0], at[1]], ao[1 - i][:, :, :]).then_inc(ao_out, 16)

            pipeline(sp, body, ahead=1)
            sp.wait_ge(y_out, NB * 16)
            sp.wait_ge(ao_out, NB * 16)

        @block.gpsimd
        def _(pool):
            def const(k, ins):
                ins.then_inc(consts, 1)
                pool.wait_ge(consts, k)

            const(1, pool.memset(half[:, :], -0.5))
            for i in range(2):
                const(2 + 3 * i, pool.memset(k_st[i][64:P, :, :], 0.0))
                const(3 + 3 * i, pool.memset(k_st[i][MROW:P, :, :], 1.0))
                const(4 + 3 * i, pool.memset(q_st[i][64:MROW, :, :], 0.0))

            def body(j, u):
                n = 2 * j + u
                i = u
                if active(j, u, 3):
                    b, o = n - 3, 1 - i
                    pool.wait_ge(post, (b + 1) * POST)
                    if not isinstance(j, int) or n >= 4:
                        pool.wait_ge(ao_d, b * NT)
                    pool.tensor_tensor(
                        prod[:, :, :].rearrange("p g (r e) -> p g r e", r=R),
                        ov[o][:, :, 0:RD].rearrange("p g (r e) -> p g r e", r=R),
                        wgt[:, :, :].unsqueeze(3).broadcast_to([P, H * NT, R, HD]), ALU.mult).then_inc(prod_d, 1)
                if active(j, u, 0):
                    pool.wait_ge(qk_d, (n + 1) * 2)
                    if not isinstance(j, int) or n >= 2:
                        pool.wait_ge(parts_out, (n - 1) * 16)

                    def split(k, ins):
                        ins.then_inc(split_d, 1)
                        pool.wait_ge(split_d, n * SPLIT + k)
                        apart(pool, spare)

                    apart(pool, spare)
                    split(1, pool.tensor_scalar(parts[i][:, :, 0, :], qk[i][:, :, :], 1.0, 0.0, ALU.mult, ALU.add))
                    split(2, pool.tensor_tensor(rest[:, :, :], qk[i][:, :, :], parts[i][:, :, 0, :], ALU.subtract))
                    split(3, pool.tensor_scalar(parts[i][:, :, 1, :], rest[:, :, :], 1.0, 0.0, ALU.mult, ALU.add))
                    split(4, pool.tensor_tensor(parts[i][:, :, 2, :], rest[:, :, :], parts[i][:, :, 1, :],
                                                ALU.subtract))
                if active(j, u, -1):
                    pool.wait_ge(mv_d, (n + 2) * NT)
                    if not isinstance(j, int) or n >= 0:
                        pool.wait_ge(z_d, (n + 1) * NT)

                    def norm(k, ins):
                        ins.then_inc(norm_d, 1)
                        pool.wait_ge(norm_d, (n + 1) * NORM + k)
                        apart(pool, spare)

                    apart(pool, spare)
                    norm(1, pool.tensor_scalar(rt[:, 0, :], mv[:, :, 1], EPS, None, ALU.add))
                    norm(2, pool.tensor_tensor(r1[:, :], rt[:, 0, :], half[:, :], ALU.pow))
                    norm(3, pool.tensor_tensor(rt[:, 1, :], r1[:, :], r1[:, :], ALU.mult))
                    norm(4, pool.tensor_tensor(rt[:, 2, :], rt[:, 1, :], mv[:, :, 1], ALU.mult))
                    norm(5, pool.tensor_scalar(rt[:, 3, :], rt[:, 2, :], EPS, None, ALU.add))
                    norm(6, pool.tensor_tensor(rt[:, 1, :], rt[:, 3, :], half[:, :], ALU.pow))
                    norm(7, pool.tensor_tensor(r2[:, :], rt[:, 1, :], r1[:, :], ALU.mult))

            pipeline(pool, body, ahead=1)

        @block.scalar
        def _(act):
            act.wait_ge(loaded, N_LOAD * 16)
            act.mul(b_qs[:, :], cols[:, 0:1], HD ** -0.5).then_inc(folded, 1)
            act.copy(ident16[:, :], ident[:, :]).then_inc(folded, 1)
            act.wait_ge(fold_p, 1)
            act.wait_ge(blank, 3)
            act.copy(w_v[:, CC:CS], bank[0][:, 0:R]).then_inc(folded, 1)
            act.mul(w_v[:, CQ:CQ + H], bank[0][:, 16:16 + H], QK ** -0.5).then_inc(folded, 1)
            act.copy(b_v[:, CC:CS], bank[0][:, 32:32 + R]).then_inc(folded, 1)
            act.activation(b_v[:, CQ:CQ + H], bank[0][:, 48:48 + H], ACT.Identity, scale=QK ** -0.5,
                           bias=cols[:, 4:5]).then_inc(folded, 1)

            def body(j, u):
                n = 2 * j + u
                i = u
                for s in range(H):
                    if s == 2 and active(j, u, 0):
                        act.wait_ge(z_t, n + 1)
                        act.activation(xn[i][:, :], zv_ps[:, 0:T], ACT.Identity, scale=cols[:, 2:3],
                                       bias=cols[:, 3:4]).then_inc(xn_d, 1)
                    if s == 4 and active(j, u, 0):
                        act.wait_ge(qk_p, n + 1)
                        act.activation(qk[i][:, 0, :], qk_ps[:, 0:T], ACT.Identity, scale=HD ** -0.5,
                                       bias=b_qs[:, 0:1]).then_inc(qk_d, 1)
                        act.activation(qk[i][:, 1, :], qk_ps[:, T:2 * T], ACT.Identity,
                                       bias=cols[:, 1:2]).then_inc(qk_d, 1)
                    for half_ in range(2):
                        if s == MT_AT[half_] and active(j, u, 1):
                            b = n - 1
                            act.wait_ge(mt_p, 2 * b + half_ + 1)
                            if not isinstance(j, int) or b >= 1:
                                act.wait_ge(mt_out, (2 * b + half_ - 1) * 16)
                            act.copy(mt[half_][:, :], mt_ps).then_inc(mt_d, 1)
                    lag, h = (1, s - OFF) if s >= OFF else (2, s + H - OFF)
                    b = n - lag
                    if active(j, u, lag):
                        act.wait_ge(shifted, b * H + h + 1)
                        if h >= 4 or not isinstance(j, int) or b >= 1:
                            act.wait_ge(pv, b * H + h - 3)
                        act.activation(prob[h % 4][:, :, :].rearrange("p a b -> p (a b)"), t_ps[h % 2][:, :],
                                       ACT.Exp).then_inc(exped, 1)
                    lag, g = (lag, h // 2 - 1) if h >= 2 else (lag + 1, H // 2 - 1)
                    b = n - lag
                    if h % 2 == 0 and active(j, u, lag):
                        act.wait_ge(pv, b * H + 2 * g + 2)
                        if g == 0 and (not isinstance(j, int) or b >= 2):
                            act.wait_ge(prod_d, b - 1)
                        act.copy(ov[(i + lag) % 2][:, 4 * g:4 * g + 4, :],
                                 o_ps[g % 2][:, 0:4 * VC].rearrange("p (g c) -> p g c", g=4)[:, :, 0:CQ]
                                 ).then_inc(ov_d, 1)
                    if s == 15 and active(j, u, 2):
                        act.wait_ge(post, (n - 2) * POST + 5)
                        if not isinstance(j, int) or n >= 3:
                            act.wait_ge(post, (n - 2) * POST)
                        act.activation(cexp[:, :, :], comp3[:, :, :], ACT.Exp).then_inc(cexp_d, 1)

            pipeline(act, body, ahead=1)

        @block.tensor
        def _(pe):
            pe.wait_ge(loaded, N_LOAD * 16)
            pe.matmul(bank[0][:, 0:R], w_vn[:, :], s_v[:, :], start=True, stop=True)
            for c in range(4):
                pe.matmul(bank[0][:, 16:16 + H], w_qv[:, c, :], s_qv[:, c, :], start=c == 0, stop=c == 3)
            pe.matmul(bank[0][:, 32:32 + R], b_vr[:, :], s_v[:, :], start=True, stop=True)
            for c in range(4):
                mm = pe.matmul(bank[0][:, 48:48 + H], b_qv[:, c, :], s_qv[:, c, :], start=c == 0, stop=c == 3)
            mm.then_inc(fold_p, 1)
            pe.wait_ge(folded, 6)
            pe.wait_ge(consts, 7)

            def body(j, u):
                n = 2 * j + u
                i = u

                def score_unit(s, t):
                    if s in S_AT and active(j, u, 1):
                        b, o, g = n - 1, 1 - i, S_AT.index(s)
                        if g % (H // 4) == 0 and t == 0:
                            pe.wait_ge(stack_in[g // (H // 4)], (b + 1) * 4 * 16)
                        w = 2 * g + t
                        if w >= 2 or not isinstance(j, int) or b >= 1:
                            pe.wait_ge(maxed, b * H + w - 1)
                        for hh in range(2):
                            mm = pe.matmul(s_ps[t][:, hh * T:(hh + 1) * T],
                                           q_st[o][0:MROW, 2 * g + hh, t * P:(t + 1) * P],
                                           k_st[o][0:MROW, 2 * g + hh, :], start=True, stop=True)
                        mm.then_inc(score, 1)

                for s in range(H):
                    if s == 1 and active(j, u, 0):
                        pe.wait_ge(z_d, (n + 1) * NT)
                        if not isinstance(j, int) or n >= 1:
                            pe.wait_ge(v_d, n)
                        for t in range(NT):
                            mm = pe.transpose(zv_ps[:, t * P:(t + 1) * P], z[i][:, t, :], ident[:, :])
                        mm.then_inc(z_t, 1)
                    if s == 3 and active(j, u, 0):
                        pe.wait_ge(xn_d, n + 1)
                        if not isinstance(j, int) or n >= 2:
                            pe.wait_ge(mt_d, 2 * (n - 1))
                        pe.matmul(qk_ps[:, 0:T], w_q[:, :], xn[i][:, :], start=True, stop=True)
                        pe.matmul(qk_ps[:, T:2 * T], w_k[:, :], xn[i][:, :], start=True, stop=True).then_inc(qk_p, 1)
                    if s == 10 and active(j, u, 0):
                        for t in range(NT):
                            mm = pe.matmul(zv_ps[:, t * VC:(t + 1) * VC], xn[i][:, t * P:(t + 1) * P], w_v[:, :],
                                           start=True, stop=True)
                        mm.then_inc(v_p, 1)
                    score_unit(s, 0)
                    for half_ in range(2):
                        if s == MT_AT[half_] and active(j, u, 1):
                            b = n - 1
                            pe.wait_ge(mp_d, b * MP + 4 * (half_ + 1))
                            pe.wait_ge(qk_d, min(n + 1, NB) * 2 if isinstance(j, int) else (n + 1) * 2)
                            if half_ or not isinstance(j, int) or b >= 1:
                                pe.wait_ge(mt_d, 2 * b + half_)
                            for t in range(NT):
                                mm = pe.transpose(mt_ps[:, t * P:(t + 1) * P],
                                                  mpart[:, t, half_, :, :].rearrange("p a h -> p (a h)"),
                                                  ident16[:, :])
                            mm.then_inc(mt_p, 1)
                    lag, h = (1, s - OFF) if s >= OFF else (2, s + H - OFF)
                    if active(j, u, lag):
                        b, o = n - lag, (i + lag) % 2
                        if h % (H // 2) == 0:
                            pe.wait_ge(m_in[h // (H // 2)], (b + 1) * 16)
                        if h >= 2 or not isinstance(j, int) or b >= 1:
                            pe.wait_ge(exped, b * H + h - 1)
                        for c in range(NT):
                            mm = pe.matmul(t_ps[h % 2][:, c * T:(c + 1) * T],
                                           k_st[o][0:KROWS, h, c * P:(c + 1) * P], q_st[o][0:KROWS, h, :],
                                           start=True, stop=True)
                        mm.then_inc(shifted, 1)
                    score_unit(s, 1)
                    lag, h = (lag, h - 1) if h else (lag + 1, H - 1)
                    if active(j, u, lag):
                        b, o = n - lag, (i + lag) % 2
                        g = h // 2
                        pe.wait_ge(exped, b * H + h + 1)
                        if h == 0:
                            pe.wait_ge(v_d, b + 1)
                        if h % 2 == 0 and (g >= 2 or not isinstance(j, int) or b >= 1):
                            pe.wait_ge(ov_d, b * (H // 2) + g - 1)
                        for t in range(NT):
                            for c in range(NT):
                                at = (2 * (h % 2) + t) * VC
                                mm = pe.matmul(o_ps[g % 2][:, at:at + VC], prob[h % 4][:, c, t * P:(t + 1) * P],
                                               vp[o][:, c, :], start=c == 0, stop=c == NT - 1)
                        mm.then_inc(pv, 1)

            pipeline(pe, body, ahead=1)

        @block.vector
        def _(dve):
            dve.memset(w_v[:, RD:VC], 0.0).then_inc(blank, 1)
            dve.memset(b_v[:, RD:VC], 0.0).then_inc(blank, 1)
            dve.wait_ge(blank, 2)
            dve.memset(b_v[:, CS:CS + 1], 1.0).then_inc(blank, 1)
            dve.wait_ge(folded, 6)

            def body(j, u):
                n = 2 * j + u
                i = u
                later = lambda k: not isinstance(j, int) or n >= k

                def reduce_unit(w):
                    b = n - 1
                    dve.wait_ge(score, b * H + w + 1)
                    g, t = w // 2, w % 2
                    if w == 0 and later(2):
                        dve.wait_ge(mp_d, b * MP)
                    dve.tensor_reduce(nmax[:, t, 2 * g:2 * g + 2],
                                      s_ps[t][:, :].rearrange("p (h k) -> p h k", h=2), AX.X, ALU.max,
                                      negate=True).then_inc(maxed, 1)

                def split_max(half_, k):
                    b = n - 1
                    hs = slice(half_ * H // 2, (half_ + 1) * H // 2)
                    high, mid, low = (mpart[:, :, half_, c, :] for c in range(NPART))
                    if k:
                        dve.wait_ge(mp_d, b * MP + 4 * half_ + k)
                    else:
                        dve.wait_ge(maxed, b * H + 8 * (half_ + 1))
                        if later(2):
                            dve.wait_ge(mt_p, 2 * (b - 1) + half_ + 1)
                    step = (lambda: dve.tensor_copy(high, nmax[:, :, hs]),
                            lambda: dve.tensor_tensor(nrest[:, :, hs], nmax[:, :, hs], high, ALU.subtract),
                            lambda: dve.tensor_copy(mid, nrest[:, :, hs]),
                            lambda: dve.tensor_tensor(low, nrest[:, :, hs], mid, ALU.subtract))[k]
                    step().then_inc(mp_d, 1)

                def moments(k):
                    t = k % NT
                    if k == 0:
                        dve.wait_ge(x_in, (n + 2) * 16)
                        if later(0):
                            dve.wait_ge(z_d, (n + 1) * NT)
                            dve.wait_ge(norm_d, (n + 1) * NORM)
                    if k < NT:
                        dve.bn_stats(stats[:, t, :], x[1 - i][:, t, :]).then_inc(stats_d, 1)
                    else:
                        dve.wait_ge(stats_d, (n + 1) * NT + t + 1)
                        apart(dve, spare)
                        dve.bn_aggr(mv[:, t, :], stats[:, t, :]).then_inc(mv_d, 1)

                def normed(k):
                    t = k % NT
                    if k == 0:
                        dve.wait_ge(norm_d, (n + 2) * NORM)
                        if later(1):
                            dve.wait_ge(y_out, n * 16)
                            dve.wait_ge(z_t, n)
                    dst, scale, done = ((y, r1, y_d), (z, r2, z_d))[k // NT]
                    dve.tensor_scalar(dst[1 - i][:, t, :], x[1 - i][:, t, :], mv[:, t, 0:1], scale[:, t:t + 1],
                                      ALU.subtract, ALU.mult).then_inc(done, 1)

                def weigh(k, b, o):
                    def wide(a):
                        return a[:, :].unsqueeze(2).broadcast_to([P, H * NT, R])

                    if k or not isinstance(b, int) or b >= 1:
                        dve.wait_ge(post, b * POST + k)
                    if k == 0:
                        dve.wait_ge(ov_d, (b + 1) * H // 2)
                    if k == 5:
                        dve.wait_ge(cexp_d, b + 1)
                    if k == 8 and (not isinstance(b, int) or b >= 1):
                        dve.wait_ge(prod_d, b)
                    by_head = lambda a: a[:, :, :].rearrange("p (h i) r -> p h i r", i=NT)
                    step = (
                        lambda: dve.reciprocal(inv[:, :], ov[o][:, :, CS]),
                        lambda: dve.tensor_tensor(comp[:, :, :], ov[o][:, :, CC:CS], wide(inv), ALU.mult),
                        lambda: dve.tensor_tensor(
                            by_head(comp2), by_head(comp), vp[o][:, :, CQ:CQ + H].rearrange("p i h -> p h i")
                            .unsqueeze(3).broadcast_to([P, H, NT, R]), ALU.add),
                        lambda: dve.tensor_reduce(cmax[:, :], comp2[:, :, :], AX.X, ALU.max),
                        lambda: dve.tensor_tensor(comp3[:, :, :], comp2[:, :, :], wide(cmax), ALU.subtract),
                        lambda: dve.tensor_reduce(csum[:, :], cexp[:, :, :], AX.X, ALU.add),
                        lambda: dve.reciprocal(cinv[:, :], csum[:, :]),
                        lambda: dve.tensor_tensor(cw[:, :], cinv[:, :], inv[:, :], ALU.mult),
                        lambda: dve.tensor_tensor(wgt[:, :, :], cexp[:, :, :], wide(cw), ALU.mult))[k]
                    step().then_inc(post, 1)

                if active(j, u, 3):
                    for k in range(5, POST):
                        weigh(k, n - 3, 1 - i)
                if active(j, u, 1):
                    for w in range(H // 2):
                        reduce_unit(w)
                    for k in range(MP // 2):
                        split_max(0, k)
                    for w in range(H // 2, H):
                        reduce_unit(w)
                for k in range(MP // 2):
                    if active(j, u, 1):
                        split_max(1, k)
                    if active(j, u, -1):
                        moments(k)
                if active(j, u, 3):
                    b, o = n - 3, 1 - i
                    dve.wait_ge(prod_d, b + 1)
                    if later(5):
                        dve.wait_ge(ao_out, (b - 1) * 16)
                    for t in range(NT):
                        dve.tensor_reduce(
                            ao[o][:, t, :].rearrange("p (h e) -> p h e", h=H),
                            prod[:, :, :].rearrange("p (h i) (r e) -> p i h e r", i=NT, r=R)[:, t],
                            AX.X, ALU.add).then_inc(ao_d, 1)
                for k in range(5):
                    if active(j, u, 2):
                        weigh(k, n - 2, i)
                    if k < 2 * NT and active(j, u, -1):
                        normed(k)
                if active(j, u, 0):
                    dve.wait_ge(v_p, n + 1)
                    if later(2):
                        dve.wait_ge(pv, (n - 1) * H)
                        dve.wait_ge(post, (n - 2) * POST + 3)
                    dve.tensor_tensor(vp[i][:, :, :], zv_ps[:, 0:NT * VC].rearrange("p (i c) -> p i c", i=NT),
                                      b_v[:, :].unsqueeze(1).broadcast_to([P, NT, VC]), ALU.add).then_inc(v_d, 1)

            pipeline(dve, body, ahead=1)


def fold_ffn(nc, d):
    ctx = ExitStack()
    with ctx:
        sb, sem = memory(nc, ctx, "w")
        w1 = [sb(f"w1_{i}", [P, NI, P]) for i in range(2)]
        w2 = [sb(f"w2_{i}", [P, NI, P]) for i in range(2)]
        bias = [sb(f"bias_{i}", [P, NI + 1]) for i in range(2)]
        ones = sb("ones", [P, P])
        ident = sb("ident", [P, P])
        rows = [sb(f"rows_{i}", [P, P]) for i in range(2)]
        col = [sb(f"col_{i}", [P, 1]) for i in range(2)]
        fold = [sb(f"fold_{i}", [P, 2, P]) for i in range(2)]
        bank = [ctx.enter_context(nc.psum_tensor(f"w_bank{i}", [P, 512], F32)) for i in range(6)]
        w_in = [sem(f"in{i}") for i in range(2)]
        ident_in = sem("ident_in")
        ones_d = sem("ones_d")
        prod_p = sem("prod_p")
        col_d = sem("col_d")
        rows_d = sem("rows_d")
        turned = sem("turned")
        fold_d = sem("fold_d")
        out_d = sem("out_d")
        block = ctx.enter_context(nc.Block())

        def store(sp, g):
            sp.wait_ge(fold_d, 2 * (g + 1))
            sp.wait_ge(out_d, 2 * g * 16)
            for c in range(2):
                sp.dma_start(d["folded"][2 * g + c], fold[g % 2][:, :, :].rearrange("p a o -> p (a o)")
                             ).then_inc(out_d, 16)

        @block.sync
        def _(sp):
            sp.dma_start(ident[:, :], d["ident"]).then_inc(ident_in, 16)
            for g in range(NG):
                i = g % 2
                if g >= 2:
                    sp.wait_ge(prod_p, g - 1)
                    sp.wait_ge(col_d, g - 1)
                sp.dma_start(w1[i][:, :, :], d["W1"][g].rearrange("(c p) h -> p c h", p=P)).then_inc(w_in[i], 16)
                sp.dma_start(w2[i][:, :, :], d["W2_t"][g].rearrange("(c p) o -> p c o", p=P)).then_inc(w_in[i], 16)
                sp.dma_start(bias[i][:, :], d["ffn_b"][g]).then_inc(w_in[i], 16)
                if g >= 1:
                    store(sp, g - 1)
            store(sp, NG - 1)
            sp.wait_ge(out_d, NG * 2 * 16)

        @block.vector
        def _(dve):
            dve.memset(ones[:, :], 1.0).then_inc(ones_d, 1)
            dve.wait_ge(ones_d, 1)
            for g in range(NG):
                i = g % 2
                dve.wait_ge(prod_p, g + 1)
                dve.tensor_tensor(col[i][:, :], bank[2 + i][:, 0:1], bias[i][:, NI:NI + 1], ALU.add).then_inc(col_d, 1)
                dve.wait_ge(col_d, g + 1)
                if g >= 2:
                    dve.wait_ge(turned, g - 1)
                dve.tensor_scalar(rows[i][:, :], ones[:, :], col[i][:, 0:1], None, ALU.mult).then_inc(rows_d, 1)

        @block.scalar
        def _(act):
            for g in range(NG):
                i = g % 2
                act.wait_ge(prod_p, g + 1)
                if g >= 2:
                    act.wait_ge(out_d, (g - 1) * 2 * 16)
                act.copy(fold[i][:, 0, :], bank[i][:, 0:P]).then_inc(fold_d, 1)
                act.wait_ge(turned, g + 1)
                act.copy(fold[i][:, 1, :], bank[4 + i][:, 0:P]).then_inc(fold_d, 1)

        @block.tensor
        def _(pe):
            pe.wait_ge(ident_in, 16)
            for g in range(NG):
                i = g % 2
                pe.wait_ge(w_in[i], (g // 2 + 1) * 48)
                if g >= 2:
                    pe.wait_ge(fold_d, 2 * (g - 1))
                for c in range(NI):
                    pe.matmul(bank[i][:, 0:P], w1[i][:, c, :], w2[i][:, c, :], start=c == 0, stop=c == NI - 1)
                for c in range(NI):
                    mm = pe.matmul(bank[2 + i][:, 0:1], w2[i][:, c, :], bias[i][:, c:c + 1], start=c == 0,
                                   stop=c == NI - 1)
                mm.then_inc(prod_p, 1)
                pe.wait_ge(rows_d, g + 1)
                pe.transpose(bank[4 + i][:, 0:P], rows[i][:, :], ident[:, :]).then_inc(turned, 1)


def dense(nc, d):
    ctx = ExitStack()
    with ctx:
        sb, sem = memory(nc, ctx, "b")
        NU, C = NB // 2, 2 * NT
        w_f = sb("w_f", [P, P])
        w_r1 = sb("w_r1", [P, 2, P])
        w_r2 = sb("w_r2", [P, 2, P])
        b_f = sb("b_f", [P, P])
        b_r2 = sb("b_r2", [P, P])
        cols = sb("cols", [P, 4])
        ident = sb("ident", [P, P])
        half = sb("half", [P, C])
        two = lambda name, shape: [sb(f"{name}{i}", shape) for i in range(2)]
        x, y, ao = two("x", [P, C, P]), two("y", [P, C, P]), two("ao", [P, C, P])
        wc = two("wc", [P, 2, P])
        ao_t, r, xr = two("ao_t", [P, C * P]), two("r", [P, C, P]), two("xr", [P, C, P])
        yb, z, on = two("yb", [P, C, P]), two("z", [P, C, P]), two("on", [P, C * P])
        hid, x1, xb = two("hid", [P, 2, C * P]), two("x1", [P, C, P]), two("xb", [P, C, P])
        z1, z1t, x2 = two("z1_", [P, C, P]), two("z1t", [P, C * P]), two("x2_", [P, C, P])
        stats, mv = two("stats", [P, C, 6]), two("mv", [P, C, 2])
        var, rs = two("var", [P, C]), two("rs", [P, C])
        bank = [ctx.enter_context(nc.psum_tensor(f"b_bank{i}", [P, 512], F32)) for i in range(8)]
        aot_ps, zt_ps, z1t_ps, r_ps, h_ps, f_ps, g_ps = *bank[0:4], bank[4:6], bank[6], bank[7]

        spare = sem("spare")
        loaded = sem("loaded")
        half_d = sem("half_d")
        ay_in = sem("ay_in")
        x_in = sem("x_in")
        wc_in = sem("wc_in")
        aot_p, aot_d = sem("aot_p"), sem("aot_d")
        yb_d = sem("yb_d")
        r_p, r_d = sem("r_p"), sem("r_d")
        xr_d = sem("xr_d")
        stat_d = [sem(f"stat_d{i}") for i in range(2)]
        mv_d = [sem(f"mv_d{i}") for i in range(2)]
        norm_d = [sem(f"norm_d{i}") for i in range(2)]
        z_d = [sem(f"z_d{i}") for i in range(2)]
        zt_p, on_d = sem("zt_p"), sem("on_d")
        h_p, hid_d = sem("h_p"), sem("hid_d")
        f_p, x1_d, xb_d = sem("f_p"), sem("x1_d"), sem("xb_d")
        z1t_p, z1t_d = sem("z1t_p"), sem("z1t_d")
        g_p, x2_d, x2_out = sem("g_p"), sem("x2_d"), sem("x2_out")

        units = lambda a: a.rearrange("b t f -> (b t) f").rearrange("(j u c p) f -> j u p c f", u=2, c=C, p=P)
        x_dram, y_dram, ao_dram, x2_dram = units(d["x"]), units(d["y"]), units(d["ao"]), units(d["x2"])
        wc_dram = d["folded"].rearrange("(j u) p f -> j u p f", u=2)
        has = lambda j, u, lag: active(j, u, lag, NU)
        later = lambda j, n, k: not isinstance(j, int) or n >= k
        flat = lambda a: a[:, :, :].rearrange("p c f -> p (c f)")
        block = ctx.enter_context(nc.Block())

        @block.sync
        def _(sp):
            for dst, src in ((w_f[:, :], d["a_Wf_t"]),
                             (w_r1[:, :, :].rearrange("p a f -> p (a f)"), d["a_Wr1_t"]),
                             (w_r2[:, :, :], d["a_Wr2_t"].rearrange("(a p) f -> p a f", p=P)),
                             (b_f[:, :], d["a_bf_b"]), (b_r2[:, :], d["a_br2_b"]), (cols[:, :], d["b_cols"]),
                             (ident[:, :], d["ident"])):
                sp.dma_start(dst, src).then_inc(loaded, 16)

            def body(j, u):
                n, i = 2 * j + u, u
                if has(j, u, 0):
                    at = pair(j, u, 0)
                    sp.wait_ge(ay_in, n * 32)
                    apart(sp, spare)
                    if later(j, n, 2):
                        sp.wait_ge(aot_p, n - 1)
                        apart(sp, spare)
                        sp.wait_ge(yb_d, n - 1)
                        apart(sp, spare)
                    sp.dma_start(ao[i][:, :, :], ao_dram[at[0], at[1]]).then_inc(ay_in, 16)
                    sp.dma_start(y[i][:, :, :], y_dram[at[0], at[1]]).then_inc(ay_in, 16)
                    if later(j, n, 2):
                        sp.wait_ge(xr_d, (n - 1) * 2)
                        apart(sp, spare)
                    sp.wait_ge(x_in, n * 16)
                    apart(sp, spare)
                    sp.dma_start(x[i][:, :, :], x_dram[at[0], at[1]]).then_inc(x_in, 16)
                if has(j, u, 2):
                    sp.wait_ge(x2_d, n - 1)
                    apart(sp, spare)
                    at = pair(j, u, 2)
                    sp.wait_ge(x2_out, (n - 2) * 16)
                    apart(sp, spare)
                    sp.dma_start(x2_dram[at[0], at[1]], x2[i][:, :, :]).then_inc(x2_out, 16)
                if has(j, u, 1):
                    at = pair(j, u, 1)
                    if later(j, n, 3):
                        sp.wait_ge(g_p, n - 2)
                        apart(sp, spare)
                        sp.wait_ge(xb_d, n - 2)
                        apart(sp, spare)
                    sp.wait_ge(wc_in, (n - 1) * 16)
                    apart(sp, spare)
                    sp.dma_start(wc[1 - i][:, :, :].rearrange("p a f -> p (a f)"), wc_dram[at[0], at[1]]
                                 ).then_inc(wc_in, 16)

            pipeline(sp, body, NU, 3)
            sp.wait_ge(x2_out, NU * 16)

        @block.gpsimd
        def _(pool):
            pool.memset(half[:, :], -0.5).then_inc(half_d, 1)
            pool.wait_ge(half_d, 1)
            pool.wait_ge(loaded, 7 * 16)

            def norm(k, n):
                pool.wait_ge(mv_d[k], (n + 1) * C)
                apart(pool, spare)
                pool.tensor_scalar(var[k][:, :], mv[k][:, :, 1], EPS, 1.0, ALU.add, ALU.mult).then_inc(norm_d[k], 1)
                pool.wait_ge(norm_d[k], 2 * n + 1)
                pool.tensor_tensor(rs[k][:, :], var[k][:, :], half[:, :], ALU.pow).then_inc(norm_d[k], 1)

            rows = lambda a: a[:, :].unsqueeze(1).broadcast_to([P, C, P])

            def body(j, u):
                n, i = 2 * j + u, u
                if has(j, u, 0):
                    pool.wait_ge(ay_in, (n + 1) * 32)
                    if later(j, n, 2):
                        pool.wait_ge(r_d, n - 1)
                    pool.tensor_tensor(yb[i][:, :, :], y[i][:, :, :], rows(b_f), ALU.add).then_inc(yb_d, 1)
                    pool.wait_ge(x_in, (n + 1) * 16)
                    if later(j, n, 2):
                        pool.wait_ge(x1_d, n - 1)
                    pool.tensor_tensor(xr[i][:, :, :], x[i][:, :, :], rows(b_r2), ALU.add).then_inc(xr_d, 1)
                    norm(0, n)
                    pool.wait_ge(r_d, n + 1)
                    pool.wait_ge(xr_d, 2 * n + 1)
                    pool.tensor_tensor(xr[i][:, :, :], xr[i][:, :, :], r[i][:, :, :], ALU.add).then_inc(xr_d, 1)
                if has(j, u, 1):
                    norm(1, n - 1)
                    pool.wait_ge(wc_in, n * 16)
                    pool.wait_ge(x1_d, n)
                    if later(j, n, 3):
                        pool.wait_ge(x2_d, n - 2)
                    pool.tensor_tensor(xb[1 - i][:, :, :], x1[1 - i][:, :, :],
                                       wc[1 - i][:, 1, :].unsqueeze(1).broadcast_to([P, C, P]), ALU.add
                                       ).then_inc(xb_d, 1)

            pipeline(pool, body, NU, 3)

        @block.scalar
        def _(act):
            act.wait_ge(loaded, 7 * 16)

            def body(j, u):
                n, i = 2 * j + u, u
                if has(j, u, 1):
                    act.wait_ge(zt_p, n)
                    act.activation(on[1 - i][:, :], zt_ps[:, :], ACT.Identity, scale=cols[:, 2:3], bias=cols[:, 3:4]
                                   ).then_inc(on_d, 1)
                if has(j, u, 0):
                    act.wait_ge(aot_p, n + 1)
                    act.copy(ao_t[i][:, :], aot_ps[:, :]).then_inc(aot_d, 1)
                if has(j, u, 1):
                    if later(j, n, 3):
                        act.wait_ge(f_p, n - 2)
                    for c in range(2):
                        act.wait_ge(h_p, 2 * (n - 1) + c + 1)
                        act.activation(hid[1 - i][:, c, :], h_ps[c][:, :], ACT.Relu, bias=cols[:, c:c + 1]
                                       ).then_inc(hid_d, 1)
                if has(j, u, 2):
                    act.wait_ge(z1t_p, n - 1)
                    act.copy(z1t[i][:, :], z1t_ps[:, :]).then_inc(z1t_d, 1)

            pipeline(act, body, NU, 3)

        @block.tensor
        def _(pe):
            pe.wait_ge(loaded, 7 * 16)

            def turn(dst, src):
                for c in range(C):
                    mm = pe.transpose(dst[:, c * P:(c + 1) * P], src[:, c, :], ident[:, :])
                return mm

            def body(j, u):
                n, i = 2 * j + u, u
                if has(j, u, 1):
                    pe.wait_ge(z_d[0], n * C)
                    if later(j, n, 2):
                        pe.wait_ge(on_d, n - 1)
                    turn(zt_ps, z[1 - i]).then_inc(zt_p, 1)
                if has(j, u, 0):
                    pe.wait_ge(ay_in, (n + 1) * 32)
                    if later(j, n, 1):
                        pe.wait_ge(aot_d, n)
                    turn(aot_ps, ao[i]).then_inc(aot_p, 1)
                if has(j, u, 1):
                    pe.wait_ge(on_d, n)
                    for c in range(2):
                        if later(j, n, 2):
                            pe.wait_ge(hid_d, 2 * (n - 2) + c + 1)
                        pe.matmul(h_ps[c][:, :], w_r1[:, c, :], on[1 - i][:, :], start=True, stop=True
                                  ).then_inc(h_p, 1)
                if has(j, u, 0):
                    pe.wait_ge(aot_d, n + 1)
                    if later(j, n, 1):
                        pe.wait_ge(r_d, n)
                    for c in range(C):
                        mm = pe.matmul(r_ps[:, c * P:(c + 1) * P], ao_t[i][:, c * P:(c + 1) * P], w_f[:, :],
                                       start=True, stop=True)
                    mm.then_inc(r_p, 1)
                if has(j, u, 1):
                    pe.wait_ge(hid_d, 2 * n)
                    if later(j, n, 2):
                        pe.wait_ge(x1_d, n - 1)
                    for c in range(C):
                        for k in range(2):
                            mm = pe.matmul(f_ps[:, c * P:(c + 1) * P], hid[1 - i][:, k, c * P:(c + 1) * P],
                                           w_r2[:, k, :], start=k == 0, stop=k == 1)
                    mm.then_inc(f_p, 1)
                if has(j, u, 2):
                    pe.wait_ge(z_d[1], (n - 1) * C)
                    if later(j, n, 3):
                        pe.wait_ge(z1t_d, n - 2)
                    turn(z1t_ps, z1[i]).then_inc(z1t_p, 1)
                    pe.wait_ge(z1t_d, n - 1)
                    pe.wait_ge(wc_in, (n - 1) * 16)
                    if later(j, n, 3):
                        pe.wait_ge(x2_d, n - 2)
                    for c in range(C):
                        mm = pe.matmul(g_ps[:, c * P:(c + 1) * P], z1t[i][:, c * P:(c + 1) * P], wc[i][:, 0, :],
                                       start=True, stop=True)
                    mm.then_inc(g_p, 1)

            pipeline(pe, body, NU, 3)

        @block.vector
        def _(dve):
            def moments(k, n, src):
                for c in range(C):
                    dve.bn_stats(stats[k][:, c, :], src[:, c, :]).then_inc(stat_d[k], 1)
                for c in range(C):
                    dve.wait_ge(stat_d[k], n * C + c + 1)
                    apart(dve, spare)
                    dve.bn_aggr(mv[k][:, c, :], stats[k][:, c, :]).then_inc(mv_d[k], 1)

            def normed(k, n, src, dst):
                dve.wait_ge(norm_d[k], 2 * (n + 1))
                for c in range(C):
                    dve.tensor_scalar(dst[:, c, :], src[:, c, :], mv[k][:, c, 0:1], rs[k][:, c:c + 1],
                                      ALU.subtract, ALU.mult).then_inc(z_d[k], 1)

            def body(j, u):
                n, i = 2 * j + u, u
                if has(j, u, 0):
                    dve.wait_ge(r_p, n + 1)
                    dve.wait_ge(yb_d, n + 1)
                    if later(j, n, 2):
                        dve.wait_ge(xr_d, 2 * (n - 1))
                    dve.tensor_tensor(flat(r[i]), r_ps[:, :], flat(yb[i]), ALU.add).then_inc(r_d, 1)
                    dve.wait_ge(r_d, n + 1)
                    moments(0, n, r[i])
                if has(j, u, 2):
                    dve.wait_ge(g_p, n - 1)
                    dve.wait_ge(xb_d, n - 1)
                    if later(j, n, 4):
                        dve.wait_ge(x2_out, (n - 3) * 16)
                    dve.tensor_tensor(flat(x2[i]), g_ps[:, :], flat(xb[i]), ALU.add).then_inc(x2_d, 1)
                if has(j, u, 0):
                    if later(j, n, 2):
                        dve.wait_ge(zt_p, n - 1)
                    normed(0, n, r[i], z[i])
                if has(j, u, 1):
                    dve.wait_ge(f_p, n)
                    dve.wait_ge(xr_d, 2 * n)
                    if later(j, n, 3):
                        dve.wait_ge(xb_d, n - 2)
                    dve.tensor_tensor(flat(x1[1 - i]), f_ps[:, :], flat(xr[1 - i]), ALU.add).then_inc(x1_d, 1)
                    dve.wait_ge(x1_d, n)
                    moments(1, n - 1, x1[1 - i])
                    if later(j, n, 3):
                        dve.wait_ge(z1t_p, n - 2)
                    normed(1, n - 1, x1[1 - i], z1[1 - i])

            pipeline(dve, body, NU, 3)


def attention_b(nc, d):
    ctx = ExitStack()
    with ctx:
        sb, sem = memory(nc, ctx, "c")
        SEG = 64
        NS = T // SEG
        HV = H * HD
        MW = HV + H
        VW = H * (HD + 1)
        WIN = 96
        ST = 8
        S0, OFF = 1, 7
        two = lambda name, shape, dt=F32: [sb(f"{name}{i}", shape, dt) for i in range(2)]
        w_kq = sb("w_kq", [P, 2, P])
        w_v = sb("w_v", [P, P])
        w_o = sb("w_o", [P, P])
        ident, ident16 = sb("ident", [P, P]), sb("ident16", [P, P], BF16)
        causal, causal_t = sb("causal", [P, 512], BF16), sb("causal_t", [P, 512], BF16)
        causal32 = sb("causal32", [P, 2 * P])
        diag = sb("diag", [P, MW])
        beta = sb("beta", [P, 4])
        bexp = sb("bexp", [P, 1])
        half = sb("half", [P, NT])
        wc = two("wc", [P, 2, P])
        x = two("x", [P, NT, P])
        z, zt = two("z", [P, NT, P]), two("zt", [P, T])
        stats, mv = two("stats", [P, NT, 6]), two("mv", [P, NT, 2])
        var, rs = two("var", [P, NT]), two("rs", [P, NT])
        kq = two("kq", [P, 2, T])
        rest = sb("rest", [P, 2, T])
        parts = two("parts", [P, 2, NPART, T], BF16)
        q_st, k_st = two("q_st", [P, H, T], BF16), two("k_st", [P, H, T], BF16)
        pos, neg, nexp = (sb(a, [P, 2, T]) for a in ("pos", "neg", "nexp"))
        sg = two("sg", [P, NS, 2, SEG])
        skn = sb("skn", [P, NS - 1, P])
        uv = two("uv", [P, NS - 1, MW])
        mz, mzt = sb("mz", [P, MW]), sb("mzt", [P, MW])
        dn, dr = sb("dn", [P, NS - 1, H]), sb("dr", [P, NS - 1, H])
        am = two("am", [P, NS - 1, P])
        vb = two("vb", [P, NT, VW + WIN])
        nmax, nrest = sb("nmax", [P, NT, H]), sb("nrest", [P, NT, H])
        mpart = sb("mpart", [P, NT, 2, NPART, H // 2], BF16)
        mt = [sb(f"mt{i}", [NPART * H // 2, T], BF16) for i in range(2)]
        prob = [sb(f"prob{i}", [P, 2, T]) for i in range(4)]
        dinv, ad = sb("dinv", [P, NT, H]), sb("ad", [P, NT, P])
        at_b = sb("at", [P, T])
        xt, x3, xb, x4 = (two(a, [P, NT, P]) for a in ("xt", "x3_", "xb", "x4_"))
        z4, z4t = sb("z4", [P, NT, P]), sb("z4t", [P, T])
        bank = [ctx.enter_context(nc.psum_tensor(f"c_bank{i}", [P, 512], F32)) for i in range(8)]
        ps_a, ps_b, ps_c, s_ps, t_ps, o_ps = *bank[0:3], bank[3:5], bank[5:7], bank[7]
        mt_ps = ps_a[0:NPART * H // 2, 0:T // 2].bitcast(BF16)

        spare, loaded, const_d, beta_d = sem("spare"), sem("loaded"), sem("const_d"), sem("beta_d")
        mask_d = sem("mask_d")
        x_in, xt_in, wc_in = sem("x_in"), sem("xt_in"), sem("wc_in")
        stat_d = [sem(f"stat_d{i}") for i in range(2)]
        mv_d = [sem(f"mv_d{i}") for i in range(2)]
        norm_d = [sem(f"norm_d{i}") for i in range(2)]
        z_d, zt_p, zt_d = sem("z_d"), sem("zt_p"), sem("zt_d")
        kq_p, kq_d = sem("kq_p"), sem("kq_d")
        pn_d, nexp_d, sg_d = sem("pn_d"), sem("nexp_d"), sem("sg_d")
        split_d, parts_out = sem("split_d"), sem("parts_out")
        stack_in = [sem(f"stack_in{i}") for i in range(2)]
        vs_p, vs_d, v_p, v_d = sem("vs_p"), sem("vs_d"), sem("v_p"), sem("v_d")
        sk_p, sk_d = sem("sk_p"), sem("sk_d")
        mem_p = sem("mem_p")
        mz_d = sem("mz_d")
        read_p = sem("read_p")
        read_d = sem("read_d")
        u_d = sem("u_d")
        score, maxed, mp_d = sem("score"), sem("maxed"), sem("mp_d")
        mt_p, mt_d, mt_out = sem("mt_p"), sem("mt_d"), sem("mt_out")
        m_in = [sem(f"m_in{i}") for i in range(2)]
        shifted, exped, pv = sem("shifted"), sem("exped"), sem("pv")
        ad_d = sem("ad_d")
        at_p, at_d = sem("at_p"), sem("at_d")
        wo_p, x3_d, xb_d = sem("wo_p"), sem("x3_d"), sem("xb_d")
        z4_d, z4_p, z4t_d, g_p, x4_d, x4_out = (sem(a) for a in ("z4_d", "z4_p", "z4t_d", "g_p", "x4_d", "x4_out"))

        USES_A = [(at_d, 2, 3), (kq_d, 2, 0), (mt_d, 2, 1)]
        USES_B = [(zt_d, 1, 0), (x3_d, 1, 3), (vs_d, 1, 0), (z4t_d, 1, 3), (x4_d, 1, 3), (v_d, 1, 0)]

        def free(eng, uses, k, j, u):
            n = 2 * j + u
            if not isinstance(j, int):
                s, per, lag = uses[k - 1]
                eng.wait_ge(s, (n - lag - (k == 0) + 1) * per)
                return
            for m, (s, per, lag) in enumerate(uses):
                done = min(n - lag - (m >= k) + 1, NB)
                if done > 0:
                    eng.wait_ge(s, done * per)

        later = lambda j, b, k: not isinstance(j, int) or b >= k
        pairs = lambda a: a.rearrange("(j u) (i p) f -> j u p i f", u=2, p=P)
        x_dram, out_dram, wc_dram = pairs(d["x2"]), pairs(d["out"]), d["folded"]
        parts_dram, m_dram = d["c_parts_dram"], d["c_m_dram"]
        flat = lambda a: a[:, :, :].rearrange("p c f -> p (c f)")
        N_LOAD, SPLIT, MP = 7, 4, 8
        MT_AT = (3, 6)

        def turn(s):
            return (1, s - OFF) if s >= OFF else (2, s + ST - OFF)

        def before(lag, g):
            return (lag, g - 1) if g else (lag + 1, ST - 1)

        block = ctx.enter_context(nc.Block())

        @block.sync
        def _(sp):
            for dst, src in ((w_kq[:, :, :].rearrange("p a f -> p (a f)"), d["b_Wkq_t"]), (w_v[:, :], d["b_Wv_t"]),
                             (w_o[:, :], d["b_Wo_t"]), (ident[:, :], d["ident"]), (causal32[:, :], d["causal"]),
                             (diag[:, :], d["diag"]), (beta[:, 0:1], d["b_beta"])):
                sp.dma_start(dst, src).then_inc(loaded, 16)
            sp.wait_ge(const_d, 16)

            def body(j, u):
                n, i = 2 * j + u, u

                def shift_rows(h2):
                    b, o = n - 1, 1 - i
                    sp.wait_ge(mt_out, (2 * b + h2 + 1) * 16)
                    apart(sp, spare)
                    sp.dma_start(q_st[o][MROW:KROWS, h2 * H // 2:(h2 + 1) * H // 2, :],
                                 m_dram[o, h2].rearrange("(a h) t -> a h t", a=NPART)).then_inc(m_in[h2], 16)

                if active(j, u, -1):
                    at = pair(j, u, -1)
                    if later(j, n, 0):
                        sp.wait_ge(x_in, (n + 1) * 16)
                        apart(sp, spare)
                    if later(j, n, 1):
                        sp.wait_ge(z_d, n * NT)
                        apart(sp, spare)
                    sp.dma_start(x[1 - i][:, :, :], x_dram[at[0], at[1]]).then_inc(x_in, 16)
                if active(j, u, 2):
                    at = pair(j, u, 2)
                    sp.wait_ge(xt_in, (n - 2) * 16)
                    apart(sp, spare)
                    sp.wait_ge(wc_in, (n - 2) * 16)
                    apart(sp, spare)
                    if later(j, n, 4):
                        sp.wait_ge(x3_d, n - 3)
                        apart(sp, spare)
                        sp.wait_ge(g_p, n - 3)
                        apart(sp, spare)
                        sp.wait_ge(xb_d, n - 3)
                        apart(sp, spare)
                    sp.dma_start(xt[i][:, :, :], x_dram[at[0], at[1]]).then_inc(xt_in, 16)
                    sp.dma_start(wc[i][:, :, :].rearrange("p a f -> p (a f)"), wc_dram[at[0]]).then_inc(wc_in, 16)
                def stack(h2):
                    hs = slice(h2 * H // 2, (h2 + 1) * H // 2)
                    if later(j, n, 2):
                        sp.wait_ge(shifted, (n - 2) * ST + (h2 + 1) * ST // 2)
                        apart(sp, spare)
                    for a in range(NPART):
                        sp.dma_start(q_st[i][a * NPART * HD:(a + 1) * NPART * HD, hs, :],
                                     parts_dram[i, NPART + a].rearrange("(d h) t -> d h t", d=HD)[:, hs]
                                     .unsqueeze(0).broadcast_to([NPART, HD, H // 2, T])
                                     ).then_inc(stack_in[h2], 16)
                    sp.dma_start(k_st[i][0:SROWS, hs, :],
                                 parts_dram[i, 0:NPART].rearrange("c (d h) t -> (c d) h t", d=HD)[:, hs]
                                 .unsqueeze(0).broadcast_to([NPART, NPART * HD, H // 2, T])
                                 ).then_inc(stack_in[h2], 16)

                if active(j, u, 0):
                    sp.wait_ge(split_d, (n + 1) * SPLIT)
                    apart(sp, spare)
                    sp.dma_start(parts_dram[i].rearrange("c p t -> p c t"),
                                 parts[i][:, :, :, :].rearrange("p q c t -> p (q c) t")).then_inc(parts_out, 16)
                    sp.wait_ge(parts_out, (n + 1) * 16)
                    apart(sp, spare)
                    stack(0)
                if active(j, u, 1):
                    shift_rows(0)
                    shift_rows(1)
                if active(j, u, 0):
                    stack(1)
                if active(j, u, 3):
                    at = pair(j, u, 3)
                    sp.wait_ge(x4_d, n - 2)
                    apart(sp, spare)
                    sp.wait_ge(x4_out, (n - 3) * 16)
                    apart(sp, spare)
                    sp.dma_start(out_dram[at[0], at[1]], x4[1 - i][:, :, :]).then_inc(x4_out, 16)

            pipeline(sp, body, ahead=1)
            sp.wait_ge(x4_out, NB * 16)

        @block.gpsimd
        def _(pool):
            def const(k, ins):
                ins.then_inc(const_d, 1)
                pool.wait_ge(const_d, k)

            const(1, pool.memset(half[:, :], -0.5))
            for i in range(2):
                const(2 + 6 * i, pool.memset(k_st[i][64:P, :, :], 0.0))
                const(3 + 6 * i, pool.memset(k_st[i][MROW:P, :, :], 1.0))
                const(4 + 6 * i, pool.memset(vb[i][:, :, :], 0.0))
                const(5 + 6 * i, pool.memset(vb[i][:, :, 0:VW].rearrange("p i (h e) -> p i h e", h=H)[:, :, :, HD:],
                                             1.0))
                const(6 + 6 * i, pool.memset(uv[i][:, :, :], 0.0))
                const(7 + 6 * i, pool.memset(uv[i][0:SEG, :, HV:MW], 1.0))
            const(14, pool.memset(skn[:, :, :], 0.0))
            for i in range(2):
                const(15 + i, pool.memset(q_st[i][64:MROW, :, :], 0.0))

            def norm(k, b):
                pool.wait_ge(mv_d[k], (b + 1) * NT)
                apart(pool, spare)
                pool.tensor_scalar(var[k][:, :], mv[k][:, :, 1], EPS, 1.0, ALU.add, ALU.mult).then_inc(norm_d[k], 1)
                pool.wait_ge(norm_d[k], 2 * b + 1)
                pool.tensor_tensor(rs[k][:, :], var[k][:, :], half[:, :], ALU.pow).then_inc(norm_d[k], 1)

            def body(j, u):
                n, i = 2 * j + u, u
                if active(j, u, 0):
                    pool.wait_ge(kq_d, (n + 1) * 2)
                    if later(j, n, 2):
                        pool.wait_ge(parts_out, (n - 1) * 16)

                    def split(k, ins):
                        ins.then_inc(split_d, 1)
                        pool.wait_ge(split_d, n * SPLIT + k)
                        apart(pool, spare)

                    apart(pool, spare)
                    split(1, pool.tensor_scalar(parts[i][:, :, 0, :], kq[i][:, :, :], 1.0, 0.0, ALU.mult, ALU.add))
                    split(2, pool.tensor_tensor(rest[:, :, :], kq[i][:, :, :], parts[i][:, :, 0, :], ALU.subtract))
                    split(3, pool.tensor_scalar(parts[i][:, :, 1, :], rest[:, :, :], 1.0, 0.0, ALU.mult, ALU.add))
                    split(4, pool.tensor_tensor(parts[i][:, :, 2, :], rest[:, :, :], parts[i][:, :, 1, :],
                                                ALU.subtract))
                if active(j, u, 3):
                    b = n - 3
                    if later(j, b, 1):
                        pool.wait_ge(z4_d, b * NT)
                    norm(1, b)
                if active(j, u, 0):
                    pool.wait_ge(nexp_d, n + 1)
                    if later(j, n, 2):
                        pool.wait_ge(read_p, (n - 1) * 3)
                    pool.tensor_tensor(sg[i][:, :, :, :].rearrange("p s a t -> p a s t"),
                                       pos[:, :, :].rearrange("p a (s t) -> p a s t", s=NS),
                                       nexp[:, :, :].rearrange("p a (s t) -> p a s t", s=NS), ALU.add
                                       ).then_inc(sg_d, 1)
                if active(j, u, 3):
                    pool.wait_ge(wc_in, (b + 1) * 16)
                    pool.wait_ge(x3_d, b + 1)
                    if later(j, b, 2):
                        pool.wait_ge(x4_d, b - 1)
                    pool.tensor_tensor(xb[1 - i][:, :, :], x3[1 - i][:, :, :],
                                       wc[1 - i][:, 1, :].unsqueeze(1).broadcast_to([P, NT, P]), ALU.add
                                       ).then_inc(xb_d, 1)
                if active(j, u, -1):
                    if later(j, n, 0):
                        pool.wait_ge(z_d, (n + 1) * NT)
                    norm(0, n + 1)

            pipeline(pool, body, ahead=1)

        @block.scalar
        def _(act):
            act.wait_ge(loaded, N_LOAD * 16)
            act.activation(bexp[:, :], beta[:, 0:1], ACT.Exp, scale=-1.0).then_inc(beta_d, 1)
            act.copy(ident16[:, :], ident[:, :]).then_inc(mask_d, 1)
            for m, dst in enumerate((causal, causal_t)):
                act.copy(dst[:, :].rearrange("p (c f) -> p c f", c=4),
                         causal32[:, m * P:(m + 1) * P].unsqueeze(1).broadcast_to([P, 4, P])).then_inc(mask_d, 1)
            act.wait_ge(beta_d, 4)
            act.wait_ge(const_d, 16)

            def body(j, u):
                n, i = 2 * j + u, u
                for s in range(ST):
                    lag, g = turn(s)
                    if active(j, u, lag):
                        b = n - lag
                        act.wait_ge(shifted, b * ST + g + 1)
                        if g >= 4 or later(j, b, 1):
                            act.wait_ge(pv, b * ST + g - 3)
                        act.activation(flat(prob[g % 4]), t_ps[g % 2][:, :],
                                       ACT.Exp).then_inc(exped, 1)
                    if s == 0 and active(j, u, 1):
                        b, o = n - 1, 1 - i
                        act.wait_ge(v_p, b + 1)
                        if later(j, b, 2):
                            act.wait_ge(pv, (b - 1) * ST)
                        act.copy(vb[o][:, :, 0:VW].rearrange("p i (h e) -> p i h e", h=H)[:, :, :, 0:HD],
                                 ps_b[:, 0:T].rearrange("p (i h e) -> p i h e", i=NT, h=H)).then_inc(v_d, 1)
                    if s == 0 and active(j, u, 1):
                        b = n - 1
                        act.wait_ge(sk_p, b + 1)
                        if later(j, b, 1):
                            act.wait_ge(mem_p, b * 3)
                        act.copy(skn[0:SEG, :, :].rearrange("p s f -> p (s f)"),
                                 ps_c[0:SEG, 0:(NS - 1) * P]).then_inc(sk_d, 1)
                    if s == 0 and active(j, u, 3):
                        b = n - 3
                        act.wait_ge(at_p, b + 1)
                        if later(j, b, 1):
                            act.wait_ge(wo_p, b)
                        act.activation(at_b[:, :], ps_a[:, 0:T], ACT.Copy, scale=beta[:, 3:4]).then_inc(at_d, 1)
                    if s == 0 and active(j, u, 0):
                        act.wait_ge(zt_p, n + 1)
                        act.copy(zt[i][:, :], ps_b[:, 0:T]).then_inc(zt_d, 1)
                    if s == 1 and active(j, u, 0):
                        act.wait_ge(kq_p, n + 1)
                        act.copy(kq[i][:, 0, :], ps_a[:, 0:T]).then_inc(kq_d, 1)
                        act.mul(kq[i][:, 1, :], ps_a[:, T:2 * T], HD ** -0.5).then_inc(kq_d, 1)
                    if s == 3 and active(j, u, 0):
                        act.wait_ge(vs_p, n + 1)
                        if later(j, n, 2):
                            act.wait_ge(mem_p, (n - 1) * 3)
                        act.copy(uv[i][0:SEG, :, 0:HV], ps_b[0:SEG, 0:(NS - 1) * P].rearrange("p (s f) -> p s f", f=P)
                                 ).then_inc(vs_d, 1)
                        act.wait_ge(pn_d, (n + 1) * 2)
                        if later(j, n, 1):
                            act.wait_ge(sg_d, n)
                        act.activation(nexp[:, :, :], neg[:, :, :], ACT.Exp).then_inc(nexp_d, 1)
                    for h2 in range(2):
                        if s == MT_AT[h2] and active(j, u, 1):
                            b = n - 1
                            act.wait_ge(mt_p, 2 * b + h2 + 1)
                            if later(j, b, 1):
                                act.wait_ge(mt_out, (2 * b + h2 - 1) * 16)
                            act.copy(mt[h2][:, :], mt_ps).then_inc(mt_d, 1)
                            act.wait_ge(mt_d, 2 * b + h2 + 1)
                            if h2 or later(j, b, 1):
                                act.wait_ge(mt_out, (2 * b + h2) * 16)
                            act.dma_start(m_dram[1 - i, h2], mt[h2][:, :]).then_inc(mt_out, 16)
                    if s == 5 and active(j, u, 3):
                        b = n - 3
                        act.wait_ge(z4_p, b + 1)
                        act.copy(z4t[:, :], ps_b[:, 0:T]).then_inc(z4t_d, 1)

            pipeline(act, body, ahead=1)

        @block.tensor
        def _(pe):
            pe.wait_ge(loaded, N_LOAD * 16)
            pe.wait_ge(const_d, 16)
            pe.wait_ge(mask_d, 3)

            def body(j, u):
                n, i = 2 * j + u, u
                o = 1 - i
                for s in range(ST):
                    lag, g = turn(s)
                    if active(j, u, lag):
                        b, st = n - lag, (i + lag) % 2
                        if g % (ST // 2) == 0:
                            pe.wait_ge(m_in[g // (ST // 2)], (b + 1) * 16)
                        if g >= 2 or later(j, b, 1):
                            pe.wait_ge(exped, b * ST + g - 1)
                        pe.matmul(t_ps[g % 2][:, :], ident16[:, :], causal_t[:, :], start=True, stop=True)
                        for hh in range(2):
                            for t in range(NT):
                                at = (hh * NT + t) * P
                                ts = slice(t * P, (t + 1) * P)
                                mm = pe.matmul(t_ps[g % 2][:, at:at + P], k_st[st][0:KROWS, 2 * g + hh, ts],
                                               q_st[st][0:KROWS, 2 * g + hh, ts], start=False,
                                               stop=True, skip_group_check=True)
                        mm.then_inc(shifted, 1)
                    if S0 <= s < S0 + 4 and active(j, u, 1):
                        b = n - 1
                        if (s - S0) % 2 == 0:
                            pe.wait_ge(stack_in[(s - S0) // 2], (b + 1) * 4 * 16)
                        for t in range(NT):
                            w = 2 * (s - S0) + t
                            ts = slice(t * P, (t + 1) * P)
                            if w >= 2 or later(j, b, 1):
                                pe.wait_ge(maxed, b * ST + w - 1)
                            pe.matmul(s_ps[t][:, :], ident16[:, :], causal[:, :], start=True, stop=True)
                            for c in range(4):
                                h = 4 * (s - S0) + c
                                mm = pe.matmul(s_ps[t][:, c * P:(c + 1) * P], q_st[o][0:MROW, h, ts],
                                               k_st[o][0:MROW, h, ts], start=False, stop=True,
                                               skip_group_check=True)
                            mm.then_inc(score, 1)
                    if s == 0 and active(j, u, 1):
                        b = n - 1
                        pe.wait_ge(sg_d, b + 1)
                        if later(j, b, 1):
                            pe.wait_ge(read_d, b * 9)
                        apart(pe, spare)
                        for c in range(NS - 1):
                            mm = pe.transpose(ps_c[0:SEG, c * P:(c + 1) * P], sg[o][:, c, 0, :], ident[:, :])
                        mm.then_inc(sk_p, 1)
                    lag, g = before(lag, g)
                    if active(j, u, lag):
                        b, st = n - lag, (i + lag) % 2
                        pe.wait_ge(exped, b * ST + g + 1)
                        if g == 0:
                            pe.wait_ge(v_d, b + 1)
                            if later(j, b, 1):
                                pe.wait_ge(ad_d, b * 2)
                        for t in range(NT):
                            for hh in range(2):
                                at = (2 * g + hh) * (HD + 1)
                                mm = pe.matmul(o_ps[:, t * 256 + at:t * 256 + at + WIN],
                                               prob[g % 4][:, hh, t * P:(t + 1) * P],
                                               vb[st][:, t, at:at + WIN], start=True, stop=True)
                        mm.then_inc(pv, 1)
                    if s == 0 and active(j, u, 3):
                        b = n - 3
                        pe.wait_ge(ad_d, (b + 1) * 2)
                        pe.wait_ge(read_d, (b + 1) * 9)
                        free(pe, USES_A, 0, j, u)
                        for t in range(NT):
                            pe.transpose(ps_a[:, t * P:(t + 1) * P], ad[:, t, :], ident[:, :])
                        for c in range(NS - 1):
                            at = T + (c + 1) * SEG
                            mm = pe.transpose(ps_a[:, at:at + SEG], am[o][SEG:P, c, :], ident[SEG:P, SEG:P])
                        mm.then_inc(at_p, 1)
                    if s == 5 and active(j, u, 3):
                        b = n - 3
                        pe.wait_ge(z4_d, (b + 1) * NT)
                        free(pe, USES_B, 3, j, u)
                        for t in range(NT):
                            mm = pe.transpose(ps_b[:, t * P:(t + 1) * P], z4[:, t, :], ident[:, :])
                        mm.then_inc(z4_p, 1)
                    if s in (1, 3, 5) and active(j, u, 1):
                        b, c = n - 1, s // 2
                        if c == 0:
                            pe.wait_ge(sk_d, b + 1)
                            pe.wait_ge(vs_d, b + 1)
                        else:
                            pe.wait_ge(u_d, b * 2 + c)
                        pe.matmul(ps_c[:, 0:MW], skn[:, c, :], uv[o][:, c, :], start=True, stop=True
                                  ).then_inc(mem_p, 1)
                    if s == 0 and active(j, u, 0):
                        pe.wait_ge(z_d, (n + 1) * NT)
                        free(pe, USES_B, 0, j, u)
                        for t in range(NT):
                            mm = pe.transpose(ps_b[:, t * P:(t + 1) * P], z[i][:, t, :], ident[:, :])
                        mm.then_inc(zt_p, 1)
                    if s in (2, 4, 6) and active(j, u, 1):
                        b, c = n - 1, s // 2 - 1
                        pe.wait_ge(mz_d, b * 5 + 2 * c + 1)
                        pe.matmul(ps_c[:, 0:MW], sg[o][:, c + 1, :, :].rearrange("p a t -> p (a t)"), mz[:, :],
                                  start=True, stop=True).then_inc(read_p, 1)
                    if s == 2 and active(j, u, 3):
                        b = n - 3
                        pe.wait_ge(at_d, 2 * (b + 1))
                        free(pe, USES_B, 1, j, u)
                        for t in range(NT):
                            mm = pe.matmul(ps_b[:, t * P:(t + 1) * P], at_b[:, t * P:(t + 1) * P], w_o[:, :],
                                           start=True, stop=True)
                        mm.then_inc(wo_p, 1)
                    if s == 1 and active(j, u, 0):
                        pe.wait_ge(zt_d, n + 1)
                        free(pe, USES_A, 1, j, u)
                        if later(j, n, 1):
                            pe.wait_ge(pn_d, n * 2)
                        pe.matmul(ps_a[:, 0:T], w_kq[:, 0, :], zt[i][:, :], start=True, stop=True)
                        pe.matmul(ps_a[:, T:2 * T], w_kq[:, 1, :], zt[i][:, :], start=True, stop=True
                                  ).then_inc(kq_p, 1)
                    if s == 3 and active(j, u, 0):
                        free(pe, USES_B, 2, j, u)
                        for c in range(NS - 1):
                            mm = pe.matmul(ps_b[0:SEG, c * P:(c + 1) * P], zt[i][:, c * SEG:(c + 1) * SEG], w_v[:, :],
                                           start=True, stop=True)
                        mm.then_inc(vs_p, 1)
                    for h2 in range(2):
                        if s == MT_AT[h2] and active(j, u, 1):
                            b = n - 1
                            pe.wait_ge(mp_d, b * MP + 4 * (h2 + 1))
                            if h2:
                                pe.wait_ge(mt_d, 2 * b + 1)
                            else:
                                free(pe, USES_A, 2, j, u)
                                pe.wait_ge(pn_d, 2 * min(n + 1, NB) if isinstance(j, int) else 2 * (n + 1))
                            for t in range(NT):
                                mm = pe.transpose(mt_ps[:, t * P:(t + 1) * P],
                                                  mpart[:, t, h2, :, :].rearrange("p a h -> p (a h)"), ident16[:, :])
                            mm.then_inc(mt_p, 1)
                    if s == 6 and active(j, u, 3):
                        b = n - 3
                        pe.wait_ge(wc_in, (b + 1) * 16)
                        pe.wait_ge(z4t_d, b + 1)
                        free(pe, USES_B, 4, j, u)
                        for t in range(NT):
                            mm = pe.matmul(ps_b[:, t * P:(t + 1) * P], z4t[:, t * P:(t + 1) * P], wc[o][:, 0, :],
                                           start=True, stop=True)
                        mm.then_inc(g_p, 1)
                    if s == 7 and active(j, u, 0):
                        free(pe, USES_B, 5, j, u)
                        for t in range(NT):
                            mm = pe.matmul(ps_b[:, t * P:(t + 1) * P], zt[i][:, t * P:(t + 1) * P], w_v[:, :],
                                           start=True, stop=True)
                        mm.then_inc(v_p, 1)

            pipeline(pe, body, ahead=1)

        @block.vector
        def _(dve):
            dve.wait_ge(loaded, N_LOAD * 16)

            def link0(k, ins):
                ins.then_inc(beta_d, 1)
                dve.wait_ge(beta_d, k)

            dve.wait_ge(beta_d, 1)
            link0(2, dve.tensor_scalar(beta[:, 1:2], bexp[:, :], 1.0, None, ALU.add))
            link0(3, dve.reciprocal(beta[:, 2:3], beta[:, 1:2]))
            link0(4, dve.tensor_tensor(beta[:, 3:4], bexp[:, :], beta[:, 2:3], ALU.mult))

            def moments(k, b, src):
                for t in range(NT):
                    dve.bn_stats(stats[k][:, t, :], src[:, t, :]).then_inc(stat_d[k], 1)
                for t in range(NT):
                    dve.wait_ge(stat_d[k], b * NT + t + 1)
                    apart(dve, spare)
                    dve.bn_aggr(mv[k][:, t, :], stats[k][:, t, :]).then_inc(mv_d[k], 1)

            def normed(k, b, src, dst, done):
                dve.wait_ge(norm_d[k], 2 * (b + 1))
                for t in range(NT):
                    dve.tensor_scalar(dst[:, t, :], src[:, t, :], mv[k][:, t, 0:1], rs[k][:, t:t + 1],
                                      ALU.subtract, ALU.mult).then_inc(done, 1)

            def body(j, u):
                n, i = 2 * j + u, u
                o = 1 - i

                def split_max(h2):
                    b = n - 1
                    hs = slice(h2 * H // 2, (h2 + 1) * H // 2)
                    dve.wait_ge(maxed, b * ST + 4 * (h2 + 1))
                    if later(j, b, 1):
                        dve.wait_ge(mt_p, 2 * (b - 1) + h2 + 1)

                    def link(k, ins):
                        ins.then_inc(mp_d, 1)
                        dve.wait_ge(mp_d, b * MP + 4 * h2 + k)

                    link(1, dve.tensor_copy(mpart[:, :, h2, 0, :], nmax[:, :, hs]))
                    link(2, dve.tensor_tensor(nrest[:, :, hs], nmax[:, :, hs], mpart[:, :, h2, 0, :], ALU.subtract))
                    link(3, dve.tensor_copy(mpart[:, :, h2, 1, :], nrest[:, :, hs]))
                    link(4, dve.tensor_tensor(mpart[:, :, h2, 2, :], nrest[:, :, hs], mpart[:, :, h2, 1, :],
                                              ALU.subtract))

                for s in range(ST):
                    if s in (3, 5) and active(j, u, 1):
                        split_max(s // 2 - 1)
                    if s == 4 and active(j, u, 3):
                        b = n - 3
                        if later(j, b, 1):
                            dve.wait_ge(z4_p, b)
                        normed(1, b, x3[o], z4, z4_d)
                    if S0 <= s < S0 + 4 and active(j, u, 1):
                        b = n - 1
                        for t in range(NT):
                            w = 2 * (s - S0) + t
                            dve.wait_ge(score, b * ST + w + 1)
                            if w == 0 and later(j, b, 1):
                                dve.wait_ge(mp_d, b * MP)
                            dve.tensor_reduce(nmax[:, t, 4 * (s - S0):4 * (s - S0) + 4],
                                              s_ps[t][:, :].rearrange("p (h k) -> p h k", h=4), AX.X, ALU.max,
                                              negate=True).then_inc(maxed, 1)
                    if s == 0 and active(j, u, 3):
                        b = n - 3
                        dve.wait_ge(at_d, 2 * b + 1)
                        dve.scalar_tensor_tensor(at_b[:, SEG:T], ps_a[:, T + SEG:2 * T], beta[:, 2:3],
                                                 at_b[:, SEG:T], ALU.mult, ALU.add).then_inc(at_d, 1)
                    if s in (1, 3, 5) and active(j, u, 1):
                        b, c = n - 1, s // 2
                        dve.wait_ge(mem_p, b * 3 + c + 1)
                        if c == 0:
                            if later(j, b, 1):
                                dve.wait_ge(read_p, b * 3)
                            dve.tensor_tensor(mz[:, :], ps_c[:, 0:MW], diag[:, :], ALU.mult).then_inc(mz_d, 1)
                        else:
                            dve.tensor_tensor(mzt[:, :], ps_c[:, 0:MW], diag[:, :], ALU.mult).then_inc(mz_d, 1)
                            dve.wait_ge(mz_d, b * 5 + 2 * c)
                            dve.wait_ge(read_p, b * 3 + c)
                            dve.tensor_tensor(mz[:, :], mz[:, :], mzt[:, :], ALU.add).then_inc(mz_d, 1)
                    if s in (2, 4, 6) and active(j, u, 1):
                        b, c = n - 1, s // 2 - 1
                        dve.wait_ge(read_p, b * 3 + c + 1)
                        if c == 0 and later(j, b, 2):
                            dve.wait_ge(at_p, b - 1)

                        def link(k, ins):
                            ins.then_inc(read_d, 1)
                            dve.wait_ge(read_d, b * 9 + 3 * c + k)

                        link(1, dve.tensor_scalar(dn[:, c, :], ps_c[:, HV:MW], 1e-6, None, ALU.add))
                        link(2, dve.reciprocal(dr[:, c, :], dn[:, c, :]))
                        link(3, dve.tensor_tensor(am[o][:, c, :].rearrange("p (h e) -> p h e", h=H),
                                                  ps_c[:, 0:HV].rearrange("p (h e) -> p h e", h=H),
                                                  dr[:, c, :].unsqueeze(2).broadcast_to([P, H, HD]), ALU.mult))
                        if c < 2:
                            dve.tensor_tensor(uv[o][0:SEG, c + 1, 0:HV], uv[o][0:SEG, c + 1, 0:HV],
                                              am[o][0:SEG, c, :], ALU.subtract).then_inc(u_d, 1)
                    if s == 2 and active(j, u, 3):
                        b = n - 3
                        dve.wait_ge(wo_p, b + 1)
                        dve.wait_ge(xt_in, (b + 1) * 16)
                        if later(j, b, 2):
                            dve.wait_ge(xb_d, b - 1)
                        dve.tensor_tensor(flat(x3[o]), ps_b[:, 0:T], flat(xt[o]), ALU.add).then_inc(x3_d, 1)
                        dve.wait_ge(x3_d, b + 1)
                        if later(j, b, 1):
                            dve.wait_ge(norm_d[1], 2 * b)
                        moments(1, b, x3[o])
                    if s == 1 and active(j, u, 0):
                        dve.wait_ge(kq_d, (n + 1) * 2)
                        if later(j, n, 1):
                            dve.wait_ge(sg_d, n)
                        dve.tensor_scalar(flat(pos), ps_a[:, :], 0.0, None, ALU.max).then_inc(pn_d, 1)
                        dve.tensor_scalar(flat(neg), ps_a[:, :], 0.0, None, ALU.min).then_inc(pn_d, 1)
                    if s == 6 and active(j, u, 3):
                        b = n - 3
                        dve.wait_ge(g_p, b + 1)
                        dve.wait_ge(xb_d, b + 1)
                        if later(j, b, 2):
                            dve.wait_ge(x4_out, (b - 1) * 16)
                        dve.tensor_tensor(flat(x4[o]), ps_b[:, 0:T], flat(xb[o]), ALU.add).then_inc(x4_d, 1)
                    if s == 5 and active(j, u, -1):
                        dve.wait_ge(x_in, (n + 2) * 16)
                        if later(j, n, 0):
                            dve.wait_ge(norm_d[0], 2 * (n + 1))
                        moments(0, n + 1, x[o])
                    if s == 7 and active(j, u, -1):
                        if later(j, n, 1):
                            dve.wait_ge(zt_p, n)
                        normed(0, n + 1, x[o], z[o], z_d)
                    if s == 7 and active(j, u, 2):
                        b = n - 2
                        dve.wait_ge(pv, (b + 1) * ST)
                        if later(j, b, 1):
                            dve.wait_ge(at_p, b)
                        out = o_ps[:, :].rearrange("p (i c) -> p i c", i=NT)[:, :, 0:VW].rearrange(
                            "p i (h e) -> p i h e", h=H)
                        dve.reciprocal(dinv[:, :, :], out[:, :, :, HD]).then_inc(ad_d, 1)
                        dve.wait_ge(ad_d, 2 * b + 1)
                        dve.tensor_tensor(ad[:, :, :].rearrange("p i (h e) -> p i h e", h=H), out[:, :, :, 0:HD],
                                          dinv[:, :, :].unsqueeze(3).broadcast_to([P, NT, H, HD]), ALU.mult
                                          ).then_inc(ad_d, 1)

            pipeline(dve, body, ahead=1)


def program(nc, d):
    attention_a(nc, d)
    fold_ffn(nc, d)
    dense(nc, d)
    attention_b(nc, d)


def laid_out(I):
    import numpy as np

    a = lambda k: np.asarray(I[f"L0_attn_a_{k}"])
    b = lambda k: np.asarray(I[f"L0_attn_b_{k}"])
    f = lambda k: np.asarray(I[f"L0_ffn_{k}"])
    on_rows = lambda v: np.broadcast_to(v, (P, v.shape[0]))
    dh = np.arange(P).reshape(H, HD).T.ravel()
    ws = a("Ws")[0]
    sel_qv = np.zeros((H, QK, H), np.float32)
    sel_v = np.zeros((R, HD, R), np.float32)
    for h in range(H):
        sel_qv[h, :, h] = ws[:QK]
    for r in range(R):
        sel_v[r, :, r] = ws[QK:]
    t = np.arange(P)
    seen = (t[:, None] // 64 == t[None] // 64) & (t[None] <= t[:, None])
    causal = np.where(seen, 0.0, -2.0 ** 100).astype(np.float32)
    diag = np.concatenate([(t % H)[:, None] == (t // HD)[None], (t % H)[:, None] == np.arange(H)[None]], 1)
    out = {
        "x": a("x"),
        "a_Wq": a("Wq")[dh].T, "a_Wk": a("Wk")[dh].T, "a_Wv_t": a("Wv").T, "a_Wv": a("Wv"), "a_Wqv": a("Wqv"),
        "a_bv_b": on_rows(a("bv")), "a_bv_r": np.broadcast_to(a("bv")[:, None], (RD, P)),
        "a_bqv_b": np.broadcast_to(a("bqv")[:, None], (QK * H, P)),
        "a_sel_qv": sel_qv.reshape(QK * H, H), "a_sel_v": sel_v.reshape(RD, R),
        "a_cols": np.stack([a("bq")[dh], a("bk")[dh], a("g1"), a("b1"), np.broadcast_to(a("bs"), P)], 1),
        "a_Wf_t": a("Wf").T, "a_Wr1_t": a("Wr1").T, "a_Wr2_t": a("Wr2").T,
        "a_bf_b": on_rows(a("bf")), "a_br2_b": on_rows(a("br2")),
        "b_cols": np.stack([a("br1")[:P], a("br1")[P:], a("g2"), a("b2")], 1),
        "W1": f("W1"), "W2_t": f("W2").transpose(0, 2, 1),
        "ffn_b": np.concatenate([f("b1").reshape(NG, NI, P).transpose(0, 2, 1), f("b2")[:, :, None]], 2),
        "b_Wkq_t": np.concatenate([b("W_k")[dh].T, b("W_q")[dh].T], 1),
        "b_Wv_t": b("W_v").T, "b_Wo_t": b("W_o").T, "b_beta": np.repeat(b("beta_param"), HD)[:, None],
        "ident": np.eye(P, dtype=np.float32),
        "causal": np.concatenate([causal, causal.T], 1),
        "diag": diag.astype(np.float32),
    }
    return {k: np.ascontiguousarray(v) for k, v in out.items()}


SCRATCH = {
    "a_parts_dram": ((2, 2 * NPART, P, T), BF16), "a_m_dram": ((2, 2, NPART * H // 2, T), BF16),
    "c_parts_dram": ((2, 2 * NPART, P, T), BF16), "c_m_dram": ((2, 2, NPART * H // 2, T), BF16),
    "y": ((NB, T, P), F32), "ao": ((NB, T, P), F32), "x2": ((NB, T, P), F32),
    "folded": ((NB // 2, P, 2 * P), F32),
}


def kernel(**inputs):
    import numpy as np
    import concourse.bacc as bacc
    from concourse.bass_utils import run_bass_kernel_spmd

    nc = bacc.Bacc("TRN2", target_bir_lowering=False, num_devices=1)
    arrays, d = {}, {}
    for name, a in laid_out(inputs).items():
        arrays[f"in_{name}"] = a
        d[name] = nc.dram_tensor(f"in_{name}", a.shape, mybir.dt.from_np(a.dtype), kind="ExternalInput").ap()
    for name, (shape, dt) in SCRATCH.items():
        d[name] = nc.dram_tensor(f"scratch_{name}", shape, dt, kind="Internal").ap()
    d["out"] = nc.dram_tensor("out", (NB, T, P), F32, kind="ExternalOutput").ap()
    program(nc, d)
    return run_bass_kernel_spmd(nc, [arrays], core_ids=[0]).results[0]["out"]
```

```python
import concourse.bass as bass
import concourse.mybir as mybir
from contextlib import ExitStack

F32 = mybir.dt.float32
BF16 = mybir.dt.bfloat16
ALU = mybir.AluOpType
ACT = mybir.ActivationFunctionType
AX = mybir.AxisListType

P = 128
NB, T = 32, 256
NT = T // P
H, HD, R, QK = 16, 8, 8, 32
RD = R * HD
NPART = 3
SROWS = NPART * NPART * HD
MROW = 96
KROWS = MROW + NPART
VC = 96
CV, CC, CS, CQ = 0, RD, RD + R, RD + R + 1
EPS = 1e-5
NG, NI = 8, 4
LAGS = 4
PEELED = 6


def active(j, u, lag, total=NB):
    return not isinstance(j, int) or 0 <= 2 * j + u - lag < total


def pair(j, u, lag):
    return j + (u - lag) // 2, (u - lag) % 2


def pipeline(eng, body, total=NB, stages=LAGS, ahead=0):
    for n in range(-ahead, PEELED):
        body(n // 2, n % 2)
    end = total // 2 - ahead
    with eng.Fori(PEELED // 2, end) as j:
        body(j, 0)
        body(j, 1)
    for n in range(2 * end, total + stages - 1):
        body(n // 2, n % 2)


def apart(eng, spare):
    eng.sem_inc(spare, 1)


def memory(nc, ctx, prefix):
    def sb(name, shape, dt=F32):
        return ctx.enter_context(nc.sbuf_tensor(f"{prefix}_{name}", shape, dt))

    def sem(name):
        return ctx.enter_context(nc.semaphore(f"{prefix}_{name}"))

    return sb, sem


def attention_a(nc, d):
    ctx = ExitStack()
    with ctx:
        def sb(name, shape, dt=F32):
            return ctx.enter_context(nc.sbuf_tensor(name, shape, dt))

        def sem(name):
            return ctx.enter_context(nc.semaphore(name))

        w_q = sb("a_w_q", [P, P])
        w_k = sb("a_w_k", [P, P])
        w_v = sb("a_w_v", [P, VC])
        b_v = sb("a_b_v", [P, VC])
        w_qv = sb("a_w_qv", [P, 4, P])
        w_vn = sb("a_w_vn", [RD, P])
        s_qv = sb("a_s_qv", [P, 4, H])
        s_v = sb("a_s_v", [RD, R])
        b_qv = sb("a_b_qv", [P, 4, P])
        b_vr = sb("a_b_vr", [RD, P])
        cols = sb("a_cols", [P, 5])
        b_qs = sb("a_b_qs", [P, 1])
        ident = sb("a_ident", [P, P])
        ident16 = sb("a_ident16", [P, P], BF16)
        half = sb("a_half", [P, NT])
        w1 = [sb(f"a_w1_{i}", [P, 2, NI, P]) for i in range(2)]
        w2 = [sb(f"a_w2_{i}", [P, 2, NI, P]) for i in range(2)]
        b1 = sb("a_b1", [P, NG, NI])
        b2 = sb("a_b2", [1, NG, P])
        one_row = sb("a_one_row", [1, P])
        ffn = [sb(f"a_ffn{i}", [P, 2, 2 * P]) for i in range(2)]
        x = [sb(f"a_x{i}", [P, NT, P]) for i in range(2)]
        y = [sb(f"a_y{i}", [P, NT, P]) for i in range(2)]
        z = [sb(f"a_z{i}", [P, NT, P]) for i in range(2)]
        stats = sb("a_stats", [P, NT, 6])
        mv = sb("a_mv", [P, NT, 2])
        r1 = sb("a_r1", [P, NT])
        r2 = sb("a_r2", [P, NT])
        rt = sb("a_rt", [P, 4, NT])
        xn = [sb(f"a_xn{i}", [P, T]) for i in range(2)]
        qk = [sb(f"a_qk{i}", [P, 2, T]) for i in range(2)]
        rest = sb("a_rest", [P, 2, T])
        parts = [sb(f"a_parts{i}", [P, 2, NPART, T], BF16) for i in range(2)]
        q_st = [sb(f"a_q_st{i}", [P, H, T], BF16) for i in range(2)]
        k_st = [sb(f"a_k_st{i}", [P, H, T], BF16) for i in range(2)]
        vp = [sb(f"a_vp{i}", [P, NT, VC]) for i in range(2)]
        nmax = sb("a_nmax", [P, NT, H])
        nrest = sb("a_nrest", [P, NT, H])
        mpart = sb("a_mpart", [P, NT, 2, NPART, H // 2], BF16)
        mt = [sb(f"a_mt{i}", [NPART * H // 2, T], BF16) for i in range(2)]
        prob = [sb(f"a_prob{i}", [P, NT, T]) for i in range(4)]
        ov = [sb(f"a_ov{i}", [P, H * NT, RD + R + 1]) for i in range(2)]
        inv = sb("a_inv", [P, H * NT])
        comp = sb("a_comp", [P, H * NT, R])
        comp2 = sb("a_comp2", [P, H * NT, R])
        cmax = sb("a_cmax", [P, H * NT])
        comp3 = sb("a_comp3", [P, H * NT, R])
        cexp = sb("a_cexp", [P, H * NT, R])
        csum = sb("a_csum", [P, H * NT])
        cinv = sb("a_cinv", [P, H * NT])
        cw = sb("a_cw", [P, H * NT])
        wgt = sb("a_wgt", [P, H * NT, R])
        prod = sb("a_prod", [P, H * NT, RD])
        ao = [sb(f"a_ao{i}", [P, NT, P]) for i in range(2)]
        bank = [ctx.enter_context(nc.psum_tensor(f"a_bank{i}", [P, 512], F32)) for i in range(8)]
        zv_ps, qk_ps, s_ps, t_ps, o_ps = bank[0], bank[1], bank[2:4], bank[4:6], bank[6:8]
        mt_ps = qk_ps[0:NPART * H // 2, 0:T // 2].bitcast(BF16)

        spare = sem("a_spare")
        loaded = sem("a_loaded")
        loaded_v = sem("a_loaded_v")
        half_d = sem("a_half_d")
        ones_d = sem("a_ones_d")
        zeros_d = sem("a_zeros_d")
        ffn_b_in = sem("a_ffn_b_in")
        ffn_in = [sem(f"a_ffn_in{i}") for i in range(2)]
        ffn_p = sem("a_ffn_p")
        ffn_d = sem("a_ffn_d")
        ffn_out = sem("a_ffn_out")
        blank = sem("a_blank")
        fold_p = sem("a_fold_p")
        folded = sem("a_folded")
        x_in = sem("a_x_in")
        stats_d = sem("a_stats_d")
        mv_d = sem("a_mv_d")
        norm_d = sem("a_norm_d")
        y_d = sem("a_y_d")
        z_d = sem("a_z_d")
        z_t = sem("a_z_t")
        xn_d = sem("a_xn_d")
        qk_p = sem("a_qk_p")
        qk_d = sem("a_qk_d")
        split_d = sem("a_split_d")
        parts_out = sem("a_parts_out")
        stack_in = [sem(f"a_stack_in{i}") for i in range(2)]
        v_p = sem("a_v_p")
        v_d = sem("a_v_d")
        score = sem("a_score")
        maxed = sem("a_maxed")
        mp_d = sem("a_mp_d")
        mt_p = sem("a_mt_p")
        mt_d = sem("a_mt_d")
        mt_out = sem("a_mt_out")
        m_in = [sem(f"a_m_in{i}") for i in range(2)]
        shifted = sem("a_shifted")
        exped = sem("a_exped")
        pv = sem("a_pv")
        ov_d = sem("a_ov_d")
        post = sem("a_post")
        cexp_d = sem("a_cexp_d")
        prod_d = sem("a_prod_d")
        ao_d = sem("a_ao_d")
        y_out = sem("a_y_out")
        ao_out = sem("a_ao_out")

        parts_dram = d["a_parts_dram"]
        m_dram = d["a_m_dram"]
        pairs = lambda a: a.rearrange("(j u) (i p) f -> j u p i f", u=2, p=P)
        x_dram, y_dram, ao_dram = pairs(d["x"]), pairs(d["y"]), pairs(d["ao"])
        SPLIT, NORM, MP, POST = 4, 7, 8, 9
        OFF = 11
        S_AT = (1, 2, 3, 4, 6, 7, 8, 9)
        MT_AT = (6, 11)
        N_LOAD, N_LOAD_V = 4, 8
        FOLD_AT = range(1, 1 + NG // 2)

        block = ctx.enter_context(nc.Block())

        @block.sync
        def _(sp):
            def load_weights():
                for dst, src in ((ident[:, :], d["ident"]), (cols[:, :], d["a_cols"]),
                                 (w_q[:, :], d["a_Wq"]), (w_k[:, :], d["a_Wk"])):
                    sp.dma_start(dst, src).then_inc(loaded, 16)
                for dst, src in ((w_v[:, 0:RD], d["a_Wv_t"]), (b_v[:, 0:RD], d["a_bv_b"]),
                                 (w_qv[:, :, :], d["a_Wqv"].rearrange("(c p) f -> p c f", p=P)),
                                 (w_vn[:, :], d["a_Wv"]),
                                 (s_qv[:, :, :], d["a_sel_qv"].rearrange("(c p) f -> p c f", p=P)),
                                 (s_v[:, :], d["a_sel_v"]),
                                 (b_qv[:, :, :], d["a_bqv_b"].rearrange("(c p) f -> p c f", p=P)),
                                 (b_vr[:, :], d["a_bv_r"])):
                    sp.dma_start(dst, src).then_inc(loaded_v, 16)
                sp.dma_start(b1[:, :, :], d["ffn_b1"]).then_inc(ffn_b_in, 16)
                sp.dma_start(b2[:, :, :], d["ffn_b2"]).then_inc(ffn_b_in, 16)

            def load_ffn(q):
                if q >= 2:
                    sp.wait_ge(ffn_p, q - 1)
                for dst, src in ((w1, "W1"), (w2, "W2_t")):
                    sp.dma_start(dst[q % 2][:, :, :, :],
                                 d[src][2 * q:2 * q + 2].rearrange("g (c p) f -> p g c f", p=P)
                                 ).then_inc(ffn_in[q % 2], 16)

            def store_ffn(q):
                sp.wait_ge(ffn_d, q + 1)
                if q:
                    sp.wait_ge(ffn_out, q * 32)
                for c in range(2):
                    sp.dma_start(d["folded"].rearrange("(q g c) p f -> q c p g f", g=2, c=2)[q, c],
                                 ffn[q % 2][:, :, :]).then_inc(ffn_out, 16)

            def body(j, u):
                n = 2 * j + u
                i = u
                if active(j, u, -1):
                    if not isinstance(j, int) or n >= 1:
                        sp.wait_ge(z_d, n * NT)
                        apart(sp, spare)
                    if not isinstance(j, int) or n >= 0:
                        sp.wait_ge(x_in, (n + 1) * 16)
                        apart(sp, spare)
                    at = pair(j, u, -1)
                    sp.dma_start(x[1 - i][:, :, :], x_dram[at[0], at[1]]).then_inc(x_in, 16)
                if isinstance(j, int) and n == -1:
                    load_weights()

                def shift_rows(half_):
                    b, o = n - 1, 1 - i
                    sp.wait_ge(mt_d, 2 * b + half_ + 1)
                    apart(sp, spare)
                    sp.dma_start(m_dram[o, half_], mt[half_][:, :]).then_inc(mt_out, 16)
                    sp.wait_ge(mt_out, (2 * b + half_ + 1) * 16)
                    apart(sp, spare)
                    hs = slice(half_ * H // 2, (half_ + 1) * H // 2)
                    sp.dma_start(q_st[o][MROW:KROWS, hs, :],
                                 m_dram[o, half_].rearrange("(a h) t -> a h t", a=NPART)).then_inc(m_in[half_], 16)

                if active(j, u, 0):
                    sp.wait_ge(y_d, (n + 1) * NT)
                    apart(sp, spare)
                    sp.wait_ge(y_out, n * 16)
                    apart(sp, spare)
                    at = pair(j, u, 0)
                    sp.dma_start(y_dram[at[0], at[1]], y[i][:, :, :]).then_inc(y_out, 16)
                if isinstance(j, int) and n + 1 in FOLD_AT:
                    load_ffn(n)
                if active(j, u, 1):
                    shift_rows(0)
                if active(j, u, 0):
                    sp.wait_ge(split_d, (n + 1) * SPLIT)
                    apart(sp, spare)
                    sp.dma_start(parts_dram[i].rearrange("c p t -> p c t"),
                                 parts[i][:, :, :, :].rearrange("p q c t -> p (q c) t")).then_inc(parts_out, 16)
                if active(j, u, 0):
                    sp.wait_ge(parts_out, (n + 1) * 16)
                    apart(sp, spare)
                    if isinstance(j, int) and n < 2:
                        sp.wait_ge(zeros_d, 2 * (n + 1))
                    for half_ in range(2):
                        hs = slice(half_ * H // 2, (half_ + 1) * H // 2)
                        if not isinstance(j, int) or n >= 2:
                            sp.wait_ge(shifted, (n - 2) * H + (half_ + 1) * H // 2)
                            apart(sp, spare)
                        for a in range(NPART):
                            sp.dma_start(q_st[i][a * NPART * HD:(a + 1) * NPART * HD, hs, :],
                                         parts_dram[i, a].rearrange("(d h) t -> d h t", d=HD)[:, hs].unsqueeze(0)
                                         .broadcast_to([NPART, HD, H // 2, T])).then_inc(stack_in[half_], 16)
                        sp.dma_start(k_st[i][0:SROWS, hs, :],
                                     parts_dram[i, NPART:2 * NPART].rearrange("c (d h) t -> (c d) h t", d=HD)[:, hs]
                                     .unsqueeze(0).broadcast_to([NPART, NPART * HD, H // 2, T])
                                     ).then_inc(stack_in[half_], 16)
                if active(j, u, 1):
                    shift_rows(1)
                if active(j, u, 3):
                    at = pair(j, u, 3)
                    sp.wait_ge(ao_d, (n - 2) * NT)
                    apart(sp, spare)
                    sp.wait_ge(ao_out, (n - 3) * 16)
                    apart(sp, spare)
                    sp.dma_start(ao_dram[at[0], at[1]], ao[1 - i][:, :, :]).then_inc(ao_out, 16)
                if isinstance(j, int) and n in FOLD_AT:
                    store_ffn(n - 1)

            pipeline(sp, body, ahead=1)
            sp.wait_ge(y_out, NB * 16)
            sp.wait_ge(ao_out, NB * 16)
            sp.wait_ge(ffn_out, NG * 16)

        @block.gpsimd
        def _(pool):
            pool.memset(half[:, :], -0.5).then_inc(half_d, 1)
            pool.wait_ge(half_d, 1)

            def body(j, u):
                n = 2 * j + u
                i = u
                if active(j, u, 3):
                    b, o = n - 3, 1 - i
                    pool.wait_ge(post, (b + 1) * POST)
                    if not isinstance(j, int) or n >= 4:
                        pool.wait_ge(ao_d, b * NT)
                    pool.tensor_tensor(
                        prod[:, :, :].rearrange("p g (r e) -> p g r e", r=R),
                        ov[o][:, :, 0:RD].rearrange("p g (r e) -> p g r e", r=R),
                        wgt[:, :, :].unsqueeze(3).broadcast_to([P, H * NT, R, HD]), ALU.mult).then_inc(prod_d, 1)
                if active(j, u, 0):
                    pool.wait_ge(qk_d, (n + 1) * 2)
                    if not isinstance(j, int) or n >= 2:
                        pool.wait_ge(parts_out, (n - 1) * 16)

                    def split(k, ins):
                        ins.then_inc(split_d, 1)
                        pool.wait_ge(split_d, n * SPLIT + k)
                        apart(pool, spare)

                    apart(pool, spare)
                    split(1, pool.tensor_scalar(parts[i][:, :, 0, :], qk[i][:, :, :], 1.0, 0.0, ALU.mult, ALU.add))
                    split(2, pool.tensor_tensor(rest[:, :, :], qk[i][:, :, :], parts[i][:, :, 0, :], ALU.subtract))
                    split(3, pool.tensor_scalar(parts[i][:, :, 1, :], rest[:, :, :], 1.0, 0.0, ALU.mult, ALU.add))
                    split(4, pool.tensor_tensor(parts[i][:, :, 2, :], rest[:, :, :], parts[i][:, :, 1, :],
                                                ALU.subtract))
                if active(j, u, -1):
                    pool.wait_ge(mv_d, (n + 2) * NT)
                    if not isinstance(j, int) or n >= 0:
                        pool.wait_ge(z_d, (n + 1) * NT)

                    def norm(k, ins):
                        ins.then_inc(norm_d, 1)
                        pool.wait_ge(norm_d, (n + 1) * NORM + k)
                        apart(pool, spare)

                    apart(pool, spare)
                    norm(1, pool.tensor_scalar(rt[:, 0, :], mv[:, :, 1], EPS, None, ALU.add))
                    norm(2, pool.tensor_tensor(r1[:, :], rt[:, 0, :], half[:, :], ALU.pow))
                    norm(3, pool.tensor_tensor(rt[:, 1, :], r1[:, :], r1[:, :], ALU.mult))
                    norm(4, pool.tensor_tensor(rt[:, 2, :], rt[:, 1, :], mv[:, :, 1], ALU.mult))
                    norm(5, pool.tensor_scalar(rt[:, 3, :], rt[:, 2, :], EPS, None, ALU.add))
                    norm(6, pool.tensor_tensor(rt[:, 1, :], rt[:, 3, :], half[:, :], ALU.pow))
                    norm(7, pool.tensor_tensor(r2[:, :], rt[:, 1, :], r1[:, :], ALU.mult))
                if isinstance(j, int) and 0 <= n < 2:
                    pool.memset(k_st[i][MROW:P, :, :], 1.0).then_inc(ones_d, 1)
                    pool.wait_ge(ones_d, n + 1)

            pipeline(pool, body, ahead=1)

        @block.scalar
        def _(act):
            act.wait_ge(loaded, N_LOAD * 16)
            act.mul(b_qs[:, :], cols[:, 0:1], HD ** -0.5).then_inc(folded, 1)
            act.copy(ident16[:, :], ident[:, :]).then_inc(folded, 1)

            def values_weights():
                act.wait_ge(fold_p, 1)
                act.wait_ge(blank, 3)
                act.copy(w_v[:, CC:CS], bank[0][:, 0:R]).then_inc(folded, 1)
                act.mul(w_v[:, CQ:CQ + H], bank[0][:, 16:16 + H], QK ** -0.5).then_inc(folded, 1)
                act.copy(b_v[:, CC:CS], bank[0][:, 32:32 + R]).then_inc(folded, 1)
                act.activation(b_v[:, CQ:CQ + H], bank[0][:, 48:48 + H], ACT.Identity, scale=QK ** -0.5,
                               bias=cols[:, 4:5]).then_inc(folded, 1)

            def body(j, u):
                n = 2 * j + u
                i = u
                for s in range(H):
                    if s == 2 and active(j, u, 0):
                        act.wait_ge(z_t, n + 1)
                        act.activation(xn[i][:, :], zv_ps[:, 0:T], ACT.Identity, scale=cols[:, 2:3],
                                       bias=cols[:, 3:4]).then_inc(xn_d, 1)
                    if s == 4 and active(j, u, 0):
                        act.wait_ge(qk_p, n + 1)
                        act.activation(qk[i][:, 0, :], qk_ps[:, 0:T], ACT.Identity, scale=HD ** -0.5,
                                       bias=b_qs[:, 0:1]).then_inc(qk_d, 1)
                        act.activation(qk[i][:, 1, :], qk_ps[:, T:2 * T], ACT.Identity,
                                       bias=cols[:, 1:2]).then_inc(qk_d, 1)
                    if s == 0 and isinstance(j, int) and n in FOLD_AT:
                        act.wait_ge(ffn_p, n)
                        if n > 2:
                            act.wait_ge(ffn_out, (n - 2) * 32)
                        act.copy(ffn[(n - 1) % 2][:, :, :].rearrange("p g f -> p (g f)"), zv_ps[:, :]
                                 ).then_inc(ffn_d, 1)
                    if s == 9 and isinstance(j, int) and n == 0:
                        values_weights()
                    for half_ in range(2):
                        if s == MT_AT[half_] and active(j, u, 1):
                            b = n - 1
                            act.wait_ge(mt_p, 2 * b + half_ + 1)
                            if not isinstance(j, int) or b >= 1:
                                act.wait_ge(mt_out, (2 * b + half_ - 1) * 16)
                            act.copy(mt[half_][:, :], mt_ps).then_inc(mt_d, 1)
                    lag, h = (1, s - OFF) if s >= OFF else (2, s + H - OFF)
                    b = n - lag
                    if active(j, u, lag):
                        act.wait_ge(shifted, b * H + h + 1)
                        if h >= 4 or not isinstance(j, int) or b >= 1:
                            act.wait_ge(pv, b * H + h - 3)
                        act.activation(prob[h % 4][:, :, :].rearrange("p a b -> p (a b)"), t_ps[h % 2][:, :],
                                       ACT.Exp).then_inc(exped, 1)
                    lag, g = (lag, h // 2 - 1) if h >= 2 else (lag + 1, H // 2 - 1)
                    b = n - lag
                    if h % 2 == 0 and active(j, u, lag):
                        act.wait_ge(pv, b * H + 2 * g + 2)
                        if g == 0 and (not isinstance(j, int) or b >= 2):
                            act.wait_ge(prod_d, b - 1)
                        act.copy(ov[(i + lag) % 2][:, 4 * g:4 * g + 4, :],
                                 o_ps[g % 2][:, 0:4 * VC].rearrange("p (g c) -> p g c", g=4)[:, :, 0:CQ]
                                 ).then_inc(ov_d, 1)
                    if s == 15 and active(j, u, 2):
                        act.wait_ge(post, (n - 2) * POST + 5)
                        if not isinstance(j, int) or n >= 3:
                            act.wait_ge(post, (n - 2) * POST)
                        act.activation(cexp[:, :, :], comp3[:, :, :], ACT.Exp).then_inc(cexp_d, 1)

            pipeline(act, body, ahead=1)

        @block.tensor
        def _(pe):
            pe.wait_ge(loaded, N_LOAD * 16)
            pe.wait_ge(folded, 2)

            def values_weights():
                pe.wait_ge(loaded_v, N_LOAD_V * 16)
                pe.wait_ge(xn_d, 1)
                pe.matmul(bank[0][:, 0:R], w_vn[:, :], s_v[:, :], start=True, stop=True)
                for c in range(4):
                    pe.matmul(bank[0][:, 16:16 + H], w_qv[:, c, :], s_qv[:, c, :], start=c == 0, stop=c == 3)
                pe.matmul(bank[0][:, 32:32 + R], b_vr[:, :], s_v[:, :], start=True, stop=True)
                for c in range(4):
                    mm = pe.matmul(bank[0][:, 48:48 + H], b_qv[:, c, :], s_qv[:, c, :], start=c == 0, stop=c == 3)
                mm.then_inc(fold_p, 1)
                pe.wait_ge(folded, 6)

            def fold(q):
                if q == 0:
                    pe.wait_ge(ffn_b_in, 32)
                    pe.wait_ge(blank, 4)
                pe.wait_ge(ffn_in[q % 2], (q // 2 + 1) * 32)
                for g in range(2):
                    at = 2 * g * P
                    for c in range(NI):
                        pe.matmul(zv_ps[:, at:at + P], w1[q % 2][:, g, c, :], w2[q % 2][:, g, c, :],
                                  start=c == 0, stop=c == NI - 1)
                    at += P
                    for c in range(NI):
                        pe.matmul(zv_ps[:, at:at + P], b1[:, 2 * q + g, c:c + 1].broadcast_to([P, P]),
                                  w2[q % 2][:, g, c, :], start=c == 0, stop=False)
                    mm = pe.matmul(zv_ps[:, at:at + P], one_row[:, :], b2[:, 2 * q + g, :], start=False, stop=True)
                mm.then_inc(ffn_p, 1)

            def body(j, u):
                n = 2 * j + u
                i = u

                def score_unit(s, t):
                    if s in S_AT and active(j, u, 1):
                        b, o, g = n - 1, 1 - i, S_AT.index(s)
                        if g % (H // 4) == 0 and t == 0:
                            pe.wait_ge(stack_in[g // (H // 4)], (b + 1) * 4 * 16)
                        w = 2 * g + t
                        if w >= 2 or not isinstance(j, int) or b >= 1:
                            pe.wait_ge(maxed, b * H + w - 1)
                        for hh in range(2):
                            mm = pe.matmul(s_ps[t][:, hh * T:(hh + 1) * T],
                                           q_st[o][0:MROW, 2 * g + hh, t * P:(t + 1) * P],
                                           k_st[o][0:MROW, 2 * g + hh, :], start=True, stop=True)
                        mm.then_inc(score, 1)

                for s in range(H):
                    if s == 0 and isinstance(j, int) and n in FOLD_AT:
                        pe.wait_ge(v_d, n)
                        fold(n - 1)
                    if s == 9 and isinstance(j, int) and n == 0:
                        values_weights()
                    if s == 1 and active(j, u, 0):
                        if isinstance(j, int) and n in FOLD_AT:
                            pe.wait_ge(ffn_d, n)
                        pe.wait_ge(z_d, (n + 1) * NT)
                        if not isinstance(j, int) or n >= 1:
                            pe.wait_ge(v_d, n)
                        for t in range(NT):
                            mm = pe.transpose(zv_ps[:, t * P:(t + 1) * P], z[i][:, t, :], ident[:, :])
                        mm.then_inc(z_t, 1)
                    if s == 3 and active(j, u, 0):
                        pe.wait_ge(xn_d, n + 1)
                        if not isinstance(j, int) or n >= 2:
                            pe.wait_ge(mt_d, 2 * (n - 1))
                        pe.matmul(qk_ps[:, 0:T], w_q[:, :], xn[i][:, :], start=True, stop=True)
                        pe.matmul(qk_ps[:, T:2 * T], w_k[:, :], xn[i][:, :], start=True, stop=True).then_inc(qk_p, 1)
                    if s == 10 and active(j, u, 0):
                        for t in range(NT):
                            mm = pe.matmul(zv_ps[:, t * VC:(t + 1) * VC], xn[i][:, t * P:(t + 1) * P], w_v[:, :],
                                           start=True, stop=True)
                        mm.then_inc(v_p, 1)
                    score_unit(s, 0)
                    for half_ in range(2):
                        if s == MT_AT[half_] and active(j, u, 1):
                            b = n - 1
                            pe.wait_ge(mp_d, b * MP + 4 * (half_ + 1))
                            pe.wait_ge(qk_d, min(n + 1, NB) * 2 if isinstance(j, int) else (n + 1) * 2)
                            if half_ or not isinstance(j, int) or b >= 1:
                                pe.wait_ge(mt_d, 2 * b + half_)
                            for t in range(NT):
                                mm = pe.transpose(mt_ps[:, t * P:(t + 1) * P],
                                                  mpart[:, t, half_, :, :].rearrange("p a h -> p (a h)"),
                                                  ident16[:, :])
                            mm.then_inc(mt_p, 1)
                    lag, h = (1, s - OFF) if s >= OFF else (2, s + H - OFF)
                    if active(j, u, lag):
                        b, o = n - lag, (i + lag) % 2
                        if isinstance(b, int) and b < 2 and h == 0:
                            pe.wait_ge(ones_d, b + 1)
                        if h % (H // 2) == 0:
                            pe.wait_ge(m_in[h // (H // 2)], (b + 1) * 16)
                        if h >= 2 or not isinstance(j, int) or b >= 1:
                            pe.wait_ge(exped, b * H + h - 1)
                        for c in range(NT):
                            mm = pe.matmul(t_ps[h % 2][:, c * T:(c + 1) * T],
                                           k_st[o][0:KROWS, h, c * P:(c + 1) * P], q_st[o][0:KROWS, h, :],
                                           start=True, stop=True)
                        mm.then_inc(shifted, 1)
                    score_unit(s, 1)
                    lag, h = (lag, h - 1) if h else (lag + 1, H - 1)
                    if active(j, u, lag):
                        b, o = n - lag, (i + lag) % 2
                        g = h // 2
                        pe.wait_ge(exped, b * H + h + 1)
                        if h == 0:
                            pe.wait_ge(v_d, b + 1)
                        if h % 2 == 0 and (g >= 2 or not isinstance(j, int) or b >= 1):
                            pe.wait_ge(ov_d, b * (H // 2) + g - 1)
                        for t in range(NT):
                            for c in range(NT):
                                at = (2 * (h % 2) + t) * VC
                                mm = pe.matmul(o_ps[g % 2][:, at:at + VC], prob[h % 4][:, c, t * P:(t + 1) * P],
                                               vp[o][:, c, :], start=c == 0, stop=c == NT - 1)
                        mm.then_inc(pv, 1)

            pipeline(pe, body, ahead=1)

        @block.vector
        def _(dve):
            def stack_zeros(i):
                dve.memset(k_st[i][64:MROW, :, :], 0.0).then_inc(zeros_d, 1)
                dve.memset(q_st[i][64:MROW, :, :], 0.0).then_inc(zeros_d, 1)

            def values_operand():
                dve.memset(w_v[:, RD:VC], 0.0).then_inc(blank, 1)
                dve.memset(b_v[:, RD:VC], 0.0).then_inc(blank, 1)
                dve.wait_ge(blank, 2)
                dve.memset(b_v[:, CS:CS + 1], 1.0).then_inc(blank, 1)
                dve.memset(one_row[:, :], 1.0).then_inc(blank, 1)

            def body(j, u):
                n = 2 * j + u
                i = u
                later = lambda k: not isinstance(j, int) or n >= k

                def reduce_unit(w):
                    b = n - 1
                    dve.wait_ge(score, b * H + w + 1)
                    g, t = w // 2, w % 2
                    if w == 0 and later(2):
                        dve.wait_ge(mp_d, b * MP)
                    dve.tensor_reduce(nmax[:, t, 2 * g:2 * g + 2],
                                      s_ps[t][:, :].rearrange("p (h k) -> p h k", h=2), AX.X, ALU.max,
                                      negate=True).then_inc(maxed, 1)

                def split_max(half_, k):
                    b = n - 1
                    hs = slice(half_ * H // 2, (half_ + 1) * H // 2)
                    high, mid, low = (mpart[:, :, half_, c, :] for c in range(NPART))
                    if k:
                        dve.wait_ge(mp_d, b * MP + 4 * half_ + k)
                    else:
                        dve.wait_ge(maxed, b * H + 8 * (half_ + 1))
                        if later(2):
                            dve.wait_ge(mt_p, 2 * (b - 1) + half_ + 1)
                    step = (lambda: dve.tensor_copy(high, nmax[:, :, hs]),
                            lambda: dve.tensor_tensor(nrest[:, :, hs], nmax[:, :, hs], high, ALU.subtract),
                            lambda: dve.tensor_copy(mid, nrest[:, :, hs]),
                            lambda: dve.tensor_tensor(low, nrest[:, :, hs], mid, ALU.subtract))[k]
                    step().then_inc(mp_d, 1)

                def moments(k):
                    t = k % NT
                    if k == 0:
                        dve.wait_ge(x_in, (n + 2) * 16)
                        if later(0):
                            dve.wait_ge(z_d, (n + 1) * NT)
                            dve.wait_ge(norm_d, (n + 1) * NORM)
                    if k < NT:
                        dve.bn_stats(stats[:, t, :], x[1 - i][:, t, :]).then_inc(stats_d, 1)
                    else:
                        dve.wait_ge(stats_d, (n + 1) * NT + t + 1)
                        apart(dve, spare)
                        dve.bn_aggr(mv[:, t, :], stats[:, t, :]).then_inc(mv_d, 1)

                def normed(k):
                    t = k % NT
                    if k == 0:
                        dve.wait_ge(norm_d, (n + 2) * NORM)
                        if later(1):
                            dve.wait_ge(y_out, n * 16)
                            dve.wait_ge(z_t, n)
                    dst, scale, done = ((y, r1, y_d), (z, r2, z_d))[k // NT]
                    dve.tensor_scalar(dst[1 - i][:, t, :], x[1 - i][:, t, :], mv[:, t, 0:1], scale[:, t:t + 1],
                                      ALU.subtract, ALU.mult).then_inc(done, 1)

                def weigh(k, b, o):
                    def wide(a):
                        return a[:, :].unsqueeze(2).broadcast_to([P, H * NT, R])

                    if k or not isinstance(b, int) or b >= 1:
                        dve.wait_ge(post, b * POST + k)
                    if k == 0:
                        dve.wait_ge(ov_d, (b + 1) * H // 2)
                    if k == 5:
                        dve.wait_ge(cexp_d, b + 1)
                    if k == 8 and (not isinstance(b, int) or b >= 1):
                        dve.wait_ge(prod_d, b)
                    by_head = lambda a: a[:, :, :].rearrange("p (h i) r -> p h i r", i=NT)
                    step = (
                        lambda: dve.reciprocal(inv[:, :], ov[o][:, :, CS]),
                        lambda: dve.tensor_tensor(comp[:, :, :], ov[o][:, :, CC:CS], wide(inv), ALU.mult),
                        lambda: dve.tensor_tensor(
                            by_head(comp2), by_head(comp), vp[o][:, :, CQ:CQ + H].rearrange("p i h -> p h i")
                            .unsqueeze(3).broadcast_to([P, H, NT, R]), ALU.add),
                        lambda: dve.tensor_reduce(cmax[:, :], comp2[:, :, :], AX.X, ALU.max),
                        lambda: dve.tensor_tensor(comp3[:, :, :], comp2[:, :, :], wide(cmax), ALU.subtract),
                        lambda: dve.tensor_reduce(csum[:, :], cexp[:, :, :], AX.X, ALU.add),
                        lambda: dve.reciprocal(cinv[:, :], csum[:, :]),
                        lambda: dve.tensor_tensor(cw[:, :], cinv[:, :], inv[:, :], ALU.mult),
                        lambda: dve.tensor_tensor(wgt[:, :, :], cexp[:, :, :], wide(cw), ALU.mult))[k]
                    step().then_inc(post, 1)

                if isinstance(j, int) and n == 0:
                    stack_zeros(0)
                    values_operand()
                if active(j, u, 3):
                    for k in range(5, POST):
                        weigh(k, n - 3, 1 - i)
                if active(j, u, 1):
                    for w in range(H // 2):
                        reduce_unit(w)
                    for k in range(MP // 2):
                        split_max(0, k)
                    for w in range(H // 2, H):
                        reduce_unit(w)
                for k in range(MP // 2):
                    if active(j, u, 1):
                        split_max(1, k)
                    if active(j, u, -1):
                        moments(k)
                if active(j, u, 3):
                    b, o = n - 3, 1 - i
                    dve.wait_ge(prod_d, b + 1)
                    if later(5):
                        dve.wait_ge(ao_out, (b - 1) * 16)
                    for t in range(NT):
                        dve.tensor_reduce(
                            ao[o][:, t, :].rearrange("p (h e) -> p h e", h=H),
                            prod[:, :, :].rearrange("p (h i) (r e) -> p i h e r", i=NT, r=R)[:, t],
                            AX.X, ALU.add).then_inc(ao_d, 1)
                for k in range(5):
                    if active(j, u, 2):
                        weigh(k, n - 2, i)
                    if k < 2 * NT and active(j, u, -1):
                        normed(k)
                if active(j, u, 0):
                    if isinstance(j, int) and n == 0:
                        dve.wait_ge(folded, 6)
                    dve.wait_ge(v_p, n + 1)
                    if later(2):
                        dve.wait_ge(pv, (n - 1) * H)
                        dve.wait_ge(post, (n - 2) * POST + 3)
                    dve.tensor_tensor(vp[i][:, :, :], zv_ps[:, 0:NT * VC].rearrange("p (i c) -> p i c", i=NT),
                                      b_v[:, :].unsqueeze(1).broadcast_to([P, NT, VC]), ALU.add).then_inc(v_d, 1)
                if isinstance(j, int) and n == 0:
                    stack_zeros(1)

            pipeline(dve, body, ahead=1)


def dense(nc, d):
    ctx = ExitStack()
    with ctx:
        sb, sem = memory(nc, ctx, "b")
        NU, C = NB // 2, 2 * NT
        w_f = sb("w_f", [P, P])
        w_r1 = sb("w_r1", [P, 2, P])
        w_r2 = sb("w_r2", [P, 2, P])
        b_f = sb("b_f", [P, P])
        b_r2 = sb("b_r2", [P, P])
        cols = sb("cols", [P, 4])
        ident = sb("ident", [P, P])
        half = sb("half", [P, C])
        two = lambda name, shape: [sb(f"{name}{i}", shape) for i in range(2)]
        x, y, ao = two("x", [P, C, P]), two("y", [P, C, P]), two("ao", [P, C, P])
        wc = two("wc", [P, 2, P])
        ao_t, r, xr = two("ao_t", [P, C * P]), two("r", [P, C, P]), two("xr", [P, C, P])
        yb, z, on = two("yb", [P, C, P]), two("z", [P, C, P]), two("on", [P, C * P])
        hid, x1, xb = two("hid", [P, 2, C * P]), two("x1", [P, C, P]), two("xb", [P, C, P])
        z1, z1t, x2 = two("z1_", [P, C, P]), two("z1t", [P, C * P]), two("x2_", [P, C, P])
        stats, mv = two("stats", [P, C, 6]), two("mv", [P, C, 2])
        var, rs = two("var", [P, C]), two("rs", [P, C])
        bank = [ctx.enter_context(nc.psum_tensor(f"b_bank{i}", [P, 512], F32)) for i in range(8)]
        aot_ps, zt_ps, z1t_ps, r_ps, h_ps, f_ps, g_ps = *bank[0:4], bank[4:6], bank[6], bank[7]

        spare = sem("spare")
        loaded = sem("loaded")
        loaded_late = sem("loaded_late")
        half_d = sem("half_d")
        ay_in = sem("ay_in")
        x_in = sem("x_in")
        wc_in = sem("wc_in")
        aot_p, aot_d = sem("aot_p"), sem("aot_d")
        yb_d = sem("yb_d")
        r_p, r_d = sem("r_p"), sem("r_d")
        xr_d = sem("xr_d")
        stat_d = [sem(f"stat_d{i}") for i in range(2)]
        mv_d = [sem(f"mv_d{i}") for i in range(2)]
        norm_d = [sem(f"norm_d{i}") for i in range(2)]
        z_d = [sem(f"z_d{i}") for i in range(2)]
        zt_p, on_d = sem("zt_p"), sem("on_d")
        h_p, hid_d = sem("h_p"), sem("hid_d")
        f_p, x1_d, xb_d = sem("f_p"), sem("x1_d"), sem("xb_d")
        z1t_p, z1t_d = sem("z1t_p"), sem("z1t_d")
        g_p, x2_d, x2_out = sem("g_p"), sem("x2_d"), sem("x2_out")

        N_LOAD, N_LATE = 4, 3
        units = lambda a: a.rearrange("b t f -> (b t) f").rearrange("(j u c p) f -> j u p c f", u=2, c=C, p=P)
        x_dram, y_dram, ao_dram, x2_dram = units(d["x"]), units(d["y"]), units(d["ao"]), units(d["x2"])
        wc_dram = d["folded"].rearrange("(j u) p f -> j u p f", u=2)
        has = lambda j, u, lag: active(j, u, lag, NU)
        later = lambda j, n, k: not isinstance(j, int) or n >= k
        flat = lambda a: a[:, :, :].rearrange("p c f -> p (c f)")
        block = ctx.enter_context(nc.Block())

        @block.sync
        def _(sp):
            def load_weights():
                for dst, src in ((ident[:, :], d["ident"]), (w_f[:, :], d["a_Wf_t"]), (b_f[:, :], d["a_bf_b"]),
                                 (cols[:, :], d["b_cols"])):
                    sp.dma_start(dst, src).then_inc(loaded, 16)
                for dst, src in ((w_r1[:, :, :].rearrange("p a f -> p (a f)"), d["a_Wr1_t"]),
                                 (w_r2[:, :, :], d["a_Wr2_t"].rearrange("(a p) f -> p a f", p=P)),
                                 (b_r2[:, :], d["a_br2_b"])):
                    sp.dma_start(dst, src).then_inc(loaded_late, 16)

            def body(j, u):
                n, i = 2 * j + u, u
                if has(j, u, -1):
                    at = pair(j, u, -1)
                    if later(j, n, 0):
                        sp.wait_ge(ay_in, (n + 1) * 32)
                        apart(sp, spare)
                        sp.wait_ge(x_in, (n + 1) * 16)
                        apart(sp, spare)
                    if later(j, n, 1):
                        sp.wait_ge(aot_p, n)
                        apart(sp, spare)
                        sp.wait_ge(yb_d, n)
                        apart(sp, spare)
                        sp.wait_ge(xr_d, 2 * n - 1)
                        apart(sp, spare)
                    sp.dma_start(ao[1 - i][:, :, :], ao_dram[at[0], at[1]]).then_inc(ay_in, 16)
                    sp.dma_start(y[1 - i][:, :, :], y_dram[at[0], at[1]]).then_inc(ay_in, 16)
                    if isinstance(j, int) and n == -1:
                        load_weights()
                    sp.dma_start(x[1 - i][:, :, :], x_dram[at[0], at[1]]).then_inc(x_in, 16)
                if has(j, u, 1):
                    at = pair(j, u, 1)
                    if later(j, n, 3):
                        sp.wait_ge(g_p, n - 2)
                        apart(sp, spare)
                        sp.wait_ge(xb_d, n - 2)
                        apart(sp, spare)
                    sp.wait_ge(wc_in, (n - 1) * 16)
                    apart(sp, spare)
                    sp.dma_start(wc[1 - i][:, :, :].rearrange("p a f -> p (a f)"), wc_dram[at[0], at[1]]
                                 ).then_inc(wc_in, 16)
                if has(j, u, 3):
                    sp.wait_ge(x2_d, n - 2)
                    apart(sp, spare)
                    at = pair(j, u, 3)
                    sp.wait_ge(x2_out, (n - 3) * 16)
                    apart(sp, spare)
                    sp.dma_start(x2_dram[at[0], at[1]], x2[1 - i][:, :, :]).then_inc(x2_out, 16)

            pipeline(sp, body, NU, 4, ahead=1)
            sp.wait_ge(x2_out, NU * 16)

        @block.gpsimd
        def _(pool):
            pool.memset(half[:, :], -0.5).then_inc(half_d, 1)
            pool.wait_ge(half_d, 1)
            pool.wait_ge(loaded, N_LOAD * 16)

            def norm(k, n):
                pool.wait_ge(mv_d[k], (n + 1) * C)
                apart(pool, spare)
                pool.tensor_scalar(var[k][:, :], mv[k][:, :, 1], EPS, 1.0, ALU.add, ALU.mult).then_inc(norm_d[k], 1)
                pool.wait_ge(norm_d[k], 2 * n + 1)
                pool.tensor_tensor(rs[k][:, :], var[k][:, :], half[:, :], ALU.pow).then_inc(norm_d[k], 1)

            rows = lambda a: a[:, :].unsqueeze(1).broadcast_to([P, C, P])

            def body(j, u):
                n, i = 2 * j + u, u
                if has(j, u, 0):
                    pool.wait_ge(ay_in, (n + 1) * 32)
                    if later(j, n, 2):
                        pool.wait_ge(r_d, n - 1)
                    pool.tensor_tensor(yb[i][:, :, :], y[i][:, :, :], rows(b_f), ALU.add).then_inc(yb_d, 1)
                if has(j, u, 2):
                    if later(j, n, 3):
                        pool.wait_ge(z_d[1], (n - 2) * C)
                    norm(1, n - 2)
                    pool.wait_ge(wc_in, (n - 1) * 16)
                    pool.wait_ge(x1_d, n - 1)
                    if later(j, n, 4):
                        pool.wait_ge(x2_d, n - 3)
                    pool.tensor_tensor(xb[i][:, :, :], x1[i][:, :, :],
                                       wc[i][:, 1, :].unsqueeze(1).broadcast_to([P, C, P]), ALU.add
                                       ).then_inc(xb_d, 1)
                if has(j, u, 0):
                    if isinstance(j, int) and n == 0:
                        pool.wait_ge(loaded_late, N_LATE * 16)
                    pool.wait_ge(x_in, (n + 1) * 16)
                    if later(j, n, 2):
                        pool.wait_ge(x1_d, n - 1)
                    pool.tensor_tensor(xr[i][:, :, :], x[i][:, :, :], rows(b_r2), ALU.add).then_inc(xr_d, 1)
                    if later(j, n, 1):
                        pool.wait_ge(z_d[0], n * C)
                    norm(0, n)
                    pool.wait_ge(r_d, n + 1)
                    pool.wait_ge(xr_d, 2 * n + 1)
                    pool.tensor_tensor(xr[i][:, :, :], xr[i][:, :, :], r[i][:, :, :], ALU.add).then_inc(xr_d, 1)

            pipeline(pool, body, NU, 4, ahead=1)

        @block.scalar
        def _(act):
            act.wait_ge(loaded, N_LOAD * 16)

            def body(j, u):
                n, i = 2 * j + u, u
                if has(j, u, 0):
                    act.wait_ge(aot_p, n + 1)
                    if later(j, n, 2):
                        act.wait_ge(r_p, n - 1)
                    act.copy(ao_t[i][:, :], aot_ps[:, :]).then_inc(aot_d, 1)
                if has(j, u, 1):
                    act.wait_ge(zt_p, n)
                    if later(j, n, 3):
                        act.wait_ge(h_p, 2 * (n - 2))
                    act.activation(on[1 - i][:, :], zt_ps[:, :], ACT.Identity, scale=cols[:, 2:3], bias=cols[:, 3:4]
                                   ).then_inc(on_d, 1)
                    if later(j, n, 3):
                        act.wait_ge(f_p, n - 2)
                    for c in range(2):
                        act.wait_ge(h_p, 2 * (n - 1) + c + 1)
                        act.activation(hid[1 - i][:, c, :], h_ps[c][:, :], ACT.Relu, bias=cols[:, c:c + 1]
                                       ).then_inc(hid_d, 1)
                if has(j, u, 2):
                    act.wait_ge(z1t_p, n - 1)
                    if later(j, n, 4):
                        act.wait_ge(g_p, n - 3)
                    act.copy(z1t[i][:, :], z1t_ps[:, :]).then_inc(z1t_d, 1)

            pipeline(act, body, NU, 4, ahead=1)

        @block.tensor
        def _(pe):
            pe.wait_ge(loaded, N_LOAD * 16)

            def turn(dst, src):
                for c in range(C):
                    mm = pe.transpose(dst[:, c * P:(c + 1) * P], src[:, c, :], ident[:, :])
                return mm

            def body(j, u):
                n, i = 2 * j + u, u
                if has(j, u, 0):
                    pe.wait_ge(ay_in, (n + 1) * 32)
                    if later(j, n, 1):
                        pe.wait_ge(aot_d, n)
                    turn(aot_ps, ao[i]).then_inc(aot_p, 1)
                if has(j, u, 3):
                    pe.wait_ge(z1t_d, n - 2)
                    pe.wait_ge(wc_in, (n - 2) * 16)
                    if later(j, n, 4):
                        pe.wait_ge(x2_d, n - 3)
                    for c in range(C):
                        mm = pe.matmul(g_ps[:, c * P:(c + 1) * P], z1t[1 - i][:, c * P:(c + 1) * P],
                                       wc[1 - i][:, 0, :], start=True, stop=True)
                    mm.then_inc(g_p, 1)
                if has(j, u, 1):
                    pe.wait_ge(z_d[0], n * C)
                    if later(j, n, 2):
                        pe.wait_ge(on_d, n - 1)
                    turn(zt_ps, z[1 - i]).then_inc(zt_p, 1)
                if has(j, u, 0):
                    pe.wait_ge(aot_d, n + 1)
                    if later(j, n, 1):
                        pe.wait_ge(r_d, n)
                    for c in range(C):
                        mm = pe.matmul(r_ps[:, c * P:(c + 1) * P], ao_t[i][:, c * P:(c + 1) * P], w_f[:, :],
                                       start=True, stop=True)
                    mm.then_inc(r_p, 1)
                if has(j, u, 1):
                    pe.wait_ge(on_d, n)
                    if isinstance(j, int) and n == 1:
                        pe.wait_ge(loaded_late, N_LATE * 16)
                    for c in range(2):
                        if later(j, n, 2):
                            pe.wait_ge(hid_d, 2 * (n - 2) + c + 1)
                        pe.matmul(h_ps[c][:, :], w_r1[:, c, :], on[1 - i][:, :], start=True, stop=True
                                  ).then_inc(h_p, 1)
                if has(j, u, 2):
                    pe.wait_ge(z_d[1], (n - 1) * C)
                    if later(j, n, 3):
                        pe.wait_ge(z1t_d, n - 2)
                    turn(z1t_ps, z1[i]).then_inc(z1t_p, 1)
                if has(j, u, 1):
                    pe.wait_ge(hid_d, 2 * n)
                    if later(j, n, 2):
                        pe.wait_ge(x1_d, n - 1)
                    for c in range(C):
                        for k in range(2):
                            mm = pe.matmul(f_ps[:, c * P:(c + 1) * P], hid[1 - i][:, k, c * P:(c + 1) * P],
                                           w_r2[:, k, :], start=k == 0, stop=k == 1)
                    mm.then_inc(f_p, 1)

            pipeline(pe, body, NU, 4, ahead=1)

        @block.vector
        def _(dve):
            def moments(k, n, src):
                for c in range(C):
                    dve.bn_stats(stats[k][:, c, :], src[:, c, :]).then_inc(stat_d[k], 1)
                for c in range(C):
                    dve.wait_ge(stat_d[k], n * C + c + 1)
                    apart(dve, spare)
                    dve.bn_aggr(mv[k][:, c, :], stats[k][:, c, :]).then_inc(mv_d[k], 1)

            def normed(k, n, src, dst):
                dve.wait_ge(norm_d[k], 2 * (n + 1))
                for c in range(C):
                    dve.tensor_scalar(dst[:, c, :], src[:, c, :], mv[k][:, c, 0:1], rs[k][:, c:c + 1],
                                      ALU.subtract, ALU.mult).then_inc(z_d[k], 1)

            def body(j, u):
                n, i = 2 * j + u, u
                if has(j, u, 1):
                    if later(j, n, 3):
                        dve.wait_ge(zt_p, n - 2)
                    normed(0, n - 1, r[1 - i], z[1 - i])
                if has(j, u, 2):
                    dve.wait_ge(f_p, n - 1)
                    dve.wait_ge(xr_d, 2 * (n - 1))
                    if later(j, n, 4):
                        dve.wait_ge(xb_d, n - 3)
                    dve.tensor_tensor(flat(x1[i]), f_ps[:, :], flat(xr[i]), ALU.add).then_inc(x1_d, 1)
                    dve.wait_ge(x1_d, n - 1)
                    if later(j, n, 3):
                        dve.wait_ge(z_d[1], (n - 2) * C)
                    moments(1, n - 2, x1[i])
                if has(j, u, 3):
                    dve.wait_ge(g_p, n - 2)
                    dve.wait_ge(xb_d, n - 2)
                    if later(j, n, 5):
                        dve.wait_ge(x2_out, (n - 4) * 16)
                    dve.tensor_tensor(flat(x2[1 - i]), g_ps[:, :], flat(xb[1 - i]), ALU.add).then_inc(x2_d, 1)
                if has(j, u, 0):
                    dve.wait_ge(r_p, n + 1)
                    dve.wait_ge(yb_d, n + 1)
                    if later(j, n, 2):
                        dve.wait_ge(xr_d, 2 * (n - 1))
                    dve.tensor_tensor(flat(r[i]), r_ps[:, :], flat(yb[i]), ALU.add).then_inc(r_d, 1)
                    dve.wait_ge(r_d, n + 1)
                    if later(j, n, 1):
                        dve.wait_ge(z_d[0], n * C)
                if has(j, u, 2):
                    if later(j, n, 4):
                        dve.wait_ge(z1t_p, n - 3)
                    normed(1, n - 2, x1[i], z1[i])
                if has(j, u, 0):
                    moments(0, n, r[i])

            pipeline(dve, body, NU, 4, ahead=1)


def attention_b(nc, d):
    ctx = ExitStack()
    with ctx:
        sb, sem = memory(nc, ctx, "c")
        SEG = 64
        NS = T // SEG
        HV = H * HD
        MW = HV + H
        VP = 2 * 2 * (HD + 1)
        WIN = 96
        VW = VP * (H // 2 - 1) + WIN
        ST = 8
        S_AT = (1, 2, 4, 5)
        OFF = 7
        two = lambda name, shape, dt=F32: [sb(f"{name}{i}", shape, dt) for i in range(2)]
        w_kq = sb("w_kq", [P, 2, P])
        w_v = sb("w_v", [P, P])
        w_o = sb("w_o", [P, P])
        ident, ident16 = sb("ident", [P, P]), sb("ident16", [P, P], BF16)
        causal, causal_t = sb("causal", [P, 512], BF16), sb("causal_t", [P, T], BF16)
        causal32 = sb("causal32", [P, P + SEG])
        diag = sb("diag", [P, MW])
        beta = sb("beta", [P, 4])
        bexp = sb("bexp", [P, 1])
        half = sb("half", [P, NT])
        wc = two("wc", [P, 2, P])
        x = two("x", [P, NT, P])
        z, zt = two("z", [P, NT, P]), two("zt", [P, NS, 2, SEG])
        stats, mv = two("stats", [P, NT, 6]), two("mv", [P, NT, 2])
        var, rs = two("var", [P, NT]), two("rs", [P, NT])
        kq = two("kq", [P, 2, T])
        rest = sb("rest", [P, 2, T])
        parts = two("parts", [P, 2, NPART, T], BF16)
        q_st, k_st = two("q_st", [P, H, T], BF16), two("k_st", [P, H, T], BF16)
        pos, neg, nexp = (sb(a, [P, 2, T]) for a in ("pos", "neg", "nexp"))
        sg = two("sg", [P, NS, 2, SEG])
        skn = sb("skn", [P, NS - 1, P])
        uv = two("uv", [P, NS - 1, MW])
        mz, mzt = sb("mz", [P, MW]), sb("mzt", [P, MW])
        dn, dr = sb("dn", [P, NS - 1, H]), sb("dr", [P, NS - 1, H])
        am = two("am", [P, NS - 1, P])
        vs = sb("vs", [P, NS, P])
        vb = two("vb", [P, NT, VW])
        nmax, nrest = sb("nmax", [P, NT, H]), sb("nrest", [P, NT, H])
        mpart = sb("mpart", [P, NT, 2, NPART, H // 2], BF16)
        mt = [sb(f"mt{i}", [NPART * H // 2, T], BF16) for i in range(2)]
        prob = [sb(f"prob{i}", [P, T]) for i in range(4)]
        dinv, ad = sb("dinv", [P, NT, H]), sb("ad", [P, NT, P])
        at_b = sb("at", [P, T])
        xt, x3, xb, x4 = (two(a, [P, NT, P]) for a in ("xt", "x3_", "xb", "x4_"))
        z4, z4t = sb("z4", [P, NT, P]), sb("z4t", [P, T])
        bank = [ctx.enter_context(nc.psum_tensor(f"c_bank{i}", [P, 512], F32)) for i in range(6)]
        ps_a, ps_b, ps_c, s_ps = *bank[0:3], bank[3:5]
        t_ps = bank[5][:, 0:T]
        o_ps = ctx.enter_context(nc.psum_tensor("c_o_bank", [P, NT, 512], F32))
        mt_ps = ps_a[0:NPART * H // 2, 0:T // 2].bitcast(BF16)

        spare, loaded, loaded_late = sem("spare"), sem("loaded"), sem("loaded_late")
        const_d, beta_d = sem("const_d"), sem("beta_d")
        mask_d = sem("mask_d")
        zeros_d, ones_d = sem("zeros_d"), sem("ones_d")
        x_in, xt_in, wc_in = sem("x_in"), sem("xt_in"), sem("wc_in")
        stat_d = [sem(f"stat_d{i}") for i in range(2)]
        mv_d = [sem(f"mv_d{i}") for i in range(2)]
        norm_d = [sem(f"norm_d{i}") for i in range(2)]
        z_d, zt_p, zt_d = sem("z_d"), sem("zt_p"), sem("zt_d")
        kq_p, kq_d = sem("kq_p"), sem("kq_d")
        pn_d, nexp_d, sg_d = sem("pn_d"), sem("nexp_d"), sem("sg_d")
        split_d, parts_out = sem("split_d"), sem("parts_out")
        stack_in = [sem(f"stack_in{i}") for i in range(2)]
        vs_p = sem("vs_p")
        vs_d = sem("vs_d")
        v_d = sem("v_d")
        sk_p, sk_d = sem("sk_p"), sem("sk_d")
        mem_p = sem("mem_p")
        mz_d = sem("mz_d")
        read_p = sem("read_p")
        read_d = sem("read_d")
        u_d = sem("u_d")
        score, maxed = sem("score"), sem("maxed")
        mp_d = sem("mp_d")
        mt_p, mt_d, mt_out = sem("mt_p"), sem("mt_d"), sem("mt_out")
        m_in = [sem(f"m_in{i}") for i in range(2)]
        shifted, exped, pv = sem("shifted"), sem("exped"), sem("pv")
        ad_d = sem("ad_d")
        at_p, at_d = sem("at_p"), sem("at_d")
        wo_p, x3_d, xb_d = sem("wo_p"), sem("x3_d"), sem("xb_d")
        z4_d, z4_p, z4t_d, g_p, x4_d, x4_out = (sem(a) for a in ("z4_d", "z4_p", "z4t_d", "g_p", "x4_d", "x4_out"))

        USES_A = [(at_d, 2, 3), (kq_d, 2, 0), (mt_d, 2, 1)]
        USES_B = [(zt_d, 1, 0), (x3_d, 1, 3), (vs_d, 2, 0), (z4t_d, 1, 3), (x4_d, 1, 3)]

        def free(eng, uses, k, j, u):
            n = 2 * j + u
            if not isinstance(j, int):
                s, per, lag = uses[k - 1]
                eng.wait_ge(s, (n - lag - (k == 0) + 1) * per)
                return
            for m, (s, per, lag) in enumerate(uses):
                done = min(n - lag - (m >= k) + 1, NB)
                if done > 0:
                    eng.wait_ge(s, done * per)

        later = lambda j, b, k: not isinstance(j, int) or b >= k
        pairs = lambda a: a.rearrange("(j u) (i p) f -> j u p i f", u=2, p=P)
        x_dram, out_dram, wc_dram = pairs(d["x2"]), pairs(d["out"]), d["folded"]
        parts_dram, m_dram = d["c_parts_dram"], d["c_m_dram"]
        flat = lambda a: a[:, :, :].rearrange("p c f -> p (c f)")
        N_LOAD, N_LATE, SPLIT, MP, AD, VD = 3, 4, 4, 8, 6, 4
        MT_AT = (3, 7)

        def value_part(a, t, p):
            return a[p * SEG:(p + 1) * SEG, t, 0:VP * H // 2].rearrange("k (g s a e) -> k s g a e", s=2, a=2,
                                                                        e=HD + 1)[:, :, :, p]

        def turn(s):
            return (1, s - OFF) if s >= OFF else (2, s + ST - OFF)

        def before(lag, g):
            return (lag, g - 1) if g else (lag + 1, ST - 1)

        block = ctx.enter_context(nc.Block())

        @block.sync
        def _(sp):
            def load_weights():
                for dst, src in ((ident[:, :], d["ident"]),
                                 (w_kq[:, :, :].rearrange("p a f -> p (a f)"), d["b_Wkq_t"]),
                                 (w_v[:, :], d["b_Wv_t"])):
                    sp.dma_start(dst, src).then_inc(loaded, 16)
                for dst, src in ((causal32[:, :], d["causal"]), (diag[:, :], d["diag"]), (w_o[:, :], d["b_Wo_t"]),
                                 (beta[:, 0:1], d["b_beta"])):
                    sp.dma_start(dst, src).then_inc(loaded_late, 16)

            def body(j, u):
                n, i = 2 * j + u, u

                def shift_rows(h2):
                    b, o = n - 1, 1 - i
                    sp.wait_ge(mt_out, (2 * b + h2 + 1) * 16)
                    apart(sp, spare)
                    sp.dma_start(q_st[o][MROW:KROWS, h2 * H // 2:(h2 + 1) * H // 2, :],
                                 m_dram[o, h2].rearrange("(a h) t -> a h t", a=NPART)).then_inc(m_in[h2], 16)

                if active(j, u, -2):
                    at = pair(j, u, -2)
                    if later(j, n, -1):
                        sp.wait_ge(x_in, (n + 2) * 16)
                        apart(sp, spare)
                    if later(j, n, 0):
                        sp.wait_ge(z_d, (n + 1) * NT)
                        apart(sp, spare)
                    sp.dma_start(x[i][:, :, :], x_dram[at[0], at[1]]).then_inc(x_in, 16)
                if isinstance(j, int) and n == -2:
                    load_weights()
                if active(j, u, 2):
                    at = pair(j, u, 2)
                    sp.wait_ge(xt_in, (n - 2) * 16)
                    apart(sp, spare)
                    sp.wait_ge(wc_in, (n - 2) * 16)
                    apart(sp, spare)
                    if later(j, n, 4):
                        sp.wait_ge(x3_d, n - 3)
                        apart(sp, spare)
                        sp.wait_ge(g_p, n - 3)
                        apart(sp, spare)
                        sp.wait_ge(xb_d, n - 3)
                        apart(sp, spare)
                    sp.dma_start(xt[i][:, :, :], x_dram[at[0], at[1]]).then_inc(xt_in, 16)
                    sp.dma_start(wc[i][:, :, :].rearrange("p a f -> p (a f)"), wc_dram[at[0]]).then_inc(wc_in, 16)

                def stack(h2):
                    hs = slice(h2 * H // 2, (h2 + 1) * H // 2)
                    if later(j, n, 2):
                        sp.wait_ge(shifted, (n - 2) * ST + (h2 + 1) * ST // 2)
                        apart(sp, spare)
                    for a in range(NPART):
                        sp.dma_start(q_st[i][a * NPART * HD:(a + 1) * NPART * HD, hs, :],
                                     parts_dram[i, NPART + a].rearrange("(d h) t -> d h t", d=HD)[:, hs]
                                     .unsqueeze(0).broadcast_to([NPART, HD, H // 2, T])
                                     ).then_inc(stack_in[h2], 16)
                    sp.dma_start(k_st[i][0:SROWS, hs, :],
                                 parts_dram[i, 0:NPART].rearrange("c (d h) t -> (c d) h t", d=HD)[:, hs]
                                 .unsqueeze(0).broadcast_to([NPART, NPART * HD, H // 2, T])
                                 ).then_inc(stack_in[h2], 16)

                if active(j, u, 0):
                    sp.wait_ge(split_d, (n + 1) * SPLIT)
                    apart(sp, spare)
                    sp.dma_start(parts_dram[i].rearrange("c p t -> p c t"),
                                 parts[i][:, :, :, :].rearrange("p q c t -> p (q c) t")).then_inc(parts_out, 16)
                    sp.wait_ge(parts_out, (n + 1) * 16)
                    apart(sp, spare)
                    if isinstance(j, int) and n < 2:
                        sp.wait_ge(zeros_d, 2 * (n + 1))
                    stack(0)
                if active(j, u, 1):
                    shift_rows(0)
                    shift_rows(1)
                if active(j, u, 0):
                    stack(1)
                if active(j, u, 3):
                    at = pair(j, u, 3)
                    sp.wait_ge(x4_d, n - 2)
                    apart(sp, spare)
                    sp.wait_ge(x4_out, (n - 3) * 16)
                    apart(sp, spare)
                    sp.dma_start(out_dram[at[0], at[1]], x4[1 - i][:, :, :]).then_inc(x4_out, 16)

            pipeline(sp, body, ahead=2)
            sp.wait_ge(x4_out, NB * 16)

        @block.gpsimd
        def _(pool):
            def const(k, ins):
                ins.then_inc(const_d, 1)
                pool.wait_ge(const_d, k)

            def value_consts(i):
                const(3 + 7 * i, pool.memset(uv[i][:, :, :], 0.0))
                const(4 + 7 * i, pool.memset(uv[i][0:SEG, :, HV:MW], 1.0))
                const(5 + 7 * i, pool.memset(vb[i][:, :, :], 0.0))
                for t in range(NT):
                    for h2 in range(2):
                        const(6 + 7 * i + 2 * t + h2, pool.memset(value_part(vb[i], t, h2)[:, :, :, HD:], 1.0))

            const(1, pool.memset(half[:, :], -0.5))
            const(2, pool.memset(skn[:, :, :], 0.0))

            def stack_ones(i):
                pool.memset(k_st[i][MROW:P, :, :], 1.0).then_inc(ones_d, 1)
                pool.wait_ge(ones_d, i + 1)

            def norm(k, b):
                pool.wait_ge(mv_d[k], (b + 1) * NT)
                apart(pool, spare)
                pool.tensor_scalar(var[k][:, :], mv[k][:, :, 1], EPS, 1.0, ALU.add, ALU.mult).then_inc(norm_d[k], 1)
                pool.wait_ge(norm_d[k], 2 * b + 1)
                pool.tensor_tensor(rs[k][:, :], var[k][:, :], half[:, :], ALU.pow).then_inc(norm_d[k], 1)

            def body(j, u):
                n, i = 2 * j + u, u
                if active(j, u, 1):
                    b, o = n - 1, 1 - i
                    pool.wait_ge(vs_d, 2 * (b + 1))
                    if later(j, b, 2):
                        pool.wait_ge(pv, (b - 1) * ST)
                    apart(pool, spare)
                    for k in range(VD):
                        t, h2 = k // 2, k % 2
                        pool.tensor_scalar(value_part(vb[o], t, h2)[:, :, :, 0:HD],
                                           vs[h2 * SEG:(h2 + 1) * SEG, 2 * t:2 * t + 2, :].rearrange(
                                               "k s (g a e) -> k s g a e", a=2, e=HD)[:, :, :, h2],
                                           1.0, 0.0, ALU.mult, ALU.add).then_inc(v_d, 1)
                        pool.wait_ge(v_d, VD * b + k + 1)
                        apart(pool, spare)
                if active(j, u, 0):
                    pool.wait_ge(kq_d, (n + 1) * 2)
                    if later(j, n, 2):
                        pool.wait_ge(parts_out, (n - 1) * 16)

                    def split(k, ins):
                        ins.then_inc(split_d, 1)
                        pool.wait_ge(split_d, n * SPLIT + k)
                        apart(pool, spare)

                    apart(pool, spare)
                    split(1, pool.tensor_scalar(parts[i][:, :, 0, :], kq[i][:, :, :], 1.0, 0.0, ALU.mult, ALU.add))
                    split(2, pool.tensor_tensor(rest[:, :, :], kq[i][:, :, :], parts[i][:, :, 0, :], ALU.subtract))
                    split(3, pool.tensor_scalar(parts[i][:, :, 1, :], rest[:, :, :], 1.0, 0.0, ALU.mult, ALU.add))
                    split(4, pool.tensor_tensor(parts[i][:, :, 2, :], rest[:, :, :], parts[i][:, :, 1, :],
                                                ALU.subtract))
                if active(j, u, 3):
                    b = n - 3
                    if later(j, b, 1):
                        pool.wait_ge(z4_d, b * NT)
                    norm(1, b)
                if active(j, u, 0):
                    pool.wait_ge(nexp_d, n + 1)
                    if later(j, n, 2):
                        pool.wait_ge(read_p, (n - 1) * 3)
                    pool.tensor_tensor(sg[i][:, :, :, :].rearrange("p s a t -> p a s t"),
                                       pos[:, :, :].rearrange("p a (s t) -> p a s t", s=NS),
                                       nexp[:, :, :].rearrange("p a (s t) -> p a s t", s=NS), ALU.add
                                       ).then_inc(sg_d, 1)
                if active(j, u, 3):
                    pool.wait_ge(wc_in, (b + 1) * 16)
                    pool.wait_ge(x3_d, b + 1)
                    if later(j, b, 2):
                        pool.wait_ge(x4_d, b - 1)
                    pool.tensor_tensor(xb[1 - i][:, :, :], x3[1 - i][:, :, :],
                                       wc[1 - i][:, 1, :].unsqueeze(1).broadcast_to([P, NT, P]), ALU.add
                                       ).then_inc(xb_d, 1)
                if active(j, u, -1):
                    if later(j, n, 0):
                        pool.wait_ge(z_d, (n + 1) * NT)
                    norm(0, n + 1)
                if isinstance(j, int) and 0 <= n < 2:
                    pool.wait_ge(norm_d[0], 2 * (n + 2))
                    stack_ones(n)
                if isinstance(j, int) and -1 <= n < 1:
                    pool.wait_ge(norm_d[0], 2 * (n + 2))
                    value_consts(n + 1)

            pipeline(pool, body, ahead=1)

        @block.scalar
        def _(act):
            act.wait_ge(loaded, N_LOAD * 16)
            act.copy(ident16[:, :], ident[:, :]).then_inc(mask_d, 1)

            def masks():
                act.wait_ge(loaded_late, N_LATE * 16)
                act.copy(causal[:, :].rearrange("p (c f) -> p c f", c=4),
                         causal32[:, 0:P].unsqueeze(1).broadcast_to([P, 4, P])).then_inc(mask_d, 1)
                act.copy(causal_t[:, :].rearrange("p (c f) -> p c f", c=NS),
                         causal32[:, P:].unsqueeze(1).broadcast_to([P, NS, SEG])).then_inc(mask_d, 1)
                act.activation(bexp[:, :], beta[:, 0:1], ACT.Exp, scale=-1.0).then_inc(beta_d, 1)

            def body(j, u):
                n, i = 2 * j + u, u
                for s in range(ST):
                    lag, g = turn(s)
                    if active(j, u, lag):
                        b = n - lag
                        act.wait_ge(shifted, b * ST + g + 1)
                        if g >= 4 or later(j, b, 1):
                            act.wait_ge(pv, b * ST + g - 3)
                        act.activation(prob[g % 4][:, :], t_ps, ACT.Exp).then_inc(exped, 1)
                    if s == 0 and active(j, u, 1):
                        b = n - 1
                        act.wait_ge(sk_p, b + 1)
                        if later(j, b, 1):
                            act.wait_ge(mem_p, b * 3)
                        act.copy(skn[0:SEG, :, :].rearrange("p s f -> p (s f)"),
                                 ps_c[0:SEG, 0:(NS - 1) * P]).then_inc(sk_d, 1)
                    if s == 0 and active(j, u, 3):
                        b = n - 3
                        act.wait_ge(at_p, b + 1)
                        if isinstance(b, int) and b == 0:
                            act.wait_ge(beta_d, 4)
                        if later(j, b, 1):
                            act.wait_ge(wo_p, b)
                        act.activation(at_b[:, :], ps_a[:, 0:T], ACT.Copy, scale=beta[:, 3:4]).then_inc(at_d, 1)
                    if s == 0 and active(j, u, 0):
                        act.wait_ge(zt_p, n + 1)
                        act.copy(zt[i][:, :, :, :], ps_b[:, 0:T].rearrange("p (s t) -> p s t", s=NS).unsqueeze(2)
                                 .broadcast_to([P, NS, 2, SEG])).then_inc(zt_d, 1)
                    if s == 1 and active(j, u, 0):
                        act.wait_ge(kq_p, n + 1)
                        act.copy(kq[i][:, 0, :], ps_a[:, 0:T]).then_inc(kq_d, 1)
                        act.mul(kq[i][:, 1, :], ps_a[:, T:2 * T], HD ** -0.5).then_inc(kq_d, 1)
                    if s == 3 and active(j, u, 0):
                        act.wait_ge(vs_p, n + 1)
                        if later(j, n, 2):
                            act.wait_ge(mem_p, (n - 1) * 3)
                        else:
                            act.wait_ge(const_d, 9 + 7 * n)
                        act.copy(uv[i][0:SEG, :, 0:HV], ps_b[0:SEG, 0:(NS - 1) * P].rearrange("p (s f) -> p s f", f=P)
                                 ).then_inc(vs_d, 1)
                        if later(j, n, 1):
                            act.wait_ge(v_d, n * VD)
                        act.copy(vs[:, :, :].rearrange("p s f -> p (s f)"), ps_b[:, :]).then_inc(vs_d, 1)
                        act.wait_ge(pn_d, (n + 1) * 2)
                        if later(j, n, 1):
                            act.wait_ge(sg_d, n)
                        act.activation(nexp[:, :, :], neg[:, :, :], ACT.Exp).then_inc(nexp_d, 1)
                    for h2 in range(2):
                        if s == MT_AT[h2] and active(j, u, 1):
                            b = n - 1
                            act.wait_ge(mt_p, 2 * b + h2 + 1)
                            if later(j, b, 1):
                                act.wait_ge(mt_out, (2 * b + h2 - 1) * 16)
                            act.copy(mt[h2][:, :], mt_ps).then_inc(mt_d, 1)
                            act.wait_ge(mt_d, 2 * b + h2 + 1)
                            if h2 or later(j, b, 1):
                                act.wait_ge(mt_out, (2 * b + h2) * 16)
                            act.dma_start(m_dram[1 - i, h2], mt[h2][:, :]).then_inc(mt_out, 16)
                    if s == 5 and active(j, u, 3):
                        b = n - 3
                        act.wait_ge(z4_p, b + 1)
                        act.copy(z4t[:, :], ps_b[:, 0:T]).then_inc(z4t_d, 1)
                if isinstance(j, int) and n == 0:
                    masks()

            pipeline(act, body, ahead=1)

        @block.tensor
        def _(pe):
            pe.wait_ge(loaded, N_LOAD * 16)

            def body(j, u):
                n, i = 2 * j + u, u
                o = 1 - i
                for s in range(ST):
                    lag, g = turn(s)
                    if active(j, u, lag):
                        b, st = n - lag, (i + lag) % 2
                        if isinstance(b, int) and b < 2 and g == 0:
                            pe.wait_ge(ones_d, b + 1)
                        if g % (ST // 2) == 0:
                            pe.wait_ge(m_in[g // (ST // 2)], (b + 1) * 16)
                        if g >= 1 or later(j, b, 1):
                            pe.wait_ge(exped, b * ST + g)
                        pe.matmul(t_ps, ident16[:, :], causal_t[:, :], start=True, stop=True)
                        for c in range(NS):
                            cs = slice(c * SEG, (c + 1) * SEG)
                            for hh in range(2):
                                mm = pe.matmul(t_ps[hh * SEG:(hh + 1) * SEG, cs],
                                               k_st[st][0:KROWS, 2 * g + hh, cs], q_st[st][0:KROWS, 2 * g + hh, cs],
                                               start=False, stop=True, skip_group_check=True)
                        mm.then_inc(shifted, 1)
                    if s in S_AT and active(j, u, 1):
                        b = n - 1
                        q = S_AT.index(s)
                        if isinstance(b, int) and b == 0 and q == 0:
                            pe.wait_ge(mask_d, 3)
                        if q % 2 == 0:
                            pe.wait_ge(stack_in[q // 2], (b + 1) * 4 * 16)
                        for t in range(NT):
                            w = 2 * q + t
                            ts = slice(t * P, (t + 1) * P)
                            if w >= 2 or later(j, b, 1):
                                pe.wait_ge(maxed, b * ST + w - 1)
                            pe.matmul(s_ps[t][:, :], ident16[:, :], causal[:, :], start=True, stop=True)
                            for c in range(4):
                                h = 4 * q + c
                                mm = pe.matmul(s_ps[t][:, c * P:(c + 1) * P], q_st[o][0:MROW, h, ts],
                                               k_st[o][0:MROW, h, ts], start=False, stop=True,
                                               skip_group_check=True)
                            mm.then_inc(score, 1)
                    if s == 0 and active(j, u, 1):
                        b = n - 1
                        pe.wait_ge(sg_d, b + 1)
                        if later(j, b, 1):
                            pe.wait_ge(read_d, b * 9)
                        apart(pe, spare)
                        for c in range(NS - 1):
                            mm = pe.transpose(ps_c[0:SEG, c * P:(c + 1) * P], sg[o][:, c, 0, :], ident[:, :])
                        mm.then_inc(sk_p, 1)
                    if s == 0 and active(j, u, 0):
                        pe.wait_ge(z_d, (n + 1) * NT)
                        free(pe, USES_B, 0, j, u)
                        for t in range(NT):
                            mm = pe.transpose(ps_b[:, t * P:(t + 1) * P], z[i][:, t, :], ident[:, :])
                        mm.then_inc(zt_p, 1)
                    lag, g = before(lag, g)
                    if active(j, u, lag):
                        b, st = n - lag, (i + lag) % 2
                        pe.wait_ge(exped, b * ST + g + 1)
                        if g == 0:
                            pe.wait_ge(v_d, (b + 1) * VD)
                            if later(j, b, 1):
                                pe.wait_ge(ad_d, b * AD)
                        for t in range(NT):
                            at = g * VP
                            mm = pe.matmul(o_ps[:, t, at:at + WIN], prob[g % 4][:, t * P:(t + 1) * P],
                                           vb[st][:, t, at:at + WIN], start=True, stop=True)
                        mm.then_inc(pv, 1)
                    if s == 0 and active(j, u, 3):
                        b = n - 3
                        pe.wait_ge(ad_d, (b + 1) * AD)
                        pe.wait_ge(read_d, (b + 1) * 9)
                        free(pe, USES_A, 0, j, u)
                        for t in range(NT):
                            pe.transpose(ps_a[:, t * P:(t + 1) * P], ad[:, t, :], ident[:, :])
                        for c in range(NS - 1):
                            at = T + (c + 1) * SEG
                            mm = pe.transpose(ps_a[:, at:at + SEG], am[o][SEG:P, c, :], ident[SEG:P, SEG:P])
                        mm.then_inc(at_p, 1)
                    if s == 5 and active(j, u, 3):
                        b = n - 3
                        pe.wait_ge(z4_d, (b + 1) * NT)
                        free(pe, USES_B, 3, j, u)
                        for t in range(NT):
                            mm = pe.transpose(ps_b[:, t * P:(t + 1) * P], z4[:, t, :], ident[:, :])
                        mm.then_inc(z4_p, 1)
                    if s in (1, 3, 5) and active(j, u, 1):
                        b, c = n - 1, s // 2
                        if c == 0:
                            pe.wait_ge(sk_d, b + 1)
                            pe.wait_ge(vs_d, b + 1)
                        else:
                            pe.wait_ge(u_d, b * 2 + c)
                        pe.matmul(ps_c[:, 0:MW], skn[:, c, :], uv[o][:, c, :], start=True, stop=True
                                  ).then_inc(mem_p, 1)
                    if s in (2, 4, 6) and active(j, u, 1):
                        b, c = n - 1, s // 2 - 1
                        pe.wait_ge(mz_d, b * 5 + 2 * c + 1)
                        pe.matmul(ps_c[:, 0:MW], sg[o][:, c + 1, :, :].rearrange("p a t -> p (a t)"), mz[:, :],
                                  start=True, stop=True).then_inc(read_p, 1)
                    if s == 2 and active(j, u, 3):
                        b = n - 3
                        pe.wait_ge(at_d, 2 * (b + 1))
                        free(pe, USES_B, 1, j, u)
                        for t in range(NT):
                            mm = pe.matmul(ps_b[:, t * P:(t + 1) * P], at_b[:, t * P:(t + 1) * P], w_o[:, :],
                                           start=True, stop=True)
                        mm.then_inc(wo_p, 1)
                    if s == 1 and active(j, u, 0):
                        pe.wait_ge(zt_d, n + 1)
                        free(pe, USES_A, 1, j, u)
                        if later(j, n, 1):
                            pe.wait_ge(pn_d, n * 2)
                        pe.matmul(ps_a[:, 0:T], w_kq[:, 0, :], zt[i][:, :, 0, :], start=True, stop=True)
                        pe.matmul(ps_a[:, T:2 * T], w_kq[:, 1, :], zt[i][:, :, 0, :], start=True, stop=True
                                  ).then_inc(kq_p, 1)
                    if s == 3 and active(j, u, 0):
                        free(pe, USES_B, 2, j, u)
                        for c in range(NS):
                            mm = pe.matmul(ps_b[:, c * P:(c + 1) * P],
                                           zt[i][:, c, :, :].rearrange("p a t -> p (a t)"), w_v[:, :],
                                           start=True, stop=True)
                        mm.then_inc(vs_p, 1)
                    for h2 in range(2):
                        if s == MT_AT[h2] and active(j, u, 1):
                            b = n - 1
                            pe.wait_ge(mp_d, b * MP + 4 * (h2 + 1))
                            if h2:
                                pe.wait_ge(mt_d, 2 * b + 1)
                            else:
                                free(pe, USES_A, 2, j, u)
                                pe.wait_ge(pn_d, 2 * min(n + 1, NB) if isinstance(j, int) else 2 * (n + 1))
                            for t in range(NT):
                                mm = pe.transpose(mt_ps[:, t * P:(t + 1) * P],
                                                  mpart[:, t, h2, :, :].rearrange("p a h -> p (a h)"), ident16[:, :])
                            mm.then_inc(mt_p, 1)
                    if s == 6 and active(j, u, 3):
                        b = n - 3
                        pe.wait_ge(wc_in, (b + 1) * 16)
                        pe.wait_ge(z4t_d, b + 1)
                        free(pe, USES_B, 4, j, u)
                        for t in range(NT):
                            mm = pe.matmul(ps_b[:, t * P:(t + 1) * P], z4t[:, t * P:(t + 1) * P], wc[o][:, 0, :],
                                           start=True, stop=True)
                        mm.then_inc(g_p, 1)

            pipeline(pe, body, ahead=1)

        @block.vector
        def _(dve):
            def stack_zeros(i):
                dve.memset(k_st[i][64:MROW, :, :], 0.0).then_inc(zeros_d, 1)
                dve.memset(q_st[i][64:MROW, :, :], 0.0).then_inc(zeros_d, 1)

            def mixing():
                dve.wait_ge(loaded_late, N_LATE * 16)

                def link0(k, ins):
                    ins.then_inc(beta_d, 1)
                    dve.wait_ge(beta_d, k)

                dve.wait_ge(beta_d, 1)
                link0(2, dve.tensor_scalar(beta[:, 1:2], bexp[:, :], 1.0, None, ALU.add))
                link0(3, dve.reciprocal(beta[:, 2:3], beta[:, 1:2]))
                link0(4, dve.tensor_tensor(beta[:, 3:4], bexp[:, :], beta[:, 2:3], ALU.mult))

            def moments(k, b, src):
                for t in range(NT):
                    dve.bn_stats(stats[k][:, t, :], src[:, t, :]).then_inc(stat_d[k], 1)
                for t in range(NT):
                    dve.wait_ge(stat_d[k], b * NT + t + 1)
                    apart(dve, spare)
                    dve.bn_aggr(mv[k][:, t, :], stats[k][:, t, :]).then_inc(mv_d[k], 1)

            def normed(k, b, src, dst, done):
                dve.wait_ge(norm_d[k], 2 * (b + 1))
                for t in range(NT):
                    dve.tensor_scalar(dst[:, t, :], src[:, t, :], mv[k][:, t, 0:1], rs[k][:, t:t + 1],
                                      ALU.subtract, ALU.mult).then_inc(done, 1)

            def body(j, u):
                n, i = 2 * j + u, u
                o = 1 - i

                def split_max(h2, k):
                    b = n - 1
                    hs = slice(h2 * H // 2, (h2 + 1) * H // 2)
                    high, mid, low = (mpart[:, :, h2, c, :] for c in range(NPART))
                    if k:
                        dve.wait_ge(mp_d, b * MP + 4 * h2 + k)
                    else:
                        dve.wait_ge(maxed, b * ST + 4 * (h2 + 1))
                        if later(j, b, 1):
                            dve.wait_ge(mt_p, 2 * (b - 1) + h2 + 1)
                    step = (lambda: dve.tensor_copy(high, nmax[:, :, hs]),
                            lambda: dve.tensor_tensor(nrest[:, :, hs], nmax[:, :, hs], high, ALU.subtract),
                            lambda: dve.tensor_copy(mid, nrest[:, :, hs]),
                            lambda: dve.tensor_tensor(low, nrest[:, :, hs], mid, ALU.subtract))[k]
                    step().then_inc(mp_d, 1)

                def reduce_unit(q, t):
                    b = n - 1
                    w = 2 * q + t
                    dve.wait_ge(score, b * ST + w + 1)
                    if w == 0 and later(j, b, 1):
                        dve.wait_ge(mp_d, b * MP)
                    dve.tensor_reduce(nmax[:, t, 4 * q:4 * q + 4],
                                      s_ps[t][:, :].rearrange("p (h k) -> p h k", h=4), AX.X, ALU.max,
                                      negate=True).then_inc(maxed, 1)

                def remember(c, k):
                    b = n - 1
                    if k == 0:
                        dve.wait_ge(mem_p, b * 3 + c + 1)
                        if c == 0 and later(j, b, 1):
                            dve.wait_ge(read_p, b * 3)
                        dve.tensor_tensor((mzt if c else mz)[:, :], ps_c[:, 0:MW], diag[:, :], ALU.mult
                                          ).then_inc(mz_d, 1)
                    elif c:
                        dve.wait_ge(mz_d, b * 5 + 2 * c)
                        dve.wait_ge(read_p, b * 3 + c)
                        dve.tensor_tensor(mz[:, :], mz[:, :], mzt[:, :], ALU.add).then_inc(mz_d, 1)

                def read(c, k):
                    b = n - 1
                    if k:
                        dve.wait_ge(read_d, b * 9 + 3 * c + k)
                    else:
                        dve.wait_ge(read_p, b * 3 + c + 1)
                        if c == 0 and later(j, b, 2):
                            dve.wait_ge(at_p, b - 1)
                    by_head = lambda a: a.rearrange("p (h e) -> p h e", h=H)
                    if k == 0:
                        dve.tensor_scalar(dn[:, c, :], ps_c[:, HV:MW], 1e-6, None, ALU.add).then_inc(read_d, 1)
                    elif k == 1:
                        dve.reciprocal(dr[:, c, :], dn[:, c, :]).then_inc(read_d, 1)
                    elif k == 2:
                        dve.tensor_tensor(by_head(am[o][:, c, :]), by_head(ps_c[:, 0:HV]),
                                          dr[:, c, :].unsqueeze(2).broadcast_to([P, H, HD]), ALU.mult
                                          ).then_inc(read_d, 1)
                    elif c < 2:
                        dve.tensor_tensor(uv[o][0:SEG, c + 1, 0:HV], uv[o][0:SEG, c + 1, 0:HV],
                                          am[o][0:SEG, c, :], ALU.subtract).then_inc(u_d, 1)

                if isinstance(j, int) and n == 0:
                    stack_zeros(0)
                for s in range(ST):
                    if s == 4 and active(j, u, 3):
                        b = n - 3
                        if later(j, b, 1):
                            dve.wait_ge(z4_p, b)
                        normed(1, b, x3[o], z4, z4_d)
                    if s == 3 and active(j, u, 1):
                        for k in range(MP // 2):
                            split_max(0, k)
                    if s in S_AT and active(j, u, 1):
                        for t in range(NT):
                            reduce_unit(S_AT.index(s), t)
                    if s == 0 and active(j, u, -1):
                        dve.wait_ge(x_in, (n + 2) * 16)
                        if later(j, n, 0):
                            dve.wait_ge(norm_d[0], 2 * (n + 1))
                        moments(0, n + 1, x[o])
                    if s == 0 and active(j, u, 3):
                        b = n - 3
                        dve.wait_ge(at_d, 2 * b + 1)
                        dve.scalar_tensor_tensor(at_b[:, SEG:T], ps_a[:, T + SEG:2 * T], beta[:, 2:3],
                                                 at_b[:, SEG:T], ALU.mult, ALU.add).then_inc(at_d, 1)
                    if s in (1, 3, 5) and active(j, u, 1):
                        for k in range(2):
                            remember(s // 2, k)
                    if s == 4 and active(j, u, 1):
                        for k in range(4):
                            read(1, k)
                    if s == 6 and active(j, u, 1):
                        for k in range(4):
                            split_max(1, k)
                            read(2, k)
                    if s == 2 and active(j, u, 1):
                        for k in range(4):
                            read(0, k)
                    if s == 2 and active(j, u, 3):
                        b = n - 3
                        dve.wait_ge(wo_p, b + 1)
                        dve.wait_ge(xt_in, (b + 1) * 16)
                        if later(j, b, 2):
                            dve.wait_ge(xb_d, b - 1)
                        dve.tensor_tensor(flat(x3[o]), ps_b[:, 0:T], flat(xt[o]), ALU.add).then_inc(x3_d, 1)
                        dve.wait_ge(x3_d, b + 1)
                        if later(j, b, 1):
                            dve.wait_ge(norm_d[1], 2 * b)
                        moments(1, b, x3[o])
                    if s == 1 and active(j, u, 0):
                        dve.wait_ge(kq_d, (n + 1) * 2)
                        if later(j, n, 1):
                            dve.wait_ge(sg_d, n)
                        dve.tensor_scalar(flat(pos), ps_a[:, :], 0.0, None, ALU.max).then_inc(pn_d, 1)
                        dve.tensor_scalar(flat(neg), ps_a[:, :], 0.0, None, ALU.min).then_inc(pn_d, 1)
                    if s == 6 and active(j, u, 3):
                        b = n - 3
                        dve.wait_ge(g_p, b + 1)
                        dve.wait_ge(xb_d, b + 1)
                        if later(j, b, 2):
                            dve.wait_ge(x4_out, (b - 1) * 16)
                        dve.tensor_tensor(flat(x4[o]), ps_b[:, 0:T], flat(xb[o]), ALU.add).then_inc(x4_d, 1)
                    if s == 7 and active(j, u, -1):
                        if later(j, n, 1):
                            dve.wait_ge(zt_p, n)
                        normed(0, n + 1, x[o], z[o], z_d)
                    if s == 7 and active(j, u, 2):
                        b = n - 2
                        dve.wait_ge(pv, (b + 1) * ST)
                        if later(j, b, 1):
                            dve.wait_ge(at_p, b)
                        out = [o_ps[h2 * SEG:(h2 + 1) * SEG, :, 0:VP * H // 2].rearrange(
                            "q t (g s a e) -> q t g s a e", s=2, a=2, e=HD + 1)[:, :, :, h2] for h2 in range(2)]
                        by_pair = lambda a, h2: a[h2 * SEG:(h2 + 1) * SEG, :, :].rearrange(
                            "q t (g a) -> q t g a", a=2)
                        for h2 in range(2):
                            dve.reciprocal(by_pair(dinv, h2), out[h2][:, :, :, :, HD]).then_inc(ad_d, 1)
                        dve.wait_ge(ad_d, AD * b + 2)
                        for h2 in range(2):
                            for t in range(NT):
                                dve.tensor_tensor(
                                    ad[h2 * SEG:(h2 + 1) * SEG, t, :].rearrange("q (g a e) -> q g a e", a=2, e=HD),
                                    out[h2][:, t, :, :, 0:HD],
                                    by_pair(dinv, h2)[:, t].unsqueeze(3).broadcast_to([SEG, H // 2, 2, HD]),
                                    ALU.mult).then_inc(ad_d, 1)

                if isinstance(j, int) and n == 0:
                    stack_zeros(1)
                    mixing()

            pipeline(dve, body, ahead=1)


def program(nc, d):
    attention_a(nc, d)
    dense(nc, d)
    attention_b(nc, d)


def laid_out(I):
    import numpy as np

    a = lambda k: np.asarray(I[f"L0_attn_a_{k}"])
    b = lambda k: np.asarray(I[f"L0_attn_b_{k}"])
    f = lambda k: np.asarray(I[f"L0_ffn_{k}"])
    on_rows = lambda v: np.broadcast_to(v, (P, v.shape[0]))
    dh = np.arange(P).reshape(H, HD).T.ravel()
    ws = a("Ws")[0]
    sel_qv = np.zeros((H, QK, H), np.float32)
    sel_v = np.zeros((R, HD, R), np.float32)
    for h in range(H):
        sel_qv[h, :, h] = ws[:QK]
    for r in range(R):
        sel_v[r, :, r] = ws[QK:]
    t = np.arange(P)
    seen = (t[:, None] // 64 == t[None] // 64) & (t[None] <= t[:, None])
    causal = np.where(seen, 0.0, -2.0 ** 100).astype(np.float32)
    diag = np.concatenate([(t % H)[:, None] == (t // HD)[None], (t % H)[:, None] == np.arange(H)[None]], 1)
    out = {
        "x": a("x"),
        "a_Wq": a("Wq")[dh].T, "a_Wk": a("Wk")[dh].T, "a_Wv_t": a("Wv").T, "a_Wv": a("Wv"), "a_Wqv": a("Wqv"),
        "a_bv_b": on_rows(a("bv")), "a_bv_r": np.broadcast_to(a("bv")[:, None], (RD, P)),
        "a_bqv_b": np.broadcast_to(a("bqv")[:, None], (QK * H, P)),
        "a_sel_qv": sel_qv.reshape(QK * H, H), "a_sel_v": sel_v.reshape(RD, R),
        "a_cols": np.stack([a("bq")[dh], a("bk")[dh], a("g1"), a("b1"), np.broadcast_to(a("bs"), P)], 1),
        "a_Wf_t": a("Wf").T, "a_Wr1_t": a("Wr1").T, "a_Wr2_t": a("Wr2").T,
        "a_bf_b": on_rows(a("bf")), "a_br2_b": on_rows(a("br2")),
        "b_cols": np.stack([a("br1")[:P], a("br1")[P:], a("g2"), a("b2")], 1),
        "W1": f("W1"), "W2_t": f("W2").transpose(0, 2, 1),
        "ffn_b1": f("b1").reshape(NG, NI, P).transpose(2, 0, 1), "ffn_b2": f("b2")[None],
        "b_Wkq_t": np.concatenate([b("W_k")[dh].T, b("W_q")[dh].T], 1),
        "b_Wv_t": b("W_v").T, "b_Wo_t": b("W_o").T, "b_beta": np.repeat(b("beta_param"), HD)[:, None],
        "ident": np.eye(P, dtype=np.float32),
        "causal": np.concatenate([causal, np.tile(causal.T[:64, :64], (2, 1))], 1),
        "diag": diag.astype(np.float32),
    }
    return {k: np.ascontiguousarray(v) for k, v in out.items()}


SCRATCH = {
    "a_parts_dram": ((2, 2 * NPART, P, T), BF16), "a_m_dram": ((2, 2, NPART * H // 2, T), BF16),
    "c_parts_dram": ((2, 2 * NPART, P, T), BF16), "c_m_dram": ((2, 2, NPART * H // 2, T), BF16),
    "y": ((NB, T, P), F32), "ao": ((NB, T, P), F32), "x2": ((NB, T, P), F32),
    "folded": ((NB // 2, P, 2 * P), F32),
}


def kernel(**inputs):
    import numpy as np
    import concourse.bacc as bacc
    from concourse.bass_utils import run_bass_kernel_spmd

    nc = bacc.Bacc("TRN2", target_bir_lowering=False, num_devices=1)
    arrays, d = {}, {}
    for name, a in laid_out(inputs).items():
        arrays[f"in_{name}"] = a
        d[name] = nc.dram_tensor(f"in_{name}", a.shape, mybir.dt.from_np(a.dtype), kind="ExternalInput").ap()
    for name, (shape, dt) in SCRATCH.items():
        d[name] = nc.dram_tensor(f"scratch_{name}", shape, dt, kind="Internal").ap()
    d["out"] = nc.dram_tensor("out", (NB, T, P), F32, kind="ExternalOutput").ap()
    program(nc, d)
    return run_bass_kernel_spmd(nc, [arrays], core_ids=[0]).results[0]["out"]
```
